# Optimizing a Trainium2 kernel written in Bass

```python
import numpy as np
import jax
import jax.numpy as jnp

def _softmax(x, axis=-1):
    return jax.nn.softmax(x, axis=axis)

def _gelu(x):
    return jax.nn.gelu(x, approximate=True)

def _silu(x):
    return jax.nn.silu(x)

def _sigmoid(x):
    return jax.nn.sigmoid(x)

def _layernorm(x, axis=-1, eps=1e-05):
    m = jnp.mean(x, axis=axis, keepdims=True)
    v = jnp.var(x, axis=axis, keepdims=True)
    return (x - m) / jnp.sqrt(v + eps)

def _scatter_add(tgt, idx, src, axis=0):
    return tgt.at[idx].add(src)

def _segment_sum(src, seg, n):
    return jax.ops.segment_sum(src, seg, n)
kernel_name = 'mk_seq_preln_d4_jaxref_r8_f11fb4'

def setup_inputs(seed: int=0):
    np.random.seed(seed)
    _w = jnp.asarray

    def _L0_attn_setup():
        import jax, jax.numpy as jnp
        import numpy as np
        from jax import lax
        D_MODEL = 128
        D_STATE = 16
        D_CONV = 4
        EXPAND = 2
        D_INNER = EXPAND * D_MODEL
        B = 4
        L = 256

        def _silu(v):
            return v * jax.nn.sigmoid(v)

        def _mamba(x, W_in, conv_w, conv_b, W_xproj, W_dt, b_dt, A_log, Dp, W_out):
            xz = x @ W_in
            xc, z = jnp.split(xz, 2, axis=-1)
            xt = jnp.swapaxes(xc, 1, 2)
            conv = lax.conv_general_dilated(xt, conv_w, window_strides=(1,), padding=[(D_CONV - 1, 0)], feature_group_count=D_INNER)
            conv = conv + conv_b[None, :, None]
            xc = _silu(jnp.swapaxes(conv, 1, 2))
            x_dbl = xc @ W_xproj
            delta = jax.nn.softplus(x_dbl[..., :1] @ W_dt + b_dt)
            Bp = x_dbl[..., 1:1 + D_STATE]
            Cp = x_dbl[..., 1 + D_STATE:]
            A = -jnp.exp(A_log)

            def step(h, inp):
                d_t, B_t, C_t, x_t = inp
                dA = jnp.exp(d_t[..., None] * A)
                h = dA * h + d_t[..., None] * B_t[:, None, :] * x_t[..., None]
                y = jnp.einsum('bds,bs->bd', h, C_t)
                return (h, y)
            tm = lambda a: jnp.swapaxes(a, 0, 1)
            h0 = jnp.zeros((x.shape[0], D_INNER, D_STATE), x.dtype)
            _, ys = lax.scan(step, h0, (tm(delta), tm(Bp), tm(Cp), tm(xc)))
            y = jnp.swapaxes(ys, 0, 1) + xc * Dp
            y = y * _silu(z)
            return y @ W_out
        key = jax.random.key(seed)
        ks = jax.random.split(key, 8)
        s = lambda fan_in: 1.0 / np.sqrt(fan_in)
        x = jax.random.normal(ks[0], (B, L, D_MODEL), jnp.float32)
        W_in = jax.random.normal(ks[1], (D_MODEL, 2 * D_INNER), jnp.float32) * s(D_MODEL)
        conv_w = jax.random.normal(ks[2], (D_INNER, 1, D_CONV), jnp.float32) * s(D_CONV)
        conv_b = jax.random.normal(ks[3], (D_INNER,), jnp.float32) * 0.01
        W_xproj = jax.random.normal(ks[4], (D_INNER, 2 * D_STATE + 1), jnp.float32) * s(D_INNER)
        W_dt = jax.random.normal(ks[5], (1, D_INNER), jnp.float32)
        b_dt = jax.random.normal(ks[6], (D_INNER,), jnp.float32) * 0.01
        A_log = jnp.log(jnp.broadcast_to(jnp.arange(1, D_STATE + 1, dtype=jnp.float32), (D_INNER, D_STATE)))
        Dp = jnp.ones((D_INNER,), jnp.float32)
        W_out = jax.random.normal(ks[7], (D_INNER, D_MODEL), jnp.float32) * s(D_INNER)
        return dict(x=x, W_in=W_in, conv_w=conv_w, conv_b=conv_b, W_xproj=W_xproj, W_dt=W_dt, b_dt=b_dt, A_log=A_log, Dp=Dp, W_out=W_out)
    _L0_attn_in = _L0_attn_setup()

    def _L0_ffn_setup():
        import jax, jax.numpy as jnp
        import numpy as np
        B, S, D = (4, 256, 128)
        DFF = 64
        E = 16
        TOP_K = 2
        N_SHARED = 2
        FUSED_DFF = DFF * N_SHARED
        key = jax.random.key(seed)
        ks = jax.random.split(key, 16)
        sc_d = 1.0 / np.sqrt(D)
        sc_f = 1.0 / np.sqrt(DFF)
        sc_sf = 1.0 / np.sqrt(FUSED_DFF)
        inp = {'x': jax.random.normal(ks[0], (B, S, D), dtype=jnp.float32), 'gate_w': jax.random.uniform(ks[1], (E, D), dtype=jnp.float32, minval=-sc_d, maxval=sc_d), 'expert_bias': jnp.zeros((E,), dtype=jnp.float32), 'w1': jax.random.uniform(ks[2], (E, DFF, D), dtype=jnp.float32, minval=-sc_d, maxval=sc_d), 'b1': jax.random.uniform(ks[3], (E, DFF), dtype=jnp.float32, minval=-sc_d, maxval=sc_d), 'w3': jax.random.uniform(ks[4], (E, DFF, D), dtype=jnp.float32, minval=-sc_d, maxval=sc_d), 'b3': jax.random.uniform(ks[5], (E, DFF), dtype=jnp.float32, minval=-sc_d, maxval=sc_d), 'w2': jax.random.uniform(ks[6], (E, D, DFF), dtype=jnp.float32, minval=-sc_f, maxval=sc_f), 'b2': jax.random.uniform(ks[7], (E, D), dtype=jnp.float32, minval=-sc_f, maxval=sc_f), 'sw1': jax.random.uniform(ks[8], (FUSED_DFF, D), dtype=jnp.float32, minval=-sc_d, maxval=sc_d), 'sb1': jax.random.uniform(ks[9], (FUSED_DFF,), dtype=jnp.float32, minval=-sc_d, maxval=sc_d), 'sw3': jax.random.uniform(ks[10], (FUSED_DFF, D), dtype=jnp.float32, minval=-sc_d, maxval=sc_d), 'sb3': jax.random.uniform(ks[11], (FUSED_DFF,), dtype=jnp.float32, minval=-sc_d, maxval=sc_d), 'sw2': jax.random.uniform(ks[12], (D, FUSED_DFF), dtype=jnp.float32, minval=-sc_sf, maxval=sc_sf), 'sb2': jax.random.uniform(ks[13], (D,), dtype=jnp.float32, minval=-sc_sf, maxval=sc_sf)}
        return inp
    _L0_ffn_in = _L0_ffn_setup()

    def _L1_attn_setup():
        import jax, jax.numpy as jnp
        import numpy as np
        TWO_PI = 6.283185307179586
        key = jax.random.key(seed)
        k1, k2, k3, k4, k5, k6 = jax.random.split(key, 6)
        B, T, D = (2, 1024, 128)
        x = jax.random.normal(k1, (B, T, D), dtype=jnp.float32)
        s = 1.0 / np.sqrt(D)
        Wk = jax.random.uniform(k2, (D, D), jnp.float32, -s, s)
        Wv = jax.random.uniform(k3, (D, D), jnp.float32, -s, s)
        Wo = jax.random.uniform(k4, (D, D), jnp.float32, -s, s)
        freqs = jax.random.uniform(k5, (D,), jnp.float32, 0.0, TWO_PI)
        return {'x': x, 'Wk': Wk, 'Wv': Wv, 'Wo': Wo, 'freqs': freqs}
    _L1_attn_in = _L1_attn_setup()

    def _L1_ffn_setup():
        import jax, jax.numpy as jnp
        import numpy as np
        DIM = 128
        DEPTH = 6
        HEADS = 16
        DIM_HEAD = 64
        WINDOW = 32
        INNER = HEADS * DIM_HEAD
        DIM_INNER = int(DIM * 4 * 2 / 3)
        QK_SCALE = 8.0

        def shift_tokens(t):
            a, s = jnp.split(t, 2, -1)
            s = jnp.pad(s, ((0, 0), (1, 0), (0, 0)))[:, :-1]
            return jnp.concatenate([a, s], -1)

        def l2norm(t):
            return t / jnp.maximum(jnp.linalg.norm(t, axis=-1, keepdims=True), 1e-12)

        def rotate_half(x):
            x1, x2 = jnp.split(x, 2, -1)
            return jnp.concatenate([-x2, x1], -1)

        def rotary_tables(n):
            half = jnp.arange(0, DIM_HEAD, 2, dtype=jnp.float32)
            inv_freq = 1.0 / 10000.0 ** (half / DIM_HEAD)
            t = jnp.arange(n, dtype=jnp.float32)
            freqs = t[:, None] * inv_freq[None, :]
            freqs = jnp.concatenate([freqs, freqs], -1)
            base_scale = (half + 0.4 * DIM_HEAD) / (1.4 * DIM_HEAD)
            power = (t - n // 2) / (WINDOW // 2)
            scale = base_scale[None, :] ** power[:, None]
            scale = jnp.concatenate([scale, scale], -1)
            return (freqs, scale)

        def local_attention(q, k, v):
            b, h, n, d = q.shape
            w = WINDOW
            nw = n // w
            bq = q.reshape(b, h, nw, w, d)
            bk = k.reshape(b, h, nw, w, d)
            bv = v.reshape(b, h, nw, w, d)

            def look(t):
                p = jnp.pad(t, ((0, 0), (0, 0), (1, 0), (0, 0), (0, 0)))
                return jnp.concatenate([p[:, :, :nw], p[:, :, 1:]], axis=3)
            bk2, bv2 = (look(bk), look(bv))
            seq = jnp.arange(n).reshape(nw, w)
            seq_p = jnp.pad(seq, ((1, 0), (0, 0)), constant_values=-1)
            jt = jnp.concatenate([seq_p[:nw], seq_p[1:]], axis=1)
            it = seq[:, :, None]
            jb = jt[:, None, :]
            mask = (it < jb) | (it > jb + w) | (jb == -1)
            sim = jnp.einsum('bhwie,bhwje->bhwij', bq, bk2) * QK_SCALE
            sim = jnp.where(mask, -jnp.finfo(sim.dtype).max, sim)
            attn = jax.nn.softmax(sim, -1)
            out = jnp.einsum('bhwij,bhwje->bhwie', attn, bv2)
            return out.reshape(b, h, n, d)

        def attn_layer(x, Wqkv, qs, ksc, Wo):
            b, n, _ = x.shape
            qkv = x @ Wqkv
            q, k, v = jnp.split(qkv, 3, -1)
            sh = lambda t: t.reshape(b, n, HEADS, DIM_HEAD).transpose(0, 2, 1, 3)
            q, k, v = (sh(q), sh(k), sh(v))
            q = l2norm(q) * qs
            k = l2norm(k) * ksc
            freqs, scale = rotary_tables(n)
            cos, sin = (jnp.cos(freqs), jnp.sin(freqs))
            q = q * cos * scale + rotate_half(q) * sin * scale
            inv = 1.0 / scale
            k = k * cos * inv + rotate_half(k) * sin * inv
            out = local_attention(q, k, v)
            out = out.transpose(0, 2, 1, 3).reshape(b, n, INNER)
            return out @ Wo

        def ffn_layer(x, g, bln, W1, b1, W2, b2):
            mu = x.mean(-1, keepdims=True)
            var = ((x - mu) ** 2).mean(-1, keepdims=True)
            xn = (x - mu) / jnp.sqrt(var + 1e-05) * g + bln
            hg = xn @ W1 + b1
            a, gate = jnp.split(hg, 2, -1)
            return a * jax.nn.gelu(gate, approximate=False) @ W2 + b2
        key = jax.random.key(seed)
        ks = jax.random.split(key, 8)
        B, N = (2, 256)
        init = lambda k, shape: jax.random.normal(k, shape, jnp.float32) * 0.02
        return {'x': jax.random.normal(ks[0], (B, N, DIM), jnp.float32), 'Wqkv': init(ks[1], (DEPTH, DIM, 3 * INNER)), 'q_scale': jnp.ones((DEPTH, DIM_HEAD), jnp.float32), 'k_scale': jnp.ones((DEPTH, DIM_HEAD), jnp.float32), 'Wo': init(ks[2], (DEPTH, INNER, DIM)), 'ln_g': jnp.ones((DEPTH, DIM), jnp.float32), 'ln_b': jnp.zeros((DEPTH, DIM), jnp.float32), 'W1': init(ks[3], (DEPTH, DIM, 2 * DIM_INNER)), 'b1': jnp.zeros((DEPTH, 2 * DIM_INNER), jnp.float32), 'W2': init(ks[4], (DEPTH, DIM_INNER, DIM)), 'b2': jnp.zeros((DEPTH, DIM), jnp.float32)}
    _L1_ffn_in = _L1_ffn_setup()

    def _L2_attn_setup():
        import jax, jax.numpy as jnp
        import numpy as np
        from jax import lax
        B, T, HID = (4, 128, 128)
        H, DK, DV = (8, 128, 128)
        KCONV = 4
        EPS = 1e-06
        KEY_DIM = H * DK
        VAL_DIM = H * DV
        CONV_DIM = 2 * KEY_DIM + VAL_DIM
        key = jax.random.key(seed)
        ks = jax.random.split(key, 11)
        s = 0.02
        return {'hidden_states': jax.random.normal(ks[0], (B, T, HID), jnp.float32), 'qkv_w': jax.random.normal(ks[1], (CONV_DIM, HID), jnp.float32) * s, 'z_w': jax.random.normal(ks[2], (VAL_DIM, HID), jnp.float32) * s, 'b_w': jax.random.normal(ks[3], (H, HID), jnp.float32) * s, 'a_w': jax.random.normal(ks[4], (H, HID), jnp.float32) * s, 'conv_w': jax.random.normal(ks[5], (CONV_DIM, 1, KCONV), jnp.float32) * 0.2, 'dt_bias': jnp.ones((H,), jnp.float32), 'A_log': jnp.log(jax.random.uniform(ks[6], (H,), jnp.float32, 0.001, 16.0)), 'norm_w': jnp.ones((DV,), jnp.float32), 'out_w': jax.random.normal(ks[7], (HID, VAL_DIM), jnp.float32) * s}
    _L2_attn_in = _L2_attn_setup()

    def _L2_ffn_setup():
        import jax, jax.numpy as jnp
        import numpy as np
        D_MODEL = 128
        NUM_EXPERTS = 8
        TOP_K = 2
        key = jax.random.key(seed)
        ks = jax.random.split(key, 5)
        scale = 1.0 / np.sqrt(D_MODEL)
        x = jax.random.normal(ks[0], (4, 256, D_MODEL), dtype=jnp.float32)
        We = jax.random.uniform(ks[1], (NUM_EXPERTS, D_MODEL, D_MODEL), jnp.float32, -scale, scale)
        be = jax.random.uniform(ks[2], (NUM_EXPERTS, D_MODEL), jnp.float32, -scale, scale)
        Wg = jax.random.uniform(ks[3], (NUM_EXPERTS, D_MODEL), jnp.float32, -scale, scale)
        bg = jax.random.uniform(ks[4], (NUM_EXPERTS,), jnp.float32, -scale, scale)
        return {'x': x, 'We': We, 'be': be, 'Wg': Wg, 'bg': bg}
    _L2_ffn_in = _L2_ffn_setup()

    def _L3_attn_setup():
        import jax, jax.numpy as jnp
        import numpy as np
        from jax import lax
        D_MODEL, D_STATE, D_CONV, EXPAND = (128, 16, 4, 2)
        D_INNER = D_MODEL * EXPAND
        BATCH, SEQ = (4, 256)

        def _mamba_forward(x, W_in, conv_w, conv_b, W_x, W_dt, b_dt, A_log, D, W_out):
            batch, seq_len, _ = x.shape
            xz = x @ W_in
            x_in, z = jnp.split(xz, 2, axis=-1)
            x_c = lax.conv_general_dilated(x_in.transpose(0, 2, 1), conv_w, window_strides=(1,), padding=[(D_CONV - 1, 0)], feature_group_count=D_INNER, dimension_numbers=('NCH', 'OIH', 'NCH')) + conv_b[None, :, None]
            x_conv = jax.nn.silu(x_c.transpose(0, 2, 1))
            A = -jnp.exp(A_log)
            Bm, Cm = jnp.split(x_conv @ W_x, 2, axis=-1)
            dt = jax.nn.softplus(x_conv @ W_dt + b_dt)

            def step(h, ins):
                u_t, dt_t, B_t, C_t = ins
                dA = jnp.exp(dt_t[:, :, None] * A)
                h = dA * h + (dt_t * u_t)[:, :, None] * B_t[:, None, :]
                y_t = jnp.einsum('bdn,bn->bd', h, C_t)
                return (h, y_t)
            h0 = jnp.zeros((batch, D_INNER, D_STATE), dtype=x.dtype)
            xs = (x_conv.transpose(1, 0, 2), dt.transpose(1, 0, 2), Bm.transpose(1, 0, 2), Cm.transpose(1, 0, 2))
            _, ys = lax.scan(step, h0, xs)
            y = ys.transpose(1, 0, 2)
            y = y + x_conv * D
            y = y * jax.nn.silu(z)
            return y @ W_out
        key = jax.random.key(seed)
        ks = jax.random.split(key, 9)
        s = lambda fan_in: 1.0 / np.sqrt(fan_in)
        return {'x': jax.random.normal(ks[0], (BATCH, SEQ, D_MODEL), dtype=jnp.float32), 'W_in': jax.random.normal(ks[1], (D_MODEL, 2 * D_INNER), dtype=jnp.float32) * s(D_MODEL), 'conv_w': jax.random.normal(ks[2], (D_INNER, 1, D_CONV), dtype=jnp.float32) * s(D_CONV), 'conv_b': jax.random.normal(ks[3], (D_INNER,), dtype=jnp.float32) * 0.01, 'W_x': jax.random.normal(ks[4], (D_INNER, 2 * D_STATE), dtype=jnp.float32) * s(D_INNER), 'W_dt': jax.random.normal(ks[5], (D_INNER, D_INNER), dtype=jnp.float32) * s(D_INNER), 'b_dt': jax.random.normal(ks[6], (D_INNER,), dtype=jnp.float32) * 0.01, 'A_log': jnp.log(jnp.arange(1, D_STATE + 1, dtype=jnp.float32)), 'D': jnp.ones((D_INNER,), dtype=jnp.float32), 'W_out': jax.random.normal(ks[7], (D_INNER, D_MODEL), dtype=jnp.float32) * s(D_INNER)}
    _L3_attn_in = _L3_attn_setup()

    def _L3_ffn_setup():
        import jax, jax.numpy as jnp
        import numpy as np
        H = 128
        I = 512
        E = 8
        TOPK = 2
        key = jax.random.key(seed)
        ks = jax.random.split(key, 6)
        B, S = (4, 256)
        hidden_states = jax.random.normal(ks[0], (B, S, H), dtype=jnp.float32)
        gate_w = jax.random.normal(ks[1], (H, E), dtype=jnp.float32) * (1.0 / np.sqrt(H))
        W1 = jax.random.normal(ks[2], (E, H, I), dtype=jnp.float32) * np.sqrt(2.0 / (H + I))
        W3 = jax.random.normal(ks[3], (E, H, I), dtype=jnp.float32) * np.sqrt(2.0 / (H + I))
        W2 = jax.random.normal(ks[4], (E, I, H), dtype=jnp.float32) * np.sqrt(2.0 / (H + I))
        dom = jax.random.normal(ks[5], (E, H), dtype=jnp.float32) * 0.02
        return {'hidden_states': hidden_states, 'gate_w': gate_w, 'W1': W1, 'W2': W2, 'W3': W3, 'dom': dom}
    _L3_ffn_in = _L3_ffn_setup()
    _d = {'L0_attn_x': _L0_attn_in['x'], 'L0_attn_W_in': _L0_attn_in['W_in'], 'L0_attn_conv_w': _L0_attn_in['conv_w'], 'L0_attn_conv_b': _L0_attn_in['conv_b'], 'L0_attn_W_xproj': _L0_attn_in['W_xproj'], 'L0_attn_W_dt': _L0_attn_in['W_dt'], 'L0_attn_b_dt': _L0_attn_in['b_dt'], 'L0_attn_A_log': _L0_attn_in['A_log'], 'L0_attn_Dp': _L0_attn_in['Dp'], 'L0_attn_W_out': _L0_attn_in['W_out'], 'L0_ffn_gate_w': _L0_ffn_in['gate_w'], 'L0_ffn_expert_bias': _L0_ffn_in['expert_bias'], 'L0_ffn_w1': _L0_ffn_in['w1'], 'L0_ffn_b1': _L0_ffn_in['b1'], 'L0_ffn_w2': _L0_ffn_in['w2'], 'L0_ffn_b2': _L0_ffn_in['b2'], 'L0_ffn_w3': _L0_ffn_in['w3'], 'L0_ffn_b3': _L0_ffn_in['b3'], 'L0_ffn_sw1': _L0_ffn_in['sw1'], 'L0_ffn_sb1': _L0_ffn_in['sb1'], 'L0_ffn_sw2': _L0_ffn_in['sw2'], 'L0_ffn_sb2': _L0_ffn_in['sb2'], 'L0_ffn_sw3': _L0_ffn_in['sw3'], 'L0_ffn_sb3': _L0_ffn_in['sb3'], 'L1_attn_Wk': _L1_attn_in['Wk'], 'L1_attn_Wv': _L1_attn_in['Wv'], 'L1_attn_Wo': _L1_attn_in['Wo'], 'L1_attn_freqs': _L1_attn_in['freqs'], 'L1_ffn_Wqkv': _L1_ffn_in['Wqkv'], 'L1_ffn_q_scale': _L1_ffn_in['q_scale'], 'L1_ffn_k_scale': _L1_ffn_in['k_scale'], 'L1_ffn_Wo': _L1_ffn_in['Wo'], 'L1_ffn_ln_g': _L1_ffn_in['ln_g'], 'L1_ffn_ln_b': _L1_ffn_in['ln_b'], 'L1_ffn_W1': _L1_ffn_in['W1'], 'L1_ffn_b1': _L1_ffn_in['b1'], 'L1_ffn_W2': _L1_ffn_in['W2'], 'L1_ffn_b2': _L1_ffn_in['b2'], 'L2_attn_qkv_w': _L2_attn_in['qkv_w'], 'L2_attn_z_w': _L2_attn_in['z_w'], 'L2_attn_b_w': _L2_attn_in['b_w'], 'L2_attn_a_w': _L2_attn_in['a_w'], 'L2_attn_conv_w': _L2_attn_in['conv_w'], 'L2_attn_dt_bias': _L2_attn_in['dt_bias'], 'L2_attn_A_log': _L2_attn_in['A_log'], 'L2_attn_norm_w': _L2_attn_in['norm_w'], 'L2_attn_out_w': _L2_attn_in['out_w'], 'L2_ffn_We': _L2_ffn_in['We'], 'L2_ffn_be': _L2_ffn_in['be'], 'L2_ffn_Wg': _L2_ffn_in['Wg'], 'L2_ffn_bg': _L2_ffn_in['bg'], 'L3_attn_W_in': _L3_attn_in['W_in'], 'L3_attn_conv_w': _L3_attn_in['conv_w'], 'L3_attn_conv_b': _L3_attn_in['conv_b'], 'L3_attn_W_x': _L3_attn_in['W_x'], 'L3_attn_W_dt': _L3_attn_in['W_dt'], 'L3_attn_b_dt': _L3_attn_in['b_dt'], 'L3_attn_A_log': _L3_attn_in['A_log'], 'L3_attn_D': _L3_attn_in['D'], 'L3_attn_W_out': _L3_attn_in['W_out'], 'L3_ffn_gate_w': _L3_ffn_in['gate_w'], 'L3_ffn_W1': _L3_ffn_in['W1'], 'L3_ffn_W2': _L3_ffn_in['W2'], 'L3_ffn_W3': _L3_ffn_in['W3'], 'L3_ffn_dom': _L3_ffn_in['dom']}
    _x0 = _d['L0_attn_x']
    _d['L0_attn_x'] = jax.random.normal(jax.random.fold_in(jax.random.key(seed), 1), (8, 256, 128), dtype=_x0.dtype)
    del _x0
    return _d

def reference(L0_attn_x, L0_attn_W_in, L0_attn_conv_w, L0_attn_conv_b, L0_attn_W_xproj, L0_attn_W_dt, L0_attn_b_dt, L0_attn_A_log, L0_attn_Dp, L0_attn_W_out, L0_ffn_gate_w, L0_ffn_expert_bias, L0_ffn_w1, L0_ffn_b1, L0_ffn_w2, L0_ffn_b2, L0_ffn_w3, L0_ffn_b3, L0_ffn_sw1, L0_ffn_sb1, L0_ffn_sw2, L0_ffn_sb2, L0_ffn_sw3, L0_ffn_sb3, L1_attn_Wk, L1_attn_Wv, L1_attn_Wo, L1_attn_freqs, L1_ffn_Wqkv, L1_ffn_q_scale, L1_ffn_k_scale, L1_ffn_Wo, L1_ffn_ln_g, L1_ffn_ln_b, L1_ffn_W1, L1_ffn_b1, L1_ffn_W2, L1_ffn_b2, L2_attn_qkv_w, L2_attn_z_w, L2_attn_b_w, L2_attn_a_w, L2_attn_conv_w, L2_attn_dt_bias, L2_attn_A_log, L2_attn_norm_w, L2_attn_out_w, L2_ffn_We, L2_ffn_be, L2_ffn_Wg, L2_ffn_bg, L3_attn_W_in, L3_attn_conv_w, L3_attn_conv_b, L3_attn_W_x, L3_attn_W_dt, L3_attn_b_dt, L3_attn_A_log, L3_attn_D, L3_attn_W_out, L3_ffn_gate_w, L3_ffn_W1, L3_ffn_W2, L3_ffn_W3, L3_ffn_dom):

    def _L0_attn_ref(x, W_in, conv_w, conv_b, W_xproj, W_dt, b_dt, A_log, Dp, W_out):
        import jax, jax.numpy as jnp
        import numpy as np
        from jax import lax
        D_MODEL = 128
        D_STATE = 16
        D_CONV = 4
        EXPAND = 2
        D_INNER = EXPAND * D_MODEL
        B = 4
        L = 256

        def _silu(v):
            return v * jax.nn.sigmoid(v)

        def _mamba(x, W_in, conv_w, conv_b, W_xproj, W_dt, b_dt, A_log, Dp, W_out):
            xz = x @ W_in
            xc, z = jnp.split(xz, 2, axis=-1)
            xt = jnp.swapaxes(xc, 1, 2)
            conv = lax.conv_general_dilated(xt, conv_w, window_strides=(1,), padding=[(D_CONV - 1, 0)], feature_group_count=D_INNER)
            conv = conv + conv_b[None, :, None]
            xc = _silu(jnp.swapaxes(conv, 1, 2))
            x_dbl = xc @ W_xproj
            delta = jax.nn.softplus(x_dbl[..., :1] @ W_dt + b_dt)
            Bp = x_dbl[..., 1:1 + D_STATE]
            Cp = x_dbl[..., 1 + D_STATE:]
            A = -jnp.exp(A_log)

            def step(h, inp):
                d_t, B_t, C_t, x_t = inp
                dA = jnp.exp(d_t[..., None] * A)
                h = dA * h + d_t[..., None] * B_t[:, None, :] * x_t[..., None]
                y = jnp.einsum('bds,bs->bd', h, C_t)
                return (h, y)
            tm = lambda a: jnp.swapaxes(a, 0, 1)
            h0 = jnp.zeros((x.shape[0], D_INNER, D_STATE), x.dtype)
            _, ys = lax.scan(step, h0, (tm(delta), tm(Bp), tm(Cp), tm(xc)))
            y = jnp.swapaxes(ys, 0, 1) + xc * Dp
            y = y * _silu(z)
            return y @ W_out
        return _mamba(x, W_in, conv_w, conv_b, W_xproj, W_dt, b_dt, A_log, Dp, W_out)

    def _L0_ffn_ref(x, gate_w, expert_bias, w1, b1, w2, b2, w3, b3, sw1, sb1, sw2, sb2, sw3, sb3):
        import jax, jax.numpy as jnp
        import numpy as np
        B, S, D = (4, 256, 128)
        DFF = 64
        E = 16
        TOP_K = 2
        N_SHARED = 2
        FUSED_DFF = DFF * N_SHARED
        Bv, Sv, Dv = x.shape
        xf = x.reshape(-1, Dv)
        logits = xf @ gate_w.T
        scores = jax.nn.sigmoid(logits)
        biased = logits + expert_bias.astype(logits.dtype)[None, :]
        _, topk_idx = jax.lax.top_k(biased, TOP_K)
        topk_w = jnp.take_along_axis(scores, topk_idx, axis=-1)
        topk_w = topk_w / (topk_w.sum(-1, keepdims=True) + 1e-10)
        gatew = (jax.nn.one_hot(topk_idx, E, dtype=xf.dtype) * topk_w[..., None]).sum(1)
        y = jnp.zeros_like(xf)
        for e in range(E):
            h = jax.nn.silu(xf @ w1[e].T + b1[e]) * (xf @ w3[e].T + b3[e])
            y = y + gatew[:, e:e + 1] * (h @ w2[e].T + b2[e])
        hs = jax.nn.silu(xf @ sw1.T + sb1) * (xf @ sw3.T + sb3)
        y = y + hs @ sw2.T + sb2
        return y.reshape(Bv, Sv, Dv)

    def _L1_attn_ref(x, Wk, Wv, Wo, freqs):
        import jax, jax.numpy as jnp
        import numpy as np
        TWO_PI = 6.283185307179586
        B, T, C = x.shape
        k_real = x @ Wk.T
        v_real = x @ Wv.T
        v = v_real.astype(jnp.complex64)
        t = jnp.arange(T, dtype=jnp.float32)
        rotors = jnp.exp(1j * (t[:, None] * freqs[None, :])).astype(jnp.complex64)
        memory_trace = jnp.cumsum(v * rotors[None, :, :], axis=1)
        retrieved = jnp.real(memory_trace * jnp.conj(rotors)[None, :, :])
        return retrieved @ Wo.T

    def _L1_ffn_ref(x, Wqkv, q_scale, k_scale, Wo, ln_g, ln_b, W1, b1, W2, b2):
        import jax, jax.numpy as jnp
        import numpy as np
        DIM = 128
        DEPTH = 6
        HEADS = 16
        DIM_HEAD = 64
        WINDOW = 32
        INNER = HEADS * DIM_HEAD
        DIM_INNER = int(DIM * 4 * 2 / 3)
        QK_SCALE = 8.0

        def shift_tokens(t):
            a, s = jnp.split(t, 2, -1)
            s = jnp.pad(s, ((0, 0), (1, 0), (0, 0)))[:, :-1]
            return jnp.concatenate([a, s], -1)

        def l2norm(t):
            return t / jnp.maximum(jnp.linalg.norm(t, axis=-1, keepdims=True), 1e-12)

        def rotate_half(x):
            x1, x2 = jnp.split(x, 2, -1)
            return jnp.concatenate([-x2, x1], -1)

        def rotary_tables(n):
            half = jnp.arange(0, DIM_HEAD, 2, dtype=jnp.float32)
            inv_freq = 1.0 / 10000.0 ** (half / DIM_HEAD)
            t = jnp.arange(n, dtype=jnp.float32)
            freqs = t[:, None] * inv_freq[None, :]
            freqs = jnp.concatenate([freqs, freqs], -1)
            base_scale = (half + 0.4 * DIM_HEAD) / (1.4 * DIM_HEAD)
            power = (t - n // 2) / (WINDOW // 2)
            scale = base_scale[None, :] ** power[:, None]
            scale = jnp.concatenate([scale, scale], -1)
            return (freqs, scale)

        def local_attention(q, k, v):
            b, h, n, d = q.shape
            w = WINDOW
            nw = n // w
            bq = q.reshape(b, h, nw, w, d)
            bk = k.reshape(b, h, nw, w, d)
            bv = v.reshape(b, h, nw, w, d)

            def look(t):
                p = jnp.pad(t, ((0, 0), (0, 0), (1, 0), (0, 0), (0, 0)))
                return jnp.concatenate([p[:, :, :nw], p[:, :, 1:]], axis=3)
            bk2, bv2 = (look(bk), look(bv))
            seq = jnp.arange(n).reshape(nw, w)
            seq_p = jnp.pad(seq, ((1, 0), (0, 0)), constant_values=-1)
            jt = jnp.concatenate([seq_p[:nw], seq_p[1:]], axis=1)
            it = seq[:, :, None]
            jb = jt[:, None, :]
            mask = (it < jb) | (it > jb + w) | (jb == -1)
            sim = jnp.einsum('bhwie,bhwje->bhwij', bq, bk2) * QK_SCALE
            sim = jnp.where(mask, -jnp.finfo(sim.dtype).max, sim)
            attn = jax.nn.softmax(sim, -1)
            out = jnp.einsum('bhwij,bhwje->bhwie', attn, bv2)
            return out.reshape(b, h, n, d)

        def attn_layer(x, Wqkv, qs, ksc, Wo):
            b, n, _ = x.shape
            qkv = x @ Wqkv
            q, k, v = jnp.split(qkv, 3, -1)
            sh = lambda t: t.reshape(b, n, HEADS, DIM_HEAD).transpose(0, 2, 1, 3)
            q, k, v = (sh(q), sh(k), sh(v))
            q = l2norm(q) * qs
            k = l2norm(k) * ksc
            freqs, scale = rotary_tables(n)
            cos, sin = (jnp.cos(freqs), jnp.sin(freqs))
            q = q * cos * scale + rotate_half(q) * sin * scale
            inv = 1.0 / scale
            k = k * cos * inv + rotate_half(k) * sin * inv
            out = local_attention(q, k, v)
            out = out.transpose(0, 2, 1, 3).reshape(b, n, INNER)
            return out @ Wo

        def ffn_layer(x, g, bln, W1, b1, W2, b2):
            mu = x.mean(-1, keepdims=True)
            var = ((x - mu) ** 2).mean(-1, keepdims=True)
            xn = (x - mu) / jnp.sqrt(var + 1e-05) * g + bln
            hg = xn @ W1 + b1
            a, gate = jnp.split(hg, 2, -1)
            return a * jax.nn.gelu(gate, approximate=False) @ W2 + b2
        for i in range(DEPTH):
            x = attn_layer(shift_tokens(x), Wqkv[i], q_scale[i], k_scale[i], Wo[i]) + x
            x = ffn_layer(shift_tokens(x), ln_g[i], ln_b[i], W1[i], b1[i], W2[i], b2[i]) + x
        return x

    def _L2_attn_ref(hidden_states, qkv_w, z_w, b_w, a_w, conv_w, dt_bias, A_log, norm_w, out_w):
        import jax, jax.numpy as jnp
        import numpy as np
        from jax import lax
        B, T, HID = (4, 128, 128)
        H, DK, DV = (8, 128, 128)
        KCONV = 4
        EPS = 1e-06
        KEY_DIM = H * DK
        VAL_DIM = H * DV
        CONV_DIM = 2 * KEY_DIM + VAL_DIM
        b_, t_, _ = hidden_states.shape
        mixed = jnp.einsum('bth,ch->btc', hidden_states, qkv_w)
        x = mixed.transpose(0, 2, 1)
        x = lax.conv_general_dilated(x, conv_w, window_strides=(1,), padding=[(KCONV - 1, 0)], feature_group_count=CONV_DIM, dimension_numbers=('NCH', 'OIH', 'NCH'))
        mixed = x.transpose(0, 2, 1)
        z = jnp.einsum('bth,vh->btv', hidden_states, z_w).reshape(b_, t_, H, DV)
        bb = jnp.einsum('bth,nh->btn', hidden_states, b_w)
        aa = jnp.einsum('bth,nh->btn', hidden_states, a_w)
        q, k, v = jnp.split(mixed, 3, axis=-1)
        q = q.reshape(b_, t_, H, DK)
        k = k.reshape(b_, t_, H, DK)
        v = v.reshape(b_, t_, H, DV)
        beta = jax.nn.sigmoid(bb)
        g = -jnp.exp(A_log) * jax.nn.softplus(aa + dt_bias)
        alpha = jnp.exp(g)

        def step(S, inp):
            q_t, k_t, v_t, beta_t, alpha_t = inp
            S = S * alpha_t[..., None, None]
            kv = jnp.einsum('bhk,bhkv->bhv', k_t, S)
            S = S + jnp.einsum('bhk,bhv->bhkv', k_t, (v_t - kv) * beta_t[..., None])
            o_t = jnp.einsum('bhk,bhkv->bhv', q_t, S)
            return (S, o_t)
        qt = q.transpose(1, 0, 2, 3)
        kt = k.transpose(1, 0, 2, 3)
        vt = v.transpose(1, 0, 2, 3)
        bt = beta.transpose(1, 0, 2)
        at = alpha.transpose(1, 0, 2)
        S0 = jnp.zeros((b_, H, DK, DV), hidden_states.dtype)
        _, o = lax.scan(step, S0, (qt, kt, vt, bt, at))
        o = o.transpose(1, 0, 2, 3)
        var = jnp.mean(jnp.square(o), axis=-1, keepdims=True)
        o = o * lax.rsqrt(var + EPS) * norm_w
        o = o * (z * jax.nn.sigmoid(z))
        out = jnp.einsum('btv,hv->bth', o.reshape(b_, t_, VAL_DIM), out_w)
        return out

    def _L2_ffn_ref(x, We, be, Wg, bg):
        import jax, jax.numpy as jnp
        import numpy as np
        D_MODEL = 128
        NUM_EXPERTS = 8
        TOP_K = 2
        B, S, D = x.shape
        xf = x.reshape(-1, D)
        gate_logits = xf @ Wg.T + bg
        topk_vals, topk_idx = jax.lax.top_k(gate_logits, TOP_K)
        gate_w = jax.nn.softmax(topk_vals, axis=-1)
        all_out = jnp.einsum('nd,ehd->neh', xf, We) + be
        sel = jnp.take_along_axis(all_out, topk_idx[:, :, None], axis=1)
        out = jnp.sum(sel * gate_w[:, :, None], axis=1)
        return out.reshape(B, S, D)

    def _L3_attn_ref(x, W_in, conv_w, conv_b, W_x, W_dt, b_dt, A_log, D, W_out):
        import jax, jax.numpy as jnp
        import numpy as np
        from jax import lax
        D_MODEL, D_STATE, D_CONV, EXPAND = (128, 16, 4, 2)
        D_INNER = D_MODEL * EXPAND
        BATCH, SEQ = (4, 256)

        def _mamba_forward(x, W_in, conv_w, conv_b, W_x, W_dt, b_dt, A_log, D, W_out):
            batch, seq_len, _ = x.shape
            xz = x @ W_in
            x_in, z = jnp.split(xz, 2, axis=-1)
            x_c = lax.conv_general_dilated(x_in.transpose(0, 2, 1), conv_w, window_strides=(1,), padding=[(D_CONV - 1, 0)], feature_group_count=D_INNER, dimension_numbers=('NCH', 'OIH', 'NCH')) + conv_b[None, :, None]
            x_conv = jax.nn.silu(x_c.transpose(0, 2, 1))
            A = -jnp.exp(A_log)
            Bm, Cm = jnp.split(x_conv @ W_x, 2, axis=-1)
            dt = jax.nn.softplus(x_conv @ W_dt + b_dt)

            def step(h, ins):
                u_t, dt_t, B_t, C_t = ins
                dA = jnp.exp(dt_t[:, :, None] * A)
                h = dA * h + (dt_t * u_t)[:, :, None] * B_t[:, None, :]
                y_t = jnp.einsum('bdn,bn->bd', h, C_t)
                return (h, y_t)
            h0 = jnp.zeros((batch, D_INNER, D_STATE), dtype=x.dtype)
            xs = (x_conv.transpose(1, 0, 2), dt.transpose(1, 0, 2), Bm.transpose(1, 0, 2), Cm.transpose(1, 0, 2))
            _, ys = lax.scan(step, h0, xs)
            y = ys.transpose(1, 0, 2)
            y = y + x_conv * D
            y = y * jax.nn.silu(z)
            return y @ W_out
        return _mamba_forward(x, W_in, conv_w, conv_b, W_x, W_dt, b_dt, A_log, D, W_out)

    def _L3_ffn_ref(hidden_states, gate_w, W1, W2, W3, dom):
        import jax, jax.numpy as jnp
        import numpy as np
        H = 128
        I = 512
        E = 8
        TOPK = 2
        B, S, Hd = hidden_states.shape
        x = hidden_states.reshape(-1, Hd)
        router_logits = x @ gate_w
        top_logits, top_idx = jax.lax.top_k(router_logits, TOPK)
        weights = jax.nn.softmax(top_logits, axis=-1)
        w_dense = jnp.einsum('tk,tke->te', weights, jax.nn.one_hot(top_idx, E, dtype=weights.dtype))
        out = jnp.zeros_like(x)
        for e in range(E):
            xe = x + dom[e]
            h = jax.nn.silu(xe @ W1[e]) * (xe @ W3[e])
            out = out + w_dense[:, e:e + 1] * (h @ W2[e])
        return out.reshape(B, S, Hd)
    x = L0_attn_x
    x = x + _L0_attn_ref(_layernorm(x, axis=-1), L0_attn_W_in, L0_attn_conv_w, L0_attn_conv_b, L0_attn_W_xproj, L0_attn_W_dt, L0_attn_b_dt, L0_attn_A_log, L0_attn_Dp, L0_attn_W_out)
    x = x + _L0_ffn_ref(_layernorm(x, axis=-1), L0_ffn_gate_w, L0_ffn_expert_bias, L0_ffn_w1, L0_ffn_b1, L0_ffn_w2, L0_ffn_b2, L0_ffn_w3, L0_ffn_b3, L0_ffn_sw1, L0_ffn_sb1, L0_ffn_sw2, L0_ffn_sb2, L0_ffn_sw3, L0_ffn_sb3)
    x = x + _L1_attn_ref(_layernorm(x, axis=-1), L1_attn_Wk, L1_attn_Wv, L1_attn_Wo, L1_attn_freqs)
    x = x + _L1_ffn_ref(_layernorm(x, axis=-1), L1_ffn_Wqkv, L1_ffn_q_scale, L1_ffn_k_scale, L1_ffn_Wo, L1_ffn_ln_g, L1_ffn_ln_b, L1_ffn_W1, L1_ffn_b1, L1_ffn_W2, L1_ffn_b2)
    x = x + _L2_attn_ref(_layernorm(x, axis=-1), L2_attn_qkv_w, L2_attn_z_w, L2_attn_b_w, L2_attn_a_w, L2_attn_conv_w, L2_attn_dt_bias, L2_attn_A_log, L2_attn_norm_w, L2_attn_out_w)
    x = x + _L2_ffn_ref(_layernorm(x, axis=-1), L2_ffn_We, L2_ffn_be, L2_ffn_Wg, L2_ffn_bg)
    x = x + _L3_attn_ref(_layernorm(x, axis=-1), L3_attn_W_in, L3_attn_conv_w, L3_attn_conv_b, L3_attn_W_x, L3_attn_W_dt, L3_attn_b_dt, L3_attn_A_log, L3_attn_D, L3_attn_W_out)
    x = x + _L3_ffn_ref(_layernorm(x, axis=-1), L3_ffn_gate_w, L3_ffn_W1, L3_ffn_W2, L3_ffn_W3, L3_ffn_dom)
    return x

_drawn_inputs = setup_inputs


def setup_inputs(seed=0):
    import zlib

    import numpy as np

    out = dict(_drawn_inputs(seed))
    spreads = {'L0_attn_Dp': (1.0, 0.2),
     'L0_ffn_expert_bias': (0.0, 0.1),
     'L1_ffn_q_scale': (1.0, 0.6),
     'L1_ffn_k_scale': (1.0, 0.6),
     'L1_ffn_ln_g': (1.0, 0.6),
     'L1_ffn_ln_b': (0.0, 0.8),
     'L1_ffn_b1': (0.0, 0.8),
     'L1_ffn_b2': (0.0, 0.1),
     'L2_attn_dt_bias': (1.0, 0.6),
     'L2_attn_norm_w': (1.0, 0.6),
     'L3_attn_D': (1.0, 0.6)}
    factors = {'L0_attn_conv_b': 4.192,
     'L0_attn_b_dt': 8.0,
     'L0_ffn_b1': 5.901,
     'L0_ffn_b3': 6.084,
     'L0_ffn_sb1': 4.465,
     'L0_ffn_sb3': 4.292,
     'L1_ffn_W1': 4.739,
     'L1_ffn_W2': 4.509,
     'L2_attn_z_w': 2.704,
     'L2_attn_b_w': 30.393,
     'L2_attn_a_w': 8.0,
     'L2_attn_A_log': 8.0,
     'L2_attn_out_w': 2.685,
     'L2_ffn_be': 18.455,
     'L3_attn_conv_b': 64.0,
     'L3_attn_b_dt': 64.0,
     'L3_ffn_dom': 64.0,
     'L2_ffn_bg': 4.876,
     'L3_attn_W_dt': 3.731,
     'L3_attn_A_log': 8.0,
     'L3_ffn_gate_w': 3.783,
     'L3_ffn_W1': 3.292,
     'L3_ffn_W2': 3.219,
     'L3_ffn_W3': 3.168}
    for name, (base, spread) in spreads.items():
        noise = np.random.default_rng([zlib.crc32(name.encode()), seed]).standard_normal(out[name].shape)
        drawn = base * np.exp(spread * noise) if base else spread * noise
        out[name] = jnp.asarray(drawn.astype(out[name].dtype))
    for name, factor in factors.items():
        out[name] = (out[name] * factor).astype(out[name].dtype)
    return out
```

```python
from contextlib import ExitStack

import numpy as np

import concourse.bass as bass
from concourse import mybir

F32 = mybir.dt.float32
BF16 = mybir.dt.bfloat16
I32 = mybir.dt.int32
U32 = mybir.dt.uint32
ALU = mybir.AluOpType
ACT = mybir.ActivationFunctionType
AX = mybir.AxisListType

LN_EXP = "natural_log_exp_and_others"
P = 128
BATCH = 8
T = 256
D = 128
N = BATCH * T
TILES = N // P
GROUP = 512
GROUPS = N // GROUP
TPG = GROUP // P
SPG = GROUP // T
EPS = 1e-5


class Shared:
    pass


class Chain:

    def __init__(self, eng, sem, base=0):
        self.eng, self.sem, self.base, self.count = eng, sem, base, 0

    def add(self, ins):
        ins.then_inc(self.sem, 1)
        self.count += 1

    def settle(self, behind=0):
        self.eng.wait_ge(self.sem, self.base + self.count - behind)

    def step(self, ins):
        self.add(ins)
        self.settle()


class Signals:

    def __init__(self, nc, tag):
        self.nc, self.tag, self.stack, self.all = nc, tag, ExitStack(), []

    def __enter__(self):
        return self

    def __call__(self, name):
        self.all.append(self.stack.enter_context(self.nc.semaphore(f"{self.tag}_{name}")))
        return self.all[-1]

    def __exit__(self, *_):
        with self.nc.Block() as block:
            @block.sync
            def _(sp):
                for s in self.all:
                    sp.sem_clear(s)
        self.stack.close()


def tok(c):
    return slice(c * GROUP, (c + 1) * GROUP)


def spread(ap, n):
    return ap.unsqueeze(2).to_broadcast([ap.shape[0], ap.shape[1], n])


def wait_apart(eng, sem, value, passed):
    eng.wait_ge(sem, value)
    eng.sem_inc(passed, 1)


def set_up(nc, g, x_dram):
    with ExitStack() as ctx:
        sem = ctx.enter_context(Signals(nc, "setup"))
        loaded, filled = sem("loaded"), sem("filled")
        block = ctx.enter_context(nc.Block())

        @block.sync
        def _(sp):
            sp.dma_start(g.x[:, :, :], x_dram.rearrange("(n p) d -> p n d", p=P)).then_inc(loaded, 16)
            sp.wait_ge(loaded, 16)

        @block.gpsimd
        def _(pool):
            pool.memset(g.ident[:, :], 0.0).then_inc(filled, 1)
            pool.memset(g.eps[:, :], EPS).then_inc(filled, 1)
            pool.memset(g.one[:, :], 1.0).then_inc(filled, 1)
            pool.wait_ge(filled, 3)
            pool.affine_select(out=g.ident[:, :], in_=g.ident[:, :], compare_op=ALU.not_equal, fill=1.0, base=0,
                               pattern=[[-1, P]], channel_multiplier=1).then_inc(filled, 1)


def norm_and_turn(nc, g, tag, loads):
    with ExitStack() as ctx:
        sem = ctx.enter_context(Signals(nc, tag))
        st = ctx.enter_context(nc.sbuf_tensor(f"{tag}_stats", [P, 5, TILES], F32))
        xc = ctx.enter_context(nc.sbuf_tensor(f"{tag}_xc", [P, TILES, D], F32))
        sq = ctx.enter_context(nc.sbuf_tensor(f"{tag}_sq", [P, TILES, D], F32))
        centred, squared, var_ready, rstd_ready = sem("centred"), sem("squared"), sem("var"), sem("rstd")
        normed, turned, dve_own, act_own = sem("normed"), sem("turned"), sem("dve"), sem("act")
        block = ctx.enter_context(nc.Block())

        @block.sync
        def _(sp):
            for dst, src in loads:
                sp.dma_start(dst, src).then_inc(g.weights, 16)
                g.weights_due += 16

        @block.vector
        def _(dve):
            own = Chain(dve, dve_own)
            own.step(dve.tensor_reduce(st[:, 0, :], g.x[:, :, :], AX.X, ALU.add))
            own.step(dve.tensor_scalar(st[:, 1, :], st[:, 0, :], -1.0 / D, None, ALU.mult))
            dve.tensor_tensor(xc[:, :, :], g.x[:, :, :], spread(st[:, 1, :], D), ALU.add).then_inc(centred, 1)
            dve.wait_ge(squared, 1)
            dve.tensor_reduce(st[:, 2, :], sq[:, :, :], AX.X, ALU.add).then_inc(var_ready, 1)
            dve.wait_ge(rstd_ready, 1)
            for c in range(GROUPS):
                t = slice(TPG * c, TPG * (c + 1))
                dve.tensor_tensor(g.xn[:, t, :], xc[:, t, :], spread(st[:, 4, t], D), ALU.mult).then_inc(normed, 1)

        @block.scalar
        def _(act):
            act.preload_act_table_set(LN_EXP)
            act.wait_ge(centred, 1)
            act.activation(sq[:, :, :], xc[:, :, :], ACT.Square).then_inc(squared, 1)
            act.wait_ge(var_ready, 1)
            act.activation(st[:, 3, :], st[:, 2, :], ACT.Ln, bias=g.eps[:, 0:1], scale=1.0 / D).then_inc(act_own, 1)
            act.wait_ge(act_own, 1)
            act.activation(st[:, 4, :], st[:, 3, :], ACT.Exp, scale=-0.5).then_inc(rstd_ready, 1)
            for c in range(GROUPS):
                act.wait_ge(turned, c + 1)
                act.activation(g.xnT[:, tok(c)], g.bank[c][:, :], ACT.Copy)

        @block.tensor
        def _(pe):
            for c in range(GROUPS):
                pe.wait_ge(normed, c + 1)
                for i in range(TPG):
                    mm = pe.transpose(g.bank[c][:, i * P:(i + 1) * P], g.xn[:, TPG * c + i, :], g.ident[:, :])
                mm.then_inc(turned, 1)


def mamba(nc, g, tag, w, d_in):
    HALVES, STATES, TAPS = 2, 16, 4
    rank_one_dt = "w_dt_col" in d_in
    with ExitStack() as ctx:
        sem = ctx.enter_context(Signals(nc, tag))

        def sb(n, shape, dt=F32):
            return ctx.enter_context(nc.sbuf_tensor(f"{tag}_{n}", shape, dt))
        w_in = sb("w_in", [P, 4 * P])
        conv_w, conv_b = sb("conv_w", [P, HALVES, TAPS]), sb("conv_b", [P, HALVES])
        w_bc = sb("w_bc", [P, HALVES, 2 * STATES])
        w_dt = sb("w_dt", [1, HALVES * P] if rank_one_dt else [P, HALVES, HALVES * P])
        w_dtc = sb("w_dtc", [P, HALVES])
        b_dt, a_log, skip = sb("b_dt", [P, HALVES]), sb("a_log", [P, HALVES, STATES]), sb("skip", [P, HALVES])
        w_out = sb("w_out", [P, HALVES, D])
        loads = [(w_in[:, :], d_in["w_in"]), (conv_w[:, :, :], d_in["conv_w"]), (conv_b[:, :], d_in["conv_b"]),
                 (w_bc[:, :, :], d_in["w_bc"]), (b_dt[:, :], d_in["b_dt"]), (a_log[:, :, :], d_in["a_log"]),
                 (skip[:, :], d_in["skip"]), (w_out[:, :, :], d_in["w_out"])]
        if rank_one_dt:
            loads += [(w_dt[:, :], d_in["w_dt"]), (w_dtc[:, :], d_in["w_dt_col"])]
        else:
            loads += [(w_dt[:, :, :], d_in["w_dt"])]
        norm_and_turn(nc, g, tag + "_ln", loads)

        xpad = sb("xpad", [P, HALVES, BATCH, T + TAPS - 1])
        cv = sb("cv", [P, HALVES, N])
        u = sb("u", [P, HALVES, N])
        sz = sb("sz", [P, HALVES, N])
        dt = sb("dt", [P, HALVES, N])
        du = sb("du", [P, HALVES, N])
        bc3 = sb("bc3", [3 * 32, N], BF16)
        part = sb("part", [32, 2, N], BF16)
        rest = sb("rest", [32, 2, N])
        dt_row = sb("dt_row", [1, N])
        pick = sb("pick", [3 * 32, 2 * STATES, P], BF16)
        a_neg = sb("a_neg", [P, HALVES, STATES])
        decay = sb("decay", [P, 2, HALVES, SPG, T])
        dbu = sb("dbu", [P, HALVES, GROUP])
        state = sb("state", [P, HALVES, GROUP])
        hc = sb("hc", [P, 2, HALVES, GROUP])
        y = sb("y", [P, HALVES, GROUP])

        prepared, picked = sem("prepared"), sem("picked")
        proj_ready, proj_used, conv_ready, u_ready = sem("proj_ready"), sem("proj_used"), sem("conv_ready"), sem("u_ready")
        bc_ready, bc_split, bc_moved = sem("bc_ready"), sem("bc_split"), sem("bc_moved")
        row_ready, row_copied, dt_psum, dt_biased = sem("row_ready"), sem("row_copied"), sem("dt_psum"), sem("dt_biased")
        log_ready, a_exp, scan_inputs = sem("log_ready"), sem("a_exp"), sem("scan_inputs")
        spread_ready, spread_used = sem("spread_ready"), sem("spread_used")
        decay_ready, decay_used = sem("decay_ready"), sem("decay_used")
        hc_ready, hc_used, sum_ready, sum_used = sem("hc_ready"), sem("hc_used"), sem("sum_ready"), sem("sum_used")
        y_ready, out_ready, out_used = sem("y_ready"), sem("out_ready"), sem("out_used")
        dve_own, act_own, act_passed = sem("dve"), sem("act"), sem("act_passed")
        block = ctx.enter_context(nc.Block())

        @block.gpsimd
        def _(pool):
            pool.memset(pick[:, :, :], 0.0).then_inc(picked, 1)
            for k in range(3):
                pool.wait_ge(picked, k + 1)
                pool.affine_select(out=pick[:, :, :], in_=pick[:, :, :], compare_op=ALU.not_equal, fill=1.0,
                                   base=-32 * k, pattern=[[-1, 2 * STATES], [0, P]],
                                   channel_multiplier=1).then_inc(picked, 1)

        @block.tensor
        def _(pe):
            pe.wait_ge(g.weights, g.weights_due)
            for i in range(4 * GROUPS):
                m, c = divmod(i, GROUPS)
                if i >= 8:
                    pe.wait_ge(proj_used, i - 7)
                pe.matmul(g.bank[i % 8][:, :], w_in[:, m * P:(m + 1) * P], g.xnT[:, tok(c)],
                          start=True, stop=True).then_inc(proj_ready, 1)
            pe.wait_ge(u_ready, HALVES)
            for c in range(GROUPS):
                pe.wait_ge(proj_used, 9 + c)
                for h in range(HALVES):
                    mm = pe.matmul(g.bank[c][0:2 * STATES, :], w_bc[:, h, :], u[:, h, tok(c)],
                                   start=(h == 0), stop=(h == 1))
                mm.then_inc(bc_ready, 1)
            pe.wait_ge(proj_used, 4 * GROUPS)
            if rank_one_dt:
                for c in range(GROUPS):
                    for h in range(HALVES):
                        mm = pe.matmul(g.bank[4 + c][0:1, :], w_dtc[:, h:h + 1], u[:, h, tok(c)],
                                       start=(h == 0), stop=(h == 1))
                    mm.then_inc(row_ready, 1)
            pe.wait_ge(bc_split, 1)
            for i in range(HALVES * GROUPS):
                h, c = divmod(i, GROUPS)
                if rank_one_dt:
                    pe.wait_ge(row_copied, GROUPS)
                    pe.matmul(g.bank[i][:, :], w_dt[0:1, h * P:(h + 1) * P], dt_row[0:1, tok(c)],
                              start=True, stop=True).then_inc(dt_psum, 1)
                else:
                    for k in range(HALVES):
                        mm = pe.matmul(g.bank[i][:, :], w_dt[:, k, h * P:(h + 1) * P], u[:, k, tok(c)],
                                       start=(k == 0), stop=(k == 1))
                    mm.then_inc(dt_psum, 1)
            pe.wait_ge(dt_biased, HALVES * GROUPS)
            pe.wait_ge(bc_moved, 2)
            pe.wait_ge(picked, 4)
            with pe.Fori(0, GROUPS) as c:
                def sum_state(s):
                    pe.wait_ge(hc_ready, c * STATES + (s + 1))
                    if s == 0:
                        pe.wait_ge(sum_used, c + 1)
                    for h in range(HALVES):
                        mm = pe.matmul(g.bank[4 + h][:, :], g.ident[:, :], hc[:, s % 2, h, :],
                                       start=(s == 0), stop=(s == STATES - 1))
                    mm.then_inc(hc_used, 1)
                    if s == STATES - 1:
                        pe.wait_ge(hc_used, c * STATES + (s + 3))
                        pe.sem_inc(sum_ready, 1)
                for s in range(STATES):
                    b = s % 2
                    pe.wait_ge(spread_used, c * STATES + (s + 1))
                    pe.matmul(g.bank[b][:, :], pick[:, s, :], bc3[:, bass.ts(c, GROUP)], start=True, stop=True)
                    pe.matmul(g.bank[2 + b][:, :], pick[:, STATES + s, :], bc3[:, bass.ts(c, GROUP)],
                              start=True, stop=True).then_inc(spread_ready, 1)
                    if s >= 1:
                        sum_state(s - 1)
                sum_state(STATES - 1)
                pe.wait_ge(y_ready, c + 1)
                pe.wait_ge(out_used, c + 1)
                for i in range(TPG):
                    for h in range(HALVES):
                        mm = pe.matmul(g.bank[6][:, i * P:(i + 1) * P], y[:, h, i * P:(i + 1) * P], w_out[:, h, :],
                                       start=(h == 0), stop=(h == 1))
                mm.then_inc(out_ready, 1)

        @block.scalar
        def _(act):
            own = Chain(act, act_own)
            act.wait_ge(prepared, 1)
            for i in range(4 * GROUPS):
                m, c = divmod(i, GROUPS)
                act.wait_ge(proj_ready, i + 1)
                if m < 2:
                    act.activation(xpad[:, m, SPG * c:SPG * (c + 1), TAPS - 1:],
                                   g.bank[i % 8][:, :].rearrange("p (b t) -> p b t", t=T), ACT.Copy).then_inc(proj_used, 1)
                else:
                    act.activation(sz[:, m - 2, tok(c)], g.bank[i % 8][:, :], ACT.Silu).then_inc(proj_used, 1)
            for h in range(HALVES):
                act.wait_ge(conv_ready, h + 1)
                act.activation(u[:, h, :], cv[:, h, :], ACT.Silu, bias=conv_b[:, h:h + 1]).then_inc(u_ready, 1)
            if rank_one_dt:
                for c in range(GROUPS):
                    act.wait_ge(row_ready, c + 1)
                    act.activation(dt_row[0:1, tok(c)], g.bank[4 + c][0:1, :], ACT.Copy).then_inc(row_copied, 1)
            act.wait_ge(bc_split, 1)
            act.activation(bc3[32:64, :], part[:, 1, :], ACT.Copy).then_inc(bc_moved, 1)
            for i in range(HALVES * GROUPS):
                h, c = divmod(i, GROUPS)
                act.wait_ge(dt_psum, i + 1)
                act.activation(dt[:, h, tok(c)], g.bank[i][:, :], ACT.Identity, bias=b_dt[:, h:h + 1]).then_inc(dt_biased, 1)
            act.preload_act_table_set(LN_EXP)
            for h in range(HALVES):
                act.wait_ge(dt_biased, GROUPS * (h + 1))
                own.step(act.activation(cv[:, h, :], dt[:, h, :], ACT.Abs))
                own.step(act.activation(cv[:, h, :], cv[:, h, :], ACT.Exp, scale=-1.0))
                act.activation(cv[:, h, :], cv[:, h, :], ACT.Ln, bias=g.one[:, 0:1]).then_inc(log_ready, 1)
            act.activation(a_neg[:, :, :], a_log[:, :, :], ACT.Exp).then_inc(a_exp, 1)
            act.wait_ge(scan_inputs, 1)
            with act.Fori(0, GROUPS) as c:
                for s in range(STATES):
                    wait_apart(act, decay_used, c * STATES + (s + 1), act_passed)
                    for h in range(HALVES):
                        ins = act.activation(
                            decay[:, s % 2, h, :, 1:T],
                            dt[:, h, bass.ts(c, GROUP)].rearrange("p (b t) -> p b t", t=T)[:, :, 1:T],
                            ACT.Exp, scale=a_neg[:, h, s:s + 1])
                    ins.then_inc(decay_ready, 1)

        @block.vector
        def _(dve):
            own = Chain(dve, dve_own)
            own.add(dve.memset(xpad[:, :, :, 0:TAPS - 1], 0.0))
            own.add(dve.memset(decay[:, :, :, :, 0:1], 0.0))
            own.settle()
            dve.sem_inc(prepared, 1)
            for h in range(HALVES):
                dve.wait_ge(proj_used, GROUPS * (h + 1))
                cvh = cv[:, h, :].rearrange("p (b t) -> p b t", t=T)
                own.step(dve.tensor_scalar(cvh, xpad[:, h, :, 0:T], conv_w[:, h, 0:1], None, ALU.mult))
                for k in range(1, TAPS):
                    ins = dve.scalar_tensor_tensor(out=cvh, in0=xpad[:, h, :, k:k + T], scalar=conv_w[:, h, k:k + 1],
                                                   in1=cvh, op0=ALU.mult, op1=ALU.add)
                    if k < TAPS - 1:
                        own.step(ins)
                ins.then_inc(conv_ready, 1)
            for c in range(GROUPS):
                dve.wait_ge(bc_ready, c + 1)
                own.step(dve.tensor_copy(bc3[0:32, tok(c)], g.bank[c][0:32, :]))
                own.add(dve.tensor_tensor(rest[:, 0, tok(c)], g.bank[c][0:32, :], bc3[0:32, tok(c)], ALU.subtract))
            own.settle()
            own.step(dve.tensor_copy(part[:, 1, :], rest[:, 0, :]))
            dve.tensor_tensor(bc3[64:96, :], rest[:, 0, :], part[:, 1, :], ALU.subtract).then_inc(bc_split, 1)
            dve.wait_ge(bc_split, 1)
            dve.sem_inc(bc_moved, 1)
            for h in range(HALVES):
                dve.wait_ge(log_ready, h + 1)
                own.step(dve.scalar_tensor_tensor(out=dt[:, h, :], in0=dt[:, h, :], scalar=0.0, in1=cv[:, h, :],
                                                  op0=ALU.max, op1=ALU.add))
                own.add(dve.tensor_tensor(du[:, h, :], dt[:, h, :], u[:, h, :], ALU.mult))
            dve.wait_ge(a_exp, 1)
            own.step(dve.tensor_scalar(a_neg[:, :, :], a_neg[:, :, :], -1.0, None, ALU.mult))
            dve.sem_inc(scan_inputs, 1)
            for free, n in ((decay_used, 2), (spread_used, 2), (hc_used, 2), (sum_used, 1), (out_used, 1)):
                dve.sem_inc(free, n)
            STEPS_PER_GROUP = 4 * STATES + HALVES
            with dve.Fori(0, GROUPS) as c:
                own = Chain(dve, dve_own, c * STEPS_PER_GROUP + own.count)
                for s in range(STATES):
                    b = s % 2
                    dve.wait_ge(spread_ready, c * STATES + (s + 1))
                    for h in range(HALVES):
                        own.add(dve.tensor_tensor(dbu[:, h, :], du[:, h, bass.ts(c, GROUP)], g.bank[b][:, :], ALU.mult))
                    dve.wait_ge(decay_ready, c * STATES + (s + 1))
                    for h in range(HALVES):
                        own.settle(behind=1)
                        own.add(dve.tensor_tensor_scan(state[:, h, :], decay[:, b, h, :, :].rearrange("p b t -> p (b t)"),
                                                       dbu[:, h, :], 0.0, ALU.mult, ALU.add))
                    dve.wait_ge(hc_used, c * STATES + (s + 1))
                    for h in range(HALVES):
                        own.settle(behind=1 - h)
                        if h == 1:
                            dve.sem_inc(decay_used, 1)
                        ins = dve.tensor_tensor(hc[:, b, h, :], state[:, h, :], g.bank[2 + b][:, :], ALU.mult)
                    ins.then_inc(hc_ready, 1)
                    dve.wait_ge(hc_ready, c * STATES + (s + 1))
                    dve.sem_inc(spread_used, 1)
                dve.wait_ge(sum_ready, c + 1)
                for h in range(HALVES):
                    own.add(dve.scalar_tensor_tensor(out=state[:, h, :], in0=u[:, h, bass.ts(c, GROUP)],
                                                     scalar=skip[:, h:h + 1], in1=g.bank[4 + h][:, :],
                                                     op0=ALU.mult, op1=ALU.add))
                own.settle()
                dve.sem_inc(sum_used, 1)
                for h in range(HALVES):
                    ins = dve.tensor_tensor(y[:, h, :], state[:, h, :], sz[:, h, bass.ts(c, GROUP)], ALU.mult)
                ins.then_inc(y_ready, 1)
                dve.wait_ge(out_ready, c + 1)
                x_c = g.x[:, bass.ts(c, TPG), :]
                dve.tensor_tensor(x_c, x_c, g.bank[6][:, :].rearrange("p (n d) -> p n d", d=D), ALU.add).then_inc(out_used, 1)
                assert own.count == STEPS_PER_GROUP


def route(nc, g, tag, experts, gates, gates_t, gates3, gate_w, bias, sigmoid_scores):
    E = experts
    with ExitStack() as ctx:
        sem = ctx.enter_context(Signals(nc, tag))

        def sb(n, shape, dt=F32):
            return ctx.enter_context(nc.sbuf_tensor(f"{tag}_{n}", shape, dt))
        raw, ranked = sb("raw", [P, TILES, E]), sb("ranked", [P, TILES, E])
        top, top_index = sb("top", [P, TILES, 8]), sb("top_index", [P, TILES, 8], U32)
        index = sb("index", [P, TILES, 8])
        number = sb("number", [P, TILES, E])
        first, second = sb("first", [P, TILES, E]), sb("second", [P, TILES, E])
        soft, weight = sb("soft", [P, TILES, E]), sb("weight", [P, 4, TILES])
        rest, part = sb("rest", [32, N]), sb("part", [32, N], BF16)
        logits, numbered, exp_in, exp_out = sem("logits"), sem("numbered"), sem("exp_in"), sem("exp_out")
        gated, turned, split, own_sem = sem("gated"), sem("turned"), sem("split"), sem("dve")
        block = ctx.enter_context(nc.Block())

        @block.gpsimd
        def _(pool):
            pool.iota(number[:, :, :], pattern=[[0, TILES], [1, E]], base=0, channel_multiplier=0,
                      allow_small_or_imprecise_dtypes=True).then_inc(numbered, 1)

        @block.tensor
        def _(pe):
            pe.wait_ge(g.weights, g.weights_due)
            for t in range(TILES):
                mm = pe.matmul(g.bank[0][:, t * E:(t + 1) * E], g.xnT[:, t * P:(t + 1) * P], gate_w,
                               start=(t == 0), stop=(t == TILES - 1), skip_group_check=True)
            mm.then_inc(logits, 1)
            pe.wait_ge(gated, 1)
            for t in range(TILES):
                mm = pe.transpose(g.bank[1 + t // TPG][0:E, (t % TPG) * P:(t % TPG + 1) * P], gates[:, t, :], g.ident[:, :])
            mm.then_inc(turned, 1)

        @block.scalar
        def _(act):
            act.wait_ge(exp_in, 1)
            if sigmoid_scores:
                act.activation(soft[:, :, :], raw[:, :, :], ACT.Exp, scale=-1.0).then_inc(exp_out, 1)
            else:
                act.activation(weight[:, 1, :], weight[:, 0, :], ACT.Exp).then_inc(exp_out, 1)
            act.wait_ge(split, 1)
            act.activation(gates3[32:64, :], part[:, :], ACT.Copy)

        @block.vector
        def _(dve):
            own = Chain(dve, own_sem)
            own.add(dve.memset(gates3[:, :], 0.0))
            own.add(dve.memset(gates_t[:, :], 1.0))
            own.add(dve.memset(part[:, :], 0.0))
            own.add(dve.memset(rest[:, :], 0.0))
            dve.wait_ge(logits, 1)
            lg = g.bank[0][:, 0:TILES * E].rearrange("p (n e) -> p n e", e=E)
            own.add(dve.tensor_copy(raw[:, :, :], lg))
            own.step(dve.tensor_tensor(ranked[:, :, :], lg, bias.unsqueeze(1).to_broadcast([P, TILES, E]), ALU.add))
            for t in range(TILES):
                own.add(dve.max(top[:, t, :], ranked[:, t, :]))
            own.settle()
            for t in range(TILES):
                own.add(dve.max_index(top_index[:, t, :], top[:, t, :], ranked[:, t, :]))
            own.settle()
            own.step(dve.tensor_copy(index[:, :, :], top_index[:, :, :]))
            dve.wait_ge(numbered, 1)
            own.add(dve.tensor_tensor(first[:, :, :], number[:, :, :], spread(index[:, :, 0], E), ALU.is_equal))
            own.add(dve.tensor_tensor(second[:, :, :], number[:, :, :], spread(index[:, :, 1], E), ALU.is_equal))
            own.settle()
            if sigmoid_scores:
                dve.sem_inc(exp_in, 1)
                own.step(dve.tensor_tensor(first[:, :, :], first[:, :, :], second[:, :, :], ALU.add))
                dve.wait_ge(exp_out, 1)
                own.step(dve.tensor_scalar(soft[:, :, :], soft[:, :, :], 1.0, None, ALU.add))
                own.step(dve.reciprocal(soft[:, :, :], soft[:, :, :]))
                own.step(dve.tensor_tensor(soft[:, :, :], soft[:, :, :], first[:, :, :], ALU.mult))
                own.step(dve.tensor_reduce(weight[:, 0, :], soft[:, :, :], AX.X, ALU.add))
                own.step(dve.tensor_scalar(weight[:, 1, :], weight[:, 0, :], 1e-10, None, ALU.add))
                own.step(dve.reciprocal(weight[:, 2, :], weight[:, 1, :]))
                own.step(dve.tensor_tensor(gates[:, :, :], soft[:, :, :], spread(weight[:, 2, :], E), ALU.mult))
            else:
                own.step(dve.tensor_tensor(weight[:, 0, :], top[:, :, 1], top[:, :, 0], ALU.subtract))
                dve.sem_inc(exp_in, 1)
                dve.wait_ge(exp_out, 1)
                own.step(dve.tensor_scalar(weight[:, 2, :], weight[:, 1, :], 1.0, None, ALU.add))
                own.step(dve.reciprocal(weight[:, 3, :], weight[:, 2, :]))
                own.step(dve.tensor_tensor(weight[:, 2, :], weight[:, 1, :], weight[:, 3, :], ALU.mult))
                own.add(dve.tensor_tensor(first[:, :, :], first[:, :, :], spread(weight[:, 3, :], E), ALU.mult))
                own.step(dve.tensor_tensor(second[:, :, :], second[:, :, :], spread(weight[:, 2, :], E), ALU.mult))
                own.step(dve.tensor_tensor(gates[:, :, :], first[:, :, :], second[:, :, :], ALU.add))
            dve.sem_inc(gated, 1)
            dve.wait_ge(turned, 1)
            for c in range(GROUPS):
                own.add(dve.tensor_copy(gates_t[0:E, tok(c)], g.bank[1 + c][0:E, :]))
            own.settle()
            own.step(dve.tensor_copy(gates3[0:E, :], gates_t[0:E, :]))
            own.step(dve.tensor_tensor(rest[0:E, :], gates_t[0:E, :], gates3[0:E, :], ALU.subtract))
            own.step(dve.tensor_copy(part[0:E, :], rest[0:E, :]))
            dve.tensor_tensor(gates3[64:96, :], rest[:, :], part[:, :], ALU.subtract).then_inc(split, 1)


def moe(nc, g, tag, d_in, experts, chunks, gate_of, biased, sigmoid_scores, domains):
    E = experts
    gated_mlp = "w1" in d_in
    SETS = max((gate_of(j) for j in range(chunks) if gate_of(j) is not None)) + 1
    HALF_SETS = SETS * 2 == E
    with ExitStack() as ctx:
        sem = ctx.enter_context(Signals(nc, tag))

        def sb(n, shape, dt=F32):
            return ctx.enter_context(nc.sbuf_tensor(f"{tag}_{n}", shape, dt))
        gate_w, gate_b = sb("gate_w", [P, E]), sb("gate_b", [P, E])
        w2 = sb("w2", [P, chunks, D])
        loads = [(gate_w[:, :], d_in["gate_w"]), (w2[:, :, :], d_in["w2"])]
        if "gate_b" in d_in:
            loads.append((gate_b[:, :], d_in["gate_b"]))
        if gated_mlp:
            w1, w3 = sb("w1", [P, chunks, P]), sb("w3", [P, chunks, P])
            loads += [(w1[:, :, :], d_in["w1"]), (w3[:, :, :], d_in["w3"])]
            b1, b3 = sb("b1", [P, chunks]), sb("b3", [P, chunks])
            if domains:
                dom = sb("dom", [P, E])
                loads.append((dom[:, :], d_in["dom"]))
            else:
                loads += [(b1[:, :], d_in["b1"]), (b3[:, :], d_in["b3"])]
        B_ROWS = 0
        if biased:
            B_ROWS = d_in["b2"].shape[0]
            b2 = sb("b2", [B_ROWS, D])
            loads.append((b2[:, :], d_in["b2"]))
        norm_and_turn(nc, g, tag + "_ln", loads)

        gates, gates_t = sb("gates", [P, TILES, E]), sb("gates_t", [32, N])
        gates3 = sb("gates3", [96, N], BF16)
        pick = sb("pick", [96, SETS, P], BF16)
        zero_b = sem("no_bias")
        if "gate_b" not in d_in:
            with nc.Block() as block:
                @block.gpsimd
                def _(pool):
                    pool.memset(gate_b[:, :], 0.0).then_inc(zero_b, 1)
        route(nc, g, tag + "_route", E, gates, gates_t, gates3, gate_w[:, :], gate_b[:, :], sigmoid_scores)

        silu = sb("silu", [P, 2, GROUP])
        prod = sb("prod", [P, 2, GROUP])
        gated = sb("gated", [P, 2, GROUP])
        gt_c = sb("gt_c", [32, GROUP])
        picked, hidden_ready, silu_ready, hidden_used = sem("picked"), sem("hidden_ready"), sem("silu_ready"), sem("hidden_used")
        spread_ready, spread_used, gated_ready, gated_used = sem("spread_ready"), sem("spread_used"), sem("gated_ready"), sem("gated_used")
        sum_ready, sum_used, gt_ready, gt_used = sem("sum_ready"), sem("sum_used"), sem("gt_ready"), sem("gt_used")
        dom_ready, dom_copied, dve_own, act_passed = sem("dom_ready"), sem("dom_copied"), sem("dve"), sem("act_passed")
        spread_at = {}
        for j in range(chunks):
            if gate_of(j) is not None:
                spread_at[j] = gate_of(j)
        last_use = {s: max(j for j in spread_at if spread_at[j] == s) for s in range(SETS)}
        assert SETS % 2 == 0 and chunks >= 2
        block = ctx.enter_context(nc.Block())

        @block.gpsimd
        def _(pool):
            pool.memset(pick[:, :, :], 0.0).then_inc(picked, 1)
            for k in range(3):
                pool.wait_ge(picked, k + 1)
                if HALF_SETS:
                    out = pick[:, :, :].rearrange("k s (h p) -> k s h p", h=2)
                    pattern = [[-2, SETS], [-1, 2], [0, P // 2]]
                else:
                    out, pattern = pick[:, :, :], [[-1, SETS], [0, P]]
                pool.affine_select(out=out, in_=out, compare_op=ALU.not_equal, fill=1.0, base=-32 * k,
                                   pattern=pattern, channel_multiplier=1).then_inc(picked, 1)

        @block.tensor
        def _(pe):
            if domains:
                for k, w in enumerate((w1, w3)):
                    for j in range(chunks):
                        e = gate_of(j)
                        mm = pe.matmul(g.bank[7][:, k * chunks + j:k * chunks + j + 1], w[:, j, :], dom[:, e:e + 1],
                                       start=(j == 0 and k == 0), stop=(j == chunks - 1 and k == 1), skip_group_check=True)
                mm.then_inc(dom_ready, 1)
            pe.wait_ge(picked, 4)
            with pe.Fori(0, GROUPS) as c:
                def add_chunk(j):
                    pe.wait_ge(gated_ready, c * chunks + (j + 1))
                    if j == 0:
                        pe.wait_ge(sum_used, c + 1)
                    for i in range(TPG):
                        mm = pe.matmul(g.bank[6][:, i * P:(i + 1) * P], gated[:, j % 2, i * P:(i + 1) * P],
                                       w2[:, j, :], start=(j == 0 and i == 0),
                                       stop=(not biased and j == chunks - 1), skip_group_check=True)
                    mm.then_inc(gated_used, 1)
                for j in range(chunks):
                    b = j % 2
                    if j in spread_at and (j == 0 or spread_at[j] != spread_at.get(j - 1)):
                        s = spread_at[j]
                        pe.wait_ge(spread_used, c * SETS + (s + 1))
                        pe.matmul(g.bank[4 + s % 2][:, :], pick[:, s, :], gates3[:, bass.ts(c, GROUP)],
                                  start=True, stop=True).then_inc(spread_ready, 1)
                    if gated_mlp:
                        pe.wait_ge(hidden_used, c * chunks + (j + 1))
                        pe.matmul(g.bank[b][:, :], w1[:, j, :], g.xnT[:, bass.ts(c, GROUP)], start=True, stop=True)
                        pe.matmul(g.bank[2 + b][:, :], w3[:, j, :], g.xnT[:, bass.ts(c, GROUP)],
                                  start=True, stop=True).then_inc(hidden_ready, 1)
                    if j >= 1:
                        add_chunk(j - 1)
                add_chunk(chunks - 1)
                if biased:
                    pe.wait_ge(gt_ready, c + 1)
                    for i in range(TPG):
                        mm = pe.matmul(g.bank[6][:, i * P:(i + 1) * P], gt_c[0:B_ROWS, i * P:(i + 1) * P], b2[:, :],
                                       start=False, stop=True, skip_group_check=True)
                    mm.then_inc(sum_ready, 1)
                else:
                    pe.wait_ge(gated_used, c * chunks + (chunks + 2))
                    pe.sem_inc(sum_ready, 1)

        @block.scalar
        def _(act):
            if domains:
                act.wait_ge(dom_ready, 1)
                act.activation(b1[:, :], g.bank[7][:, 0:chunks], ACT.Copy).then_inc(dom_copied, 1)
                act.activation(b3[:, :], g.bank[7][:, chunks:2 * chunks], ACT.Copy).then_inc(dom_copied, 1)
                act.wait_ge(dom_copied, 2)
            with act.Fori(0, GROUPS) as c:
                if biased:
                    wait_apart(act, gt_used, c + 1, act_passed)
                    act.activation(gt_c[:, :], gates_t[:, bass.ts(c, GROUP)], ACT.Copy).then_inc(gt_ready, 1)
                if gated_mlp:
                    for j in range(chunks):
                        act.wait_ge(hidden_used, c * chunks + (j + 1))
                        act.wait_ge(hidden_ready, c * chunks + (j + 1))
                        act.activation(silu[:, j % 2, :], g.bank[j % 2][:, :], ACT.Silu,
                                       bias=b1[:, j:j + 1]).then_inc(silu_ready, 1)

        @block.vector
        def _(dve):
            for free, n in ((spread_used, 2), (hidden_used, 2), (gated_used, 2), (sum_used, 1), (gt_used, 1)):
                dve.sem_inc(free, n)
            if domains:
                dve.wait_ge(dom_copied, 2)
            with dve.Fori(0, GROUPS) as c:
                for j in range(chunks):
                    b = j % 2
                    if gated_mlp:
                        dve.wait_ge(silu_ready, c * chunks + (j + 1))
                        if j >= 2:
                            dve.wait_ge(gated_ready, c * chunks + (j - 1))
                        if j not in spread_at:
                            dve.wait_ge(gated_used, c * chunks + (j + 1))
                        source = prod[:, b, :] if j in spread_at else gated[:, b, :]
                        dve.scalar_tensor_tensor(out=source, in0=g.bank[2 + b][:, :], scalar=b3[:, j:j + 1],
                                                 in1=silu[:, b, :], op0=ALU.add, op1=ALU.mult).then_inc(hidden_used, 1)
                        dve.wait_ge(hidden_used, c * chunks + (j + 3))
                    else:
                        source = g.xnT[:, bass.ts(c, GROUP)]
                    if j in spread_at:
                        s = spread_at[j]
                        dve.wait_ge(spread_ready, c * SETS + (s + 1))
                        dve.wait_ge(gated_used, c * chunks + (j + 1))
                        dve.tensor_tensor(gated[:, b, :], source, g.bank[4 + s % 2][:, :], ALU.mult).then_inc(gated_ready, 1)
                        if last_use[s] == j:
                            dve.wait_ge(gated_ready, c * chunks + (j + 1))
                            dve.sem_inc(spread_used, 1)
                    else:
                        dve.sem_inc(gated_ready, 1)
                dve.wait_ge(sum_ready, c + 1)
                x_c = g.x[:, bass.ts(c, TPG), :]
                dve.tensor_tensor(x_c, x_c, g.bank[6][:, :].rearrange("p (n d) -> p n d", d=D), ALU.add).then_inc(sum_used, 1)
                if biased:
                    dve.sem_inc(gt_used, 1)


def two_pi_parts():
    parts, rest = [], 2 * np.pi
    for bits in (8, 11, 24):
        unit = 2.0 ** (np.floor(np.log2(rest)) + 1 - bits)
        parts.append(float(np.floor(rest / unit) * unit))
        rest -= parts[-1]
    return parts


def rotor_memory(nc, g, d_in):
    TWO_PI = two_pi_parts()
    ROUND = 1.5 * 2.0 ** 23
    PI_DOWN = 3.1415925
    with ExitStack() as ctx:
        sem = ctx.enter_context(Signals(nc, "rotor"))

        def sb(n, shape, dt=F32):
            return ctx.enter_context(nc.sbuf_tensor(f"rotor_{n}", shape, dt))
        w_v, w_o, freqs = sb("w_v", [P, P]), sb("w_o", [P, P]), sb("freqs", [P, 1])
        norm_and_turn(nc, g, "rotor_ln", [(w_v[:, :], d_in["w_v"]), (w_o[:, :], d_in["w_o"]), (freqs[:, :], d_in["freqs"])])
        time, theta = sb("time", [P, T]), sb("theta", [P, T])
        turns, angle = sb("turns", [P, 2, T]), sb("angle", [P, 2, T])
        table = sb("table", [P, 2, T])
        keep = sb("keep", [P, SPG, T])
        term, total = sb("term", [P, 2, N]), sb("total", [P, 2, N])
        found = sb("found", [P, N])
        timed, angles, tables = sem("timed"), sem("angles"), sem("tables")
        v_ready, found_ready, out_ready, dve_own = sem("v_ready"), sem("found_ready"), sem("out_ready"), sem("dve")
        block = ctx.enter_context(nc.Block())

        @block.gpsimd
        def _(pool):
            pool.iota(time[:, :], pattern=[[1, T]], base=0, channel_multiplier=0,
                      allow_small_or_imprecise_dtypes=True).then_inc(timed, 1)

        @block.scalar
        def _(act):
            act.wait_ge(angles, 1)
            act.activation(table[:, :, :], angle[:, :, :], ACT.Sin).then_inc(tables, 1)

        @block.tensor
        def _(pe):
            pe.wait_ge(g.weights, g.weights_due)
            for c in range(GROUPS):
                pe.matmul(g.bank[c][:, :], w_v[:, :], g.xnT[:, tok(c)], start=True, stop=True).then_inc(v_ready, 1)
            for c in range(GROUPS):
                pe.wait_ge(found_ready, c + 1)
                for i in range(TPG):
                    mm = pe.matmul(g.bank[4 + c][:, i * P:(i + 1) * P], found[:, c * GROUP + i * P:c * GROUP + (i + 1) * P],
                                   w_o[:, :], start=True, stop=True)
                mm.then_inc(out_ready, 1)

        @block.vector
        def _(dve):
            own = Chain(dve, dve_own)
            own.step(dve.memset(keep[:, :, :], 1.0))
            own.add(dve.memset(keep[:, :, 0:1], 0.0))
            dve.wait_ge(timed, 1)
            dve.wait_ge(g.weights, g.weights_due)
            own.step(dve.tensor_scalar(theta[:, :], time[:, :], freqs[:, 0:1], None, ALU.mult))
            for q in range(2):
                own.add(dve.tensor_scalar(turns[:, q, :], theta[:, :], 1 / (2 * np.pi), 0.25 * q, ALU.mult, ALU.add))
            own.settle()
            own.step(dve.tensor_scalar(turns[:, :, :], turns[:, :, :], ROUND, None, ALU.add))
            own.step(dve.tensor_scalar(turns[:, :, :], turns[:, :, :], ROUND, None, ALU.subtract))
            theta2 = theta[:, :].unsqueeze(1).to_broadcast([P, 2, T])
            for k, part in enumerate(TWO_PI):
                own.step(dve.scalar_tensor_tensor(out=angle[:, :, :], in0=turns[:, :, :], scalar=-part,
                                                  in1=theta2 if k == 0 else angle[:, :, :], op0=ALU.mult, op1=ALU.add))
            own.step(dve.tensor_scalar(angle[:, 1, :], angle[:, 1, :], np.pi / 2, None, ALU.add))
            dve.tensor_scalar(angle[:, :, :], angle[:, :, :], PI_DOWN, -PI_DOWN, ALU.min, ALU.max).then_inc(angles, 1)
            dve.wait_ge(tables, 1)
            for c in range(GROUPS):
                dve.wait_ge(v_ready, c + 1)
                v = g.bank[c][:, :].rearrange("p (b t) -> p b t", t=T)

                def per_seq(buf, q):
                    return buf[:, q, tok(c)].rearrange("p (b t) -> p b t", t=T)
                tables2 = [table[:, q, :].unsqueeze(1).to_broadcast([P, SPG, T]) for q in range(2)]
                for q in range(2):
                    own.add(dve.tensor_tensor(per_seq(term, q), v, tables2[q], ALU.mult))
                for q in range(2):
                    own.settle(behind=1)
                    own.add(dve.tensor_tensor_scan(total[:, q, tok(c)], keep[:, :, :].rearrange("p b t -> p (b t)"),
                                                   term[:, q, tok(c)], 0.0, ALU.mult, ALU.add))
                for q in range(2):
                    own.settle(behind=1)
                    own.add(dve.tensor_tensor(per_seq(term, q), per_seq(total, q), tables2[q], ALU.mult))
                own.settle()
                dve.tensor_tensor(found[:, tok(c)], term[:, 0, tok(c)], term[:, 1, tok(c)], ALU.add).then_inc(found_ready, 1)
            for c in range(GROUPS):
                dve.wait_ge(out_ready, c + 1)
                x_c = g.x[:, TPG * c:TPG * (c + 1), :]
                dve.tensor_tensor(x_c, x_c, g.bank[4 + c][:, :].rearrange("p (n d) -> p n d", d=D), ALU.add)


def delta_rule(nc, g, d_in):
    HEADS, TAPS, C, QUAD, LEVELS, DUO = 8, 4, P, 4, 7, 2
    QUADS = TILES // QUAD
    with ExitStack() as ctx:
        sem = ctx.enter_context(Signals(nc, "delta"))

        def sb(n, shape, dt=F32):
            return ctx.enter_context(nc.sbuf_tensor(f"delta_{n}", shape, dt))
        w_qkv, w_z, w_o = sb("w_qkv", [P, HEADS, 3, P]), sb("w_z", [P, HEADS, P]), sb("w_o", [P, HEADS, D])
        taps = sb("taps", [P, HEADS, 3, TAPS])
        w_ab, ab_bias = sb("w_ab", [P, 2 * HEADS]), sb("ab_bias", [P, 2 * HEADS])
        a_log, norm_w = sb("a_log", [P, HEADS]), sb("norm_w", [P, 1])
        norm_and_turn(nc, g, "delta_ln", [
            (w_ab[:, :], d_in["w_ab"]), (ab_bias[:, :], d_in["ab_bias"]), (a_log[:, :], d_in["a_log"]),
            (norm_w[:, :], d_in["norm_w"]), (taps[:, :, :, :], d_in["taps"]), (w_qkv[:, :, :, :], d_in["w_qkv"]),
            (w_z[:, :, :], d_in["w_z"]), (w_o[:, :, :], d_in["w_o"])])
        beta = sb("beta", [P, TILES, HEADS])
        alpha3 = sb("alpha3", [96, N], BF16)

        with ExitStack() as inner:
            sem1 = inner.enter_context(Signals(nc, "delta_ab"))

            def sb1(n, shape, dt=F32):
                return inner.enter_context(nc.sbuf_tensor(f"delta_ab_{n}", shape, dt))
            ab, soft = sb1("ab", [P, TILES, 2 * HEADS]), sb1("soft", [P, TILES, HEADS])
            rate, alpha = sb1("rate", [P, HEADS]), sb1("alpha", [P, TILES, HEADS])
            sig = sb1("sig", [P, TILES, HEADS])
            alpha_t, rest, part = sb1("alpha_t", [32, N]), sb1("rest", [32, N]), sb1("part", [32, N], BF16)
            projected, biased, softened, rated = sem1("projected"), sem1("biased"), sem1("softened"), sem1("rated")
            alpha_ready, turned, split = sem1("alpha_ready"), sem1("turned"), sem1("split")
            act_own, dve_own = sem1("act"), sem1("dve")
            block = inner.enter_context(nc.Block())

            @block.tensor
            def _(pe):
                pe.wait_ge(g.weights, g.weights_due)
                for t in range(TILES):
                    mm = pe.matmul(g.bank[0][:, t * 16:(t + 1) * 16], g.xnT[:, t * P:(t + 1) * P], w_ab[:, :],
                                   start=(t == 0), stop=(t == TILES - 1), skip_group_check=True)
                mm.then_inc(projected, 1)
                pe.wait_ge(alpha_ready, 1)
                for t in range(TILES):
                    mm = pe.transpose(g.bank[1 + t // TPG][0:HEADS, (t % TPG) * P:(t % TPG + 1) * P], alpha[:, t, :],
                                      g.ident[:, :])
                mm.then_inc(turned, 1)

            @block.scalar
            def _(act):
                own = Chain(act, act_own)
                act.preload_act_table_set(LN_EXP)
                act.wait_ge(g.weights, g.weights_due)
                own.add(act.activation(rate[:, :], a_log[:, :], ACT.Exp))
                act.wait_ge(biased, 1)
                own.add(act.activation(sig[:, :, :], ab[:, :, HEADS:], ACT.Exp, scale=-1.0))
                own.step(act.activation(soft[:, :, :], ab[:, :, 0:HEADS], ACT.Abs))
                own.step(act.activation(soft[:, :, :], soft[:, :, :], ACT.Exp, scale=-1.0))
                act.activation(soft[:, :, :], soft[:, :, :], ACT.Ln, bias=g.one[:, 0:1]).then_inc(softened, 1)
                act.wait_ge(rated, 1)
                act.activation(alpha[:, :, :], soft[:, :, :], ACT.Exp, scale=-1.0).then_inc(alpha_ready, 1)
                act.wait_ge(split, 1)
                act.activation(alpha3[32:64, :], part[:, :], ACT.Copy)

            @block.vector
            def _(dve):
                own = Chain(dve, dve_own)
                own.add(dve.memset(alpha_t[:, :], 0.0))
                dve.wait_ge(projected, 1)
                dve.wait_ge(g.weights, g.weights_due)
                dve.tensor_tensor(ab[:, :, :], g.bank[0][:, 0:16 * TILES].rearrange("p (n e) -> p n e", e=16),
                                  ab_bias[:, :].unsqueeze(1).to_broadcast([P, TILES, 16]), ALU.add).then_inc(biased, 1)
                dve.wait_ge(softened, 1)
                own.step(dve.scalar_tensor_tensor(out=soft[:, :, :], in0=ab[:, :, 0:HEADS], scalar=0.0,
                                                  in1=soft[:, :, :], op0=ALU.max, op1=ALU.add))
                dve.tensor_tensor(soft[:, :, :], soft[:, :, :], rate[:, :].unsqueeze(1).to_broadcast([P, TILES, HEADS]),
                                  ALU.mult).then_inc(rated, 1)
                own.step(dve.tensor_scalar(sig[:, :, :], sig[:, :, :], 1.0, None, ALU.add))
                own.add(dve.reciprocal(beta[:, :, :], sig[:, :, :]))
                dve.wait_ge(turned, 1)
                for c in range(GROUPS):
                    own.add(dve.tensor_copy(alpha_t[0:HEADS, tok(c)], g.bank[1 + c][0:HEADS, :]))
                own.settle()
                own.step(dve.tensor_copy(alpha3[0:32, :], alpha_t[:, :]))
                own.step(dve.tensor_tensor(rest[:, :], alpha_t[:, :], alpha3[0:32, :], ALU.subtract))
                own.step(dve.tensor_copy(part[:, :], rest[:, :]))
                dve.tensor_tensor(alpha3[64:96, :], rest[:, :], part[:, :], ALU.subtract).then_inc(split, 1)

        pick = sb("pick", [96, HEADS, P], BF16)
        pick_h = sb("pick_h", [96, P], BF16)
        w_h, wz_h, wo_h = sb("w_h", [P, 3, P]), sb("wz_h", [P, P]), sb("wo_h", [P, D])
        taps_h, beta_h = sb("taps_h", [P, 3, TAPS]), sb("beta_h", [P, TILES])
        joint = sb("joint", [P, LEVELS, C])
        pad = sb("pad", [P, 3, BATCH, T + TAPS - 1])
        qkv = sb("qkv", [P, 3, N])
        alpha_in = sb("alpha_in", [P, TILES, C])
        alpha_first = sb("alpha_first", [P, TILES, C])
        grow = sb("grow", [P, TILES, C])
        kq_g = sb("kq_g", [P, 2, BATCH, C])
        diag, db = sb("diag", [P, DUO, QUAD, C]), sb("db", [P, DUO, QUAD, C])
        lt, at = sb("lt", [P, DUO, QUAD, C]), sb("at", [P, DUO, QUAD, C])
        lt_n = sb("lt_n", [P, DUO, QUAD, C])
        xi, xt, px = sb("xi", [P, DUO, QUAD, C]), sb("xt", [P, DUO, QUAD, C]), sb("px", [P, DUO, QUAD, C])
        v_tok, k_tok = sb("v_tok", [P, DUO, QUAD, C]), sb("k_tok", [P, DUO, 2, C])
        w_sol, s_one = sb("w_sol", [P, DUO, QUAD, C]), sb("s_one", [P, DUO, 2, C])
        sz, o_sq = sb("sz", [P, DUO, QUAD, C]), sb("o_sq", [P, DUO, QUAD, C])
        o_n, o_t = sb("o_n", [P, DUO, QUAD, C]), sb("o_t", [P, DUO, QUAD, C])
        stat = sb("stat", [P, DUO, 3, QUAD])
        eps_o = sb("eps_o", [P, 1])
        picked, masks = sem("picked"), sem("masks")
        staged, pe_head, dve_head, act_head = sem("staged"), sem("pe_head"), sem("dve_head"), sem("act_head")
        pads_zero = sem("pads_zero")
        proj_ready, proj_used, conv_ready = sem("proj_ready"), sem("proj_used"), sem("conv_ready")
        a_ready, a_copied, kq_ready = sem("a_ready"), sem("a_copied"), sem("kq_ready")
        scores_ready, lt_ready, at_ready = sem("scores_ready"), sem("lt_ready"), sem("at_ready")
        masked, masked_used = sem("masked"), sem("masked_used")
        p_ready, p_copied, xp_ready, x_ready, xpt_ready, xt_ready = (
            sem("p_ready"), sem("p_copied"), sem("xp_ready"), sem("x_ready"), sem("xpt_ready"), sem("xt_ready"))
        turned, tok_ready = sem("turned"), sem("tok_ready")
        ks_ready, rhs_ready = sem("ks_ready"), sem("rhs_ready")
        w_ready, w_copied, s_ready, s_copied = sem("w_ready"), sem("w_copied"), sem("s_ready"), sem("s_copied")
        z_ready, sz_ready, o_ready = sem("z_ready"), sem("sz_ready"), sem("o_ready")
        sq_ready, var_ready, rstd_ready, on_ready = sem("sq_ready"), sem("var_ready"), sem("rstd_ready"), sem("on_ready")
        ot_ready, ot_copied, out_ready, out_added = sem("ot_ready"), sem("ot_copied"), sem("out_ready"), sem("out_added")
        pool_own, dve_own, act_own = sem("pool"), sem("dve"), sem("act")
        HALVES = QUADS // DUO
        R = HALVES * DUO
        block = ctx.enter_context(nc.Block())

        def flat(buf, d):
            return buf[:, d, :, :].rearrange("p a c -> p (a c)")

        @block.gpsimd
        def _(pool):
            own = Chain(pool, pool_own)
            own.step(pool.memset(pick[:, :, :], 0.0))
            for k in range(3):
                own.step(pool.affine_select(out=pick[:, :, :], in_=pick[:, :, :], compare_op=ALU.not_equal, fill=1.0,
                                            base=-32 * k, pattern=[[-1, HEADS], [0, P]], channel_multiplier=1))
            own.step(pool.memset(joint[:, :, :], 0.0))
            for lv in range(LEVELS):
                n = 1 << lv
                view = joint[:, lv, :].rearrange("p (a two r) -> p a two r", two=2, r=n)[:, :, 1, :]
                own.step(pool.memset(view, 1.0))
                own.step(pool.affine_select(out=view, in_=view, compare_op=ALU.is_ge, fill=0.0, base=0,
                                            pattern=[[-2 * n, C // (2 * n)], [0, n]], channel_multiplier=1))
                own.step(pool.affine_select(out=view, in_=view, compare_op=ALU.is_gt, fill=0.0, base=n,
                                            pattern=[[2 * n, C // (2 * n)], [0, n]], channel_multiplier=-1))
            SETUP = own.count
            PER_HEAD = 6
            with pool.Fori(0, HEADS) as h:
                own = Chain(pool, pool_own, h * PER_HEAD + SETUP)
                for done in (pe_head, dve_head, act_head):
                    pool.wait_ge(done, h + 1)
                own.add(pool.tensor_copy(w_h[:, :, :], w_qkv[:, bass.ts(h, 1), :, :].rearrange("p a m c -> p (a m) c")))
                own.add(pool.tensor_copy(wz_h[:, :], w_z[:, bass.ts(h, 1), :].rearrange("p a c -> p (a c)")))
                own.add(pool.tensor_copy(wo_h[:, :], w_o[:, bass.ts(h, 1), :].rearrange("p a c -> p (a c)")))
                own.add(pool.tensor_copy(taps_h[:, :, :], taps[:, bass.ts(h, 1), :, :].rearrange("p a m c -> p (a m) c")))
                own.add(pool.tensor_copy(beta_h[:, :], beta[:, :, bass.ts(h, 1)].rearrange("p a c -> p (a c)")))
                own.step(pool.tensor_copy(pick_h[:, :], pick[:, bass.ts(h, 1), :].rearrange("p a c -> p (a c)")))
                pool.sem_inc(staged, 1)
                for half in range(HALVES):
                    for lv in range(LEVELS):
                        for d in range(DUO):
                            n = DUO * half + d
                            if lv == 0:
                                pool.wait_ge(lt_ready, h * R + (n + 1))
                            pool.wait_ge(masked_used, h * (R * LEVELS) + (half * DUO * LEVELS + lv * DUO + d + 1))
                            pool.tensor_tensor(lt_n[:, d, :, :], lt[:, d, :, :],
                                               joint[:, lv, :].unsqueeze(1).to_broadcast([P, QUAD, C]),
                                               ALU.mult).then_inc(masked, 1)

        @block.tensor
        def _(pe):
            def chunks(bank, lhs, rhs, signal, which=range(4), start=None, stop=True):
                for i in which:
                    mm = pe.matmul(bank[:, i * C:(i + 1) * C], lhs(i), rhs(i), start=True if start is None else start(i),
                                   stop=stop)
                mm.then_inc(signal, 1)

            with pe.Fori(0, HEADS) as h:
                pe.wait_ge(staged, h + 1)
                for i in range(3 * GROUPS):
                    m, c = divmod(i, GROUPS)
                    if i >= 8:
                        pe.wait_ge(proj_used, h * (3 * GROUPS) + (i - 7))
                    pe.matmul(g.bank[i % 8][:, :], w_h[:, m, :], g.xnT[:, tok(c)], start=True, stop=True).then_inc(proj_ready, 1)
                for c in range(GROUPS):
                    pe.wait_ge(proj_used, h * (3 * GROUPS) + (5 + c))
                    pe.matmul(g.bank[4 + c][:, :], pick_h[:, :], alpha3[:, tok(c)], start=True, stop=True).then_inc(a_ready, 1)
                pe.wait_ge(conv_ready, h * 3 + 3)
                pe.wait_ge(kq_ready, h + 1)
                pe.wait_ge(proj_used, h * (3 * GROUPS) + 3 * GROUPS)
                pe.wait_ge(a_copied, h * GROUPS + GROUPS)
                for half in range(HALVES):
                    for d in range(DUO):
                        at0 = (DUO * half + d) * GROUP

                        def seg(m, i, at0=at0):
                            return qkv[:, m, at0 + i * C:at0 + (i + 1) * C]
                        if half:
                            pe.wait_ge(out_added, h * R + DUO * (half - 1) + d + 1)
                        chunks(g.bank[d], lambda i: seg(1, i), lambda i: seg(1, i), scores_ready)
                        chunks(g.bank[2 + d], lambda i: seg(1, i), lambda i: seg(0, i), scores_ready)
                        for i in range(4):
                            mm = pe.transpose(g.bank[4 + d][:, i * C:(i + 1) * C], seg(2, i), g.ident[:, :])
                        mm.then_inc(turned, 1)
                        for i in (0, 2):
                            mm = pe.transpose(g.bank[6 + d][:, (i // 2) * C:(i // 2 + 1) * C], seg(1, i), g.ident[:, :])
                        mm.then_inc(turned, 1)
                    for lv in range(LEVELS):
                        for d in range(DUO):
                            n = R * LEVELS
                            it = half * DUO * LEVELS + lv * DUO + d
                            pe.wait_ge(masked, h * n + (it + 1))
                            if lv == 0:
                                pe.wait_ge(at_ready, h * R + (DUO * half + d + 1))
                                for i in range(4):
                                    mm = pe.transpose(g.bank[d][:, i * C:(i + 1) * C], lt_n[:, d, i, :], g.ident[:, :])
                                mm.then_inc(p_ready, 1)
                            else:
                                pe.wait_ge(x_ready, h * (R * (LEVELS - 1)) + (half * DUO * (LEVELS - 1) + (lv - 1) * DUO + d + 1))
                                chunks(g.bank[d], lambda i, d=d: lt_n[:, d, i, :], lambda i, d=d: xi[:, d, i, :], p_ready)
                        if lv == 0:
                            continue
                        for d in range(DUO):
                            it = half * DUO * LEVELS + lv * DUO + d
                            pe.wait_ge(p_copied, h * (R * LEVELS) + (it + 1))
                            pe.wait_ge(xt_ready, h * (R * LEVELS) + (it - DUO + 1))
                            if lv < LEVELS - 1:
                                chunks(g.bank[2 + d], lambda i, d=d: xt[:, d, i, :], lambda i, d=d: px[:, d, i, :], xp_ready)
                            if lv == 1:
                                pe.wait_ge(tok_ready, h * (2 * R) + (2 * (DUO * half + d) + 2))
                            chunks(g.bank[4 + d], lambda i, d=d: px[:, d, i, :], lambda i, d=d: xt[:, d, i, :], xpt_ready)
                    for d in range(DUO):
                        it = half * DUO * LEVELS + (LEVELS - 1) * DUO + d
                        pe.wait_ge(xt_ready, h * (R * LEVELS) + (it + 1))
                        chunks(g.bank[d], lambda i, d=d: xt[:, d, i, :], lambda i, d=d: v_tok[:, d, i, :], w_ready, (0, 2))
                    for d in range(DUO):
                        n = DUO * half + d
                        pe.wait_ge(w_copied, h * (2 * R) + (2 * DUO * half + d + 1))
                        chunks(g.bank[2 + d], lambda i, d=d: k_tok[:, d, i, :], lambda i, d=d: w_sol[:, d, 2 * i, :], s_ready, (0, 1))
                    for d in range(DUO):
                        n = DUO * half + d
                        pe.wait_ge(s_copied, h * R + (n + 1))
                        chunks(g.bank[4 + d], lambda i, n=n: kq_g[:, 1, 2 * n + i, :], lambda i, d=d: s_one[:, d, i, :],
                               ks_ready, (0, 1))
                    for d in range(DUO):
                        n = DUO * half + d
                        chunks(g.bank[6 + d], lambda i, n=n: g.xnT[:, (4 * n + i) * P:(4 * n + i + 1) * P], lambda i: wz_h[:, :], z_ready)
                    for d in range(DUO):
                        n = DUO * half + d
                        pe.wait_ge(rhs_ready, h * R + (n + 1))
                        chunks(g.bank[d], lambda i, d=d: xt[:, d, i, :], lambda i, d=d: v_tok[:, d, i, :], w_ready, (1, 3))
                    for d in range(DUO):
                        n = DUO * half + d
                        pe.wait_ge(w_copied, h * (2 * R) + (2 * DUO * half + DUO + d + 1))
                        for i in range(4):
                            mm = pe.matmul(g.bank[2 + d][:, i * C:(i + 1) * C], at[:, d, i, :], w_sol[:, d, i, :],
                                           start=True, stop=(i % 2 == 0))
                            if i % 2:
                                mm = pe.matmul(g.bank[2 + d][:, i * C:(i + 1) * C], kq_g[:, 0, 2 * n + i // 2, :],
                                               s_one[:, d, i // 2, :], start=False, stop=True)
                        mm.then_inc(o_ready, 1)
                    for d in range(DUO):
                        n = DUO * half + d
                        pe.wait_ge(on_ready, h * R + (n + 1))
                        for i in range(4):
                            mm = pe.transpose(g.bank[4 + d][:, i * C:(i + 1) * C], o_n[:, d, i, :], g.ident[:, :])
                        mm.then_inc(ot_ready, 1)
                    for d in range(DUO):
                        n = DUO * half + d
                        pe.wait_ge(ot_copied, h * R + (n + 1))
                        chunks(g.bank[d], lambda i, d=d: o_t[:, d, i, :], lambda i: wo_h[:, :], out_ready)
                pe.wait_ge(out_added, h * R + R)
                pe.sem_inc(pe_head, 1)

        @block.scalar
        def _(act):
            act.wait_ge(pads_zero, 1)
            act.sem_inc(act_head, 1)
            with act.Fori(0, HEADS) as h:
                for i in range(3 * GROUPS):
                    m, c = divmod(i, GROUPS)
                    act.wait_ge(proj_ready, h * (3 * GROUPS) + (i + 1))
                    act.activation(pad[:, m, SPG * c:SPG * (c + 1), TAPS - 1:],
                                   g.bank[i % 8][:, :].rearrange("p (b t) -> p b t", t=T), ACT.Copy).then_inc(proj_used, 1)
                for c in range(GROUPS):
                    act.wait_ge(a_ready, h * GROUPS + (c + 1))
                    a = g.bank[4 + c][:, :].rearrange("p (n c) -> p n c", c=C)
                    t = slice(TPG * c, TPG * (c + 1))
                    act.activation(alpha_in[:, t, 1:], a[:, :, 1:], ACT.Copy)
                    act.activation(alpha_first[:, t, 0:1], a[:, :, 0:1], ACT.Copy).then_inc(a_copied, 1)
                for half in range(HALVES):
                    for d in range(DUO):
                        n = DUO * half + d
                        act.wait_ge(turned, h * (2 * R) + (2 * n + 2))
                        act.activation(flat(v_tok, d), g.bank[4 + d][:, :], ACT.Copy).then_inc(tok_ready, 1)
                        act.wait_ge(lt_ready, h * R + (n + 1))
                        for i in range(2):
                            ins = act.activation(k_tok[:, d, i, :], g.bank[6 + d][:, i * C:(i + 1) * C], ACT.Copy,
                                                 scale=db[:, d, 2 * i, C - 1:C])
                        ins.then_inc(tok_ready, 1)
                    for lv in range(LEVELS):
                        for d in range(DUO):
                            it = half * DUO * LEVELS + lv * DUO + d
                            act.wait_ge(p_ready, h * (R * LEVELS) + (it + 1))
                            act.activation(flat(px, d), g.bank[d][:, :], ACT.Copy).then_inc(p_copied, 1)
                    for d in range(DUO):
                        act.wait_ge(w_ready, h * (2 * R) + (2 * DUO * half + d + 1))
                        act.activation(w_sol[:, d, 0:4:2, :], g.bank[d][:, :].rearrange("p (a c) -> p a c", c=C)[:, 0:4:2, :],
                                       ACT.Copy).then_inc(w_copied, 1)
                    for d in range(DUO):
                        n = DUO * half + d
                        act.wait_ge(s_ready, h * R + (n + 1))
                        act.activation(flat(s_one, d), g.bank[2 + d][:, 0:2 * C], ACT.Copy).then_inc(s_copied, 1)
                    for d in range(DUO):
                        act.wait_ge(z_ready, h * R + (DUO * half + d + 1))
                        act.activation(flat(sz, d), g.bank[6 + d][:, :], ACT.Silu).then_inc(sz_ready, 1)
                    act.preload_act_table_set(LN_EXP)
                    for d in range(DUO):
                        act.wait_ge(w_ready, h * (2 * R) + (2 * DUO * half + DUO + d + 1))
                        act.activation(w_sol[:, d, 1:4:2, :], g.bank[d][:, :].rearrange("p (a c) -> p a c", c=C)[:, 1:4:2, :],
                                       ACT.Copy).then_inc(w_copied, 1)
                    for d in range(DUO):
                        act.wait_ge(o_ready, h * R + (DUO * half + d + 1))
                        act.activation(flat(o_sq, d), g.bank[2 + d][:, :], ACT.Square).then_inc(sq_ready, 1)
                    for d in range(DUO):
                        n = DUO * half + d
                        act.wait_ge(var_ready, h * R + (n + 1))
                        act.activation(stat[:, d, 1, :], stat[:, d, 0, :], ACT.Ln, bias=eps_o[:, 0:1], scale=1.0 / P).then_inc(act_own, 1)
                        act.wait_ge(act_own, h * R + (n + 1))
                        act.activation(stat[:, d, 2, :], stat[:, d, 1, :], ACT.Exp, scale=-0.5).then_inc(rstd_ready, 1)
                    for d in range(DUO):
                        act.wait_ge(ot_ready, h * R + (DUO * half + d + 1))
                        act.activation(flat(o_t, d), g.bank[4 + d][:, :], ACT.Copy, scale=norm_w[:, 0:1]).then_inc(ot_copied, 1)
                act.wait_ge(ot_copied, h * R + R)
                act.sem_inc(act_head, 1)

        @block.vector
        def _(dve):
            own = Chain(dve, dve_own)
            own.add(dve.memset(pad[:, :, :, 0:TAPS - 1], 0.0))
            own.add(dve.memset(alpha_in[:, :, 0:1], 0.0))
            own.add(dve.memset(alpha_first[:, :, :], 0.0))
            own.add(dve.memset(eps_o[:, :], 1e-6))
            own.settle()
            for free in (pads_zero, dve_head, pe_head):
                dve.sem_inc(free, 1)
            dve.sem_inc(masked_used, DUO)
            SETUP, PER_HEAD = own.count, 27
            with dve.Fori(0, HEADS) as h:
                own = Chain(dve, dve_own, h * PER_HEAD + SETUP)
                dve.wait_ge(staged, h + 1)
                for m in range(3):
                    dve.wait_ge(proj_used, h * (3 * GROUPS) + GROUPS * (m + 1))
                    conv = qkv[:, m, :].rearrange("p (b t) -> p b t", t=T)
                    own.step(dve.tensor_scalar(conv, pad[:, m, :, 0:T], taps_h[:, m, 0:1], None, ALU.mult))
                    for k in range(1, TAPS):
                        own.step(dve.scalar_tensor_tensor(out=conv, in0=pad[:, m, :, k:k + T], scalar=taps_h[:, m, k:k + 1],
                                                          in1=conv, op0=ALU.mult, op1=ALU.add))
                    dve.sem_inc(conv_ready, 1)
                dve.wait_ge(a_copied, h * GROUPS + GROUPS)
                own.step(dve.tensor_tensor_scan(grow[:, :, :].rearrange("p n c -> p (n c)"),
                                                alpha_in[:, :, :].rearrange("p n c -> p (n c)"),
                                                alpha_first[:, :, :].rearrange("p n c -> p (n c)"), 0.0, ALU.mult, ALU.add))
                for m in range(2):
                    own.add(dve.tensor_tensor(kq_g[:, m, :, :], qkv[:, m, :].rearrange("p (b n c) -> p b n c", n=2, c=C)[:, :, 1, :],
                                              grow[:, 1:TILES:2, :], ALU.mult))
                own.settle()
                dve.sem_inc(kq_ready, 1)
                for half in range(HALVES):
                    for d in range(DUO):
                        n = DUO * half + d
                        t = slice(QUAD * n, QUAD * (n + 1))
                        own.step(dve.tensor_tensor(diag[:, d, :, :], g.ident[:, :].unsqueeze(1).to_broadcast([P, QUAD, C]),
                                                   spread(beta_h[:, t], C), ALU.mult))
                        own.step(dve.tensor_tensor_scan(flat(db, d), alpha_in[:, t, :].rearrange("p n c -> p (n c)"),
                                                        flat(diag, d), 0.0, ALU.mult, ALU.add))
                        dve.wait_ge(scores_ready, h * (2 * R) + (2 * n + 2))
                        dve.tensor_tensor(flat(lt, d), flat(db, d), g.bank[d][:, :], ALU.mult).then_inc(lt_ready, 1)
                        dve.tensor_tensor(flat(at, d), flat(db, d), g.bank[2 + d][:, :], ALU.mult).then_inc(at_ready, 1)
                    for lv in range(LEVELS):
                        for d in range(DUO):
                            it = half * DUO * LEVELS + lv * DUO + d
                            xit = half * DUO * (LEVELS - 1) + lv * DUO + d
                            if lv == 0:
                                ident4 = g.ident[:, :].unsqueeze(1).to_broadcast([P, QUAD, C])
                                dve.wait_ge(p_copied, h * (R * LEVELS) + (it + 1))
                                dve.tensor_tensor(xi[:, d, :, :], ident4, px[:, d, :, :], ALU.subtract).then_inc(x_ready, 1)
                                dve.tensor_tensor(xt[:, d, :, :], ident4, lt_n[:, d, :, :], ALU.subtract).then_inc(xt_ready, 1)
                            else:
                                if lv < LEVELS - 1:
                                    dve.wait_ge(xp_ready, h * (R * (LEVELS - 2)) + (half * DUO * (LEVELS - 2) + (lv - 1) * DUO + d + 1))
                                    dve.wait_ge(x_ready, h * (R * (LEVELS - 1)) + (xit - DUO + 1))
                                    dve.tensor_tensor(flat(xi, d), flat(xi, d), g.bank[2 + d][:, :], ALU.subtract).then_inc(x_ready, 1)
                                dve.wait_ge(xpt_ready, h * (R * (LEVELS - 1)) + (half * DUO * (LEVELS - 1) + (lv - 1) * DUO + d + 1))
                                dve.wait_ge(xt_ready, h * (R * LEVELS) + (it - DUO + 1))
                                dve.tensor_tensor(flat(xt, d), flat(xt, d), g.bank[4 + d][:, :], ALU.subtract).then_inc(xt_ready, 1)
                            dve.wait_ge(xt_ready, h * (R * LEVELS) + (it + 1))
                            dve.sem_inc(masked_used, 1)
                    for d in range(DUO):
                        n = DUO * half + d
                        dve.wait_ge(ks_ready, h * R + (n + 1))
                        dve.tensor_tensor(v_tok[:, d, 1:4:2, :], v_tok[:, d, 1:4:2, :],
                                          g.bank[4 + d][:, 0:2 * C].rearrange("p (a c) -> p a c", c=C), ALU.subtract).then_inc(rhs_ready, 1)
                    for d in range(DUO):
                        n = DUO * half + d
                        dve.wait_ge(sq_ready, h * R + (n + 1))
                        dve.tensor_reduce(stat[:, d, 0, :], o_sq[:, d, :, :], AX.X, ALU.add).then_inc(var_ready, 1)
                    for d in range(DUO):
                        n = DUO * half + d
                        dve.wait_ge(rstd_ready, h * R + (n + 1))
                        own.step(dve.tensor_tensor(o_n[:, d, :, :], g.bank[2 + d][:, :].rearrange("p (a c) -> p a c", c=C),
                                                   spread(stat[:, d, 2, :], C), ALU.mult))
                        dve.wait_ge(sz_ready, h * R + (n + 1))
                        dve.tensor_tensor(flat(o_n, d), flat(o_n, d), flat(sz, d), ALU.mult).then_inc(on_ready, 1)
                    for d in range(DUO):
                        n = DUO * half + d
                        dve.wait_ge(out_ready, h * R + (n + 1))
                        x_q = g.x[:, QUAD * n:QUAD * (n + 1), :]
                        dve.tensor_tensor(x_q, x_q, g.bank[d][:, :].rearrange("p (n d) -> p n d", d=D), ALU.add).then_inc(out_added, 1)
                dve.wait_ge(out_added, h * R + R)
                dve.sem_inc(dve_head, 1)
                assert own.count == PER_HEAD, own.count


def rotary_tables():
    half = np.arange(0, 64, 2, dtype=np.float32)
    inv_freq = np.float32(1.0) / np.power(np.float32(10000.0), half / np.float32(64))
    t = np.arange(T, dtype=np.float32)
    freqs = t[:, None] * inv_freq[None, :]
    freqs = np.concatenate([freqs, freqs], -1).T
    base = (half + np.float32(0.4 * 64)) / np.float32(1.4 * 64)
    scale = base[None, :] ** ((t - T // 2) / np.float32(16))[:, None]
    scale = np.concatenate([scale, scale], -1).T
    sign = np.repeat(np.array([-1, 1], np.float32), 32)[:, None]
    cos, sin = np.cos(freqs), np.sin(freqs) * sign
    one = np.stack([8 * cos * scale, 8 * sin * scale, cos / scale, sin / scale], 1).astype(np.float32)
    return np.concatenate([one, one])


def local_stack(nc, g, d_in):
    LAYERS, PAIRS, W, E = 6, 8, 32, 64
    WINDOWS = T // W
    UNITS, CHUNKS = 341, 3
    LAST = UNITS - 2 * P
    SEQS = 4
    LN_SCALE = 2.0 ** 20
    with ExitStack() as ctx:
        sem = ctx.enter_context(Signals(nc, "local"))

        def sb(n, shape, dt=F32):
            return ctx.enter_context(nc.sbuf_tensor(f"local_{n}", shape, dt))
        base = sb("base", [P, 4, T])
        norm_and_turn(nc, g, "local_ln", [(base[:, :, :], d_in["base"])])
        w_layer = sb("w_layer", [P, PAIRS, 5 * P])
        w_pair = sb("w_pair", [P, 5, P])
        w_o, w_up, w_down = sb("w_o", [P, PAIRS, D]), sb("w_up", [P, 2 * UNITS]), sb("w_down", [P, CHUNKS, D])
        vecs = sb("vecs", [P, 12])
        table = sb("table", [P, 4, T])
        xs = sb("xs", [P, BATCH, W + T])
        q_rot, k_rot = sb("q_rot", [P, N]), sb("k_rot", [P, BATCH, W + T])
        v_at, v_moved = sb("v_at", [P, TILES, P]), sb("v_moved", [P, TILES, P])
        attn = sb("attn", [P, PAIRS, N])
        sq, inv = sb("sq", [P, 2, GROUP]), sb("inv", [P, 2, 2, GROUP])
        mask = sb("mask", [P, 2, 2 * W])
        z = sb("z", [P, 4, SEQS, 2, 2 * W])
        term = z[:, :, :, :, :].rearrange("p a b s k -> p a (b s k)").rearrange("p a (b t) -> p a b t", t=T)
        most, norm = sb("most", [P, 4, SEQS * 2]), sb("norm", [P, 4, 2, SEQS * 2])
        pt = sb("pt", [P, 2, GROUP])
        lg = pt
        same_head, mean_of = sb("same_head", [P, P]), sb("mean_of", [P, P])
        guard, unscale = sb("guard", [P, 1]), sb("unscale", [P, 1])
        gelu, hid = sq, sb("hid", [P, 2, CHUNKS, GROUP])
        xc = q_rot
        rstd = v_at
        made, vecs_loaded, pair_loaded, ffn_loaded = sem("made"), sem("vecs_loaded"), sem("pair_loaded"), sem("ffn_loaded")
        vecs_free, pair_free, ffn_free = sem("vecs_free"), sem("pair_free"), sem("ffn_free")
        staged, stage_free, tabled = sem("staged"), sem("stage_free"), sem("tabled")
        xr_ready, turned, xs_ready = sem("xr_ready"), sem("turned"), sem("xs_ready")
        proj_ready, proj_used, sq_ready = sem("proj_ready"), sem("proj_used"), sem("sq_ready")
        v_ready, v_used = sem("v_ready"), sem("v_used")
        norm_ready, norm_used, inv_ready, inv_used = sem("norm_ready"), sem("norm_used"), sem("inv_ready"), sem("inv_used")
        qk_ready, s_ready, z_ready, e_ready, p_ready = sem("qk_ready"), sem("s_ready"), sem("z_ready"), sem("e_ready"), sem("p_ready")
        pt_ready, pt_copied, o_ready, o_copied, wo_ready = (
            sem("pt_ready"), sem("pt_copied"), sem("o_ready"), sem("o_copied"), sem("wo_ready"))
        mean_ready, xc_ready, xsq_ready, var_ready, rstd_ready, h_ready = (
            sem("mean_ready"), sem("xc_ready"), sem("xsq_ready"), sem("var_ready"), sem("rstd_ready"), sem("h_ready"))
        up_ready, gelu_ready, hid_ready, down_ready = sem("up_ready"), sem("gelu_ready"), sem("hid_ready"), sem("down_ready")
        dve_own, act_own, pool_own, act_passed, sp_passed = sem("dve"), sem("act"), sem("pool"), sem("act_passed"), sem("sp_passed")
        pe_passed, dve_passed, pool_passed = sem("pe_passed"), sem("dve_passed"), sem("pool_passed")
        block = ctx.enter_context(nc.Block())
        FFN = GROUPS * CHUNKS
        normed = sem("normed")

        def add_down(dve, l, c):
            dve.wait_ge(down_ready, l * GROUPS + (c + 1))
            xr = g.xn[:, TPG * c:TPG * (c + 1), :]
            dve.tensor_tensor(xr, xr, g.bank[4 + c % 2][:, :].rearrange("p (n d) -> p n d", d=D), ALU.add).then_inc(xr_ready, 1)

        def seqs(c):
            return slice(SPG * c, SPG * (c + 1))

        @block.sync
        def _(sp):
            sp.wait_ge(made, 1)
            with sp.Fori(0, LAYERS) as l:
                wait_apart(sp, vecs_free, l + 1, sp_passed)
                sp.dma_start(vecs[:, :], d_in["vecs"][bass.ts(l, 1), :, :].rearrange("a p n -> (a p) n")).then_inc(vecs_loaded, 16)
                wait_apart(sp, pair_free, l + 1, sp_passed)
                sp.dma_start(w_layer[:, :, :], d_in["w_layer"][bass.ts(l, 1), :, :, :].rearrange("a p n m -> (a p) n m")
                             ).then_inc(pair_loaded, 16)
                wait_apart(sp, ffn_free, l + 1, sp_passed)
                sp.dma_start(w_o[:, :, :], d_in["w_o"][bass.ts(l, 1), :, :, :].rearrange("a p n m -> (a p) n m")).then_inc(ffn_loaded, 16)
                sp.dma_start(w_up[:, :], d_in["w_up"][bass.ts(l, 1), :, :].rearrange("a p n -> (a p) n")).then_inc(ffn_loaded, 16)
                sp.dma_start(w_down[:, :, :], d_in["w_down"][bass.ts(l, 1), :, :, :].rearrange("a p n m -> (a p) n m")
                             ).then_inc(ffn_loaded, 16)

        @block.gpsimd
        def _(pool):
            own = Chain(pool, pool_own)
            own.step(pool.memset(xs[:, :, 0:W + 1], 0.0))
            own.step(pool.memset(k_rot[:, :, 0:W], 0.0))
            own.step(pool.memset(same_head[:, :], 0.0))
            own.step(pool.memset(mean_of[:, :], 1.0 / D))
            own.step(pool.memset(guard[:, :], 1e-24 * LN_SCALE))
            own.step(pool.memset(unscale[:, :], 0.5 * float(np.log(LN_SCALE))))
            own.step(pool.memset(hid[64:P, :, CHUNKS - 1, :], 1.0))
            own.step(pool.memset(mask[:, :, :], 0.0))
            own.settle()
            for hh in range(2):
                own.step(pool.memset(same_head[E * hh:E * hh + E, E * hh:E * hh + E], 1.0))
            for quadrant in range(4):
                own.settle()
                m = mask[W * quadrant:W * (quadrant + 1), :, :]
                own.step(pool.affine_select(out=m, in_=m, compare_op=ALU.is_ge, fill=-1e30, base=0,
                                            pattern=[[0, 2], [1, 2 * W]], channel_multiplier=-1))
                own.step(pool.affine_select(out=m, in_=m, compare_op=ALU.is_ge, fill=-1e30, base=W,
                                            pattern=[[0, 2], [-1, 2 * W]], channel_multiplier=1))
            own.step(pool.memset(mask[0:W, 0, 0:W], -1e30))
            pool.sem_inc(made, 1)
            with pool.Fori(0, LAYERS) as l:
                wait_apart(pool, pair_loaded, l * 16 + 16, pool_passed)
                with pool.Fori(0, PAIRS) as hp:
                    pool.wait_ge(stage_free, l * PAIRS + hp + 1)
                    pool.tensor_copy(w_pair[:, :, :].rearrange("p a c -> p (a c)"),
                                     w_layer[:, bass.ts(hp, 1), :].rearrange("p a c -> p (a c)")).then_inc(staged, 1)
                pool.wait_ge(staged, l * PAIRS + PAIRS)
                pool.sem_inc(pair_free, 1)

        @block.tensor
        def _(pe):
            pe.wait_ge(made, 1)

            def turn(l, second):
                for c in range(GROUPS):
                    pe.wait_ge(xr_ready, l * 8 + (4 * second + c + 1))
                    for i in range(TPG):
                        mm = pe.transpose(g.bank[c][:, i * P:(i + 1) * P], g.xn[:, TPG * c + i, :], g.ident[:, :])
                    mm.then_inc(turned, 1)

            with pe.Fori(0, LAYERS) as l:
                turn(l, 0)
                wait_apart(pe, xs_ready, l * 8 + 4, pe_passed)
                with pe.Fori(0, PAIRS) as hp:
                    it = l * PAIRS + hp
                    pe.wait_ge(staged, it + 1)
                    for c in range(GROUPS):
                        pe.wait_ge(proj_used, it * 4 + (c + 1))
                        for m in range(4):
                            mm = pe.matmul(g.bank[m][:, :].rearrange("p (b t) -> p b t", t=T), w_pair[:, m, :], xs[:, seqs(c), W:],
                                           start=True, stop=True)
                        mm.then_inc(proj_ready, 1)
                        pe.wait_ge(v_used, it * 4 + (c + 1))
                        if c == 0:
                            pe.wait_ge(o_copied, it * 2 + 2)
                        for b in range(SPG):
                            for n in range(2):
                                i = 2 * b + n
                                pe.matmul(g.bank[6][:, i * P:(i + 1) * P], xs[:, SPG * c + b, W + n * P:W + (n + 1) * P],
                                          w_pair[:, 4, :], start=True, stop=True)
                                mm = pe.matmul(g.bank[7][:, i * P:(i + 1) * P], xs[:, SPG * c + b, n * P:(n + 1) * P],
                                               w_pair[:, 4, :], start=True, stop=True)
                        mm.then_inc(v_ready, 1)
                        pe.wait_ge(sq_ready, it * 4 + (c + 1))
                        pe.wait_ge(norm_used, it * 4 + (c + 1))
                        for m in range(2):
                            mm = pe.matmul(g.bank[4 + m][:, :], same_head[:, :], sq[:, m, :], start=True, stop=True)
                        mm.then_inc(norm_ready, 1)
                    pe.wait_ge(norm_ready, it * 4 + 4)
                    pe.sem_inc(stage_free, 1)
                    wait_apart(pe, qk_ready, it * 4 + 4, pe_passed)
                    for idx in range(4):
                        half, hh = divmod(idx, 2)
                        rows = slice(E * hh, E * (hh + 1))
                        for b in range(SEQS):
                            for w in range(WINDOWS):
                                n, s, r = w // 4, w // 2 % 2, w % 2
                                part = slice(64 * n + 32 * r, 64 * n + 32 * r + W)
                                seq = SEQS * half + b
                                mm = pe.matmul(g.bank[idx][part, b * P + s * 2 * W:b * P + (s + 1) * 2 * W],
                                               q_rot[rows, seq * T + w * W:seq * T + (w + 1) * W],
                                               k_rot[rows, seq, w * W:(w + 2) * W], start=True, stop=True)
                        mm.then_inc(s_ready, 1)

                    def turn_probs(idx):
                        pe.wait_ge(p_ready, it * 4 + (idx + 1))
                        for b in range(SEQS):
                            mm = pe.transpose(g.bank[4 + idx % 2][:, b * P:(b + 1) * P],
                                              z[:, idx, b, :, :].rearrange("p s k -> p (s k)"), g.ident[:, :])
                        mm.then_inc(pt_ready, 1)

                    def weigh_values(idx):
                        half, hh = divmod(idx, 2)
                        wait_apart(pe, pt_copied, it * 4 + (idx + 1), pe_passed)
                        if idx == 2:
                            wait_apart(pe, o_copied, it * 2 + 3, pe_passed)
                        for b in range(SEQS):
                            for w in range(WINDOWS):
                                n, s, r = w // 4, w // 2 % 2, w % 2
                                keys = slice(64 * s, 64 * s + 64)
                                q0 = b * P + 64 * n + 32 * r
                                v = (v_at if r else v_moved)[keys, 2 * (SEQS * half + b) + n, E * hh:E * (hh + 1)]
                                mm = pe.matmul(g.bank[6 + s][E * hh:E * (hh + 1), q0:q0 + W], v, pt[keys, hh, q0:q0 + W],
                                               start=True, stop=True)
                        mm.then_inc(o_ready, 1)
                    turn_probs(0)
                    turn_probs(1)
                    weigh_values(0)
                    turn_probs(2)
                    weigh_values(1)
                    turn_probs(3)
                    weigh_values(2)
                    weigh_values(3)
                pe.wait_ge(ffn_loaded, l * 48 + 48)
                pe.wait_ge(o_copied, (l * PAIRS + PAIRS) * 2 + 2)
                for c in range(GROUPS):
                    for i in range(TPG):
                        for p in range(PAIRS):
                            t0 = c * GROUP + i * P
                            mm = pe.matmul(g.bank[4 + c][:, i * P:(i + 1) * P], attn[:, p, t0:t0 + P], w_o[:, p, :],
                                           start=(p == 0), stop=(p == PAIRS - 1))
                    mm.then_inc(wo_ready, 1)
                turn(l, 1)
                for c in range(GROUPS):
                    pe.wait_ge(xs_ready, l * 8 + (5 + c))
                    pe.matmul(g.bank[c][:, :].rearrange("p (b t) -> p b t", t=T), mean_of[:, :], xs[:, seqs(c), W:],
                              start=True, stop=True).then_inc(mean_ready, 1)
                for c in range(GROUPS):
                    pe.wait_ge(xsq_ready, l * GROUPS + (c + 1))
                    pe.matmul(g.bank[4 + c][:, :], mean_of[:, :], attn[:, 0, tok(c)], start=True, stop=True).then_inc(var_ready, 1)
                for c in range(GROUPS):
                    pe.wait_ge(h_ready, l * GROUPS + (c + 1))
                    for m in range(CHUNKS):
                        i = CHUNKS * c + m
                        rows = P if m < CHUNKS - 1 else LAST
                        if i >= 2:
                            pe.wait_ge(hid_ready, l * FFN + (i - 1))
                        for k in range(2):
                            mm = pe.matmul(g.bank[2 * k + i % 2][0:rows, :], w_up[:, k * UNITS + m * P:k * UNITS + m * P + rows],
                                           g.xnT[:, tok(c)], start=True, stop=True)
                        mm.then_inc(up_ready, 1)
                    pe.wait_ge(hid_ready, l * FFN + CHUNKS * (c + 1))
                    if c == 0:
                        pe.wait_ge(rstd_ready, l * GROUPS + GROUPS)
                    if c >= 2:
                        pe.wait_ge(xr_ready, l * 8 + (8 + c - 1))
                    for i in range(TPG):
                        for m in range(CHUNKS):
                            rows = P if m < CHUNKS - 1 else LAST + 1
                            mm = pe.matmul(g.bank[4 + c % 2][:, i * P:(i + 1) * P], hid[0:rows, c % 2, m, i * P:(i + 1) * P],
                                           w_down[0:rows, m, :], start=(m == 0), stop=(m == CHUNKS - 1))
                    mm.then_inc(down_ready, 1)
                pe.wait_ge(down_ready, l * GROUPS + GROUPS)
                pe.sem_inc(ffn_free, 1)

        @block.scalar
        def _(act):
            own = Chain(act, act_own)
            act.wait_ge(made, 1)
            for free, n in ((stage_free, 1), (pair_free, 1), (ffn_free, 1), (norm_used, 1), (v_used, 1), (o_copied, 2)):
                act.sem_inc(free, n)

            def turn(l, second):
                for c in range(GROUPS):
                    act.wait_ge(turned, l * 8 + (4 * second + c + 1))
                    bank = g.bank[c][:, :].rearrange("p (b t) -> p b t", t=T)
                    act.activation(xs[0:64, seqs(c), W:], bank[0:64, :, :], ACT.Copy)
                    act.activation(xs[64:P, seqs(c), W + 1:], bank[64:P, :, 0:T - 1], ACT.Copy).then_inc(xs_ready, 1)

            LN_STEPS = GROUPS * 2
            with act.Fori(0, LAYERS) as l:
                act.preload_act_table_set(LN_EXP)
                turn(l, 0)
                with act.Fori(0, PAIRS) as hp:
                    it = l * PAIRS + hp
                    for c in range(GROUPS):
                        act.wait_ge(proj_ready, it * 4 + (c + 1))
                        for m in range(2):
                            ins = act.activation(sq[:, m, :], g.bank[2 * m][:, :], ACT.Square)
                        ins.then_inc(sq_ready, 1)
                        act.wait_ge(v_ready, it * 4 + (c + 1))
                        t = slice(TPG * c, TPG * (c + 1))
                        act.activation(v_at[:, t, :].rearrange("p n c -> p (n c)"), g.bank[6][:, :], ACT.Copy)
                        act.activation(v_moved[:, t, :].rearrange("p n c -> p (n c)"), g.bank[7][:, :], ACT.Copy).then_inc(v_used, 1)
                        act.wait_ge(norm_ready, it * 4 + (c + 1))
                        for m in range(2):
                            ins = act.activation(lg[:, m, :], g.bank[4 + m][:, :], ACT.Ln, bias=guard[:, 0:1], scale=LN_SCALE)
                        ins.then_inc(norm_used, 1)
                        act.wait_ge(norm_used, it * 4 + (c + 2))
                        act.wait_ge(inv_used, it * 4 + (c + 1))
                        act.activation(inv[:, c % 2, :, :], lg[:, :, :], ACT.Exp, bias=unscale[:, 0:1], scale=-0.5).then_inc(inv_ready, 1)
                    for idx in range(4):
                        act.wait_ge(z_ready, it * 4 + (idx + 1))
                        act.activation(z[:, idx, :, :, :], z[:, idx, :, :, :], ACT.Exp).then_inc(e_ready, 1)

                    def copy_turned(idx):
                        act.wait_ge(pt_ready, it * 4 + (idx + 1))
                        if idx >= 2:
                            act.wait_ge(o_ready, it * 4 + (idx - 1))
                        act.activation(pt[:, idx % 2, :], g.bank[4 + idx % 2][:, :], ACT.Copy).then_inc(pt_copied, 1)

                    def copy_out(half):
                        wait_apart(act, o_ready, it * 4 + (2 * half + 2), act_passed)
                        for s in range(2):
                            tokens = attn[:, bass.ts(hp, 1), half * SEQS * T:(half + 1) * SEQS * T].rearrange(
                                "p a (b n s q) -> p (a b n) s q", n=2, s=2, q=64)
                            ins = act.activation(tokens[:, :, s, :], g.bank[6 + s][:, :].rearrange("p (x q) -> p x q", q=64), ACT.Copy)
                        ins.then_inc(o_copied, 1)
                    copy_turned(0)
                    copy_turned(1)
                    copy_turned(2)
                    copy_out(0)
                    copy_turned(3)
                    copy_out(1)
                turn(l, 1)
                own = Chain(act, act_own, l * LN_STEPS)
                for c in range(GROUPS):
                    act.wait_ge(xc_ready, l * GROUPS + (c + 1))
                    act.activation(attn[:, 0, tok(c)], xc[:, tok(c)], ACT.Square).then_inc(xsq_ready, 1)
                for c in range(GROUPS):
                    act.wait_ge(var_ready, l * GROUPS + (c + 1))
                    own.step(act.activation(lg[:, c % 2, :], g.bank[4 + c][:, :], ACT.Ln, bias=g.eps[:, 0:1]))
                    own.add(act.activation(rstd[:, TPG * c:TPG * (c + 1), :].rearrange("p n c -> p (n c)"), lg[:, c % 2, :],
                                           ACT.Exp, scale=-0.5))
                    own.settle()
                    act.sem_inc(rstd_ready, 1)
                for c in range(GROUPS):
                    for m in range(CHUNKS):
                        i = CHUNKS * c + m
                        rows = P if m < CHUNKS - 1 else LAST
                        act.wait_ge(up_ready, l * FFN + (i + 1))
                        if i >= 2:
                            act.wait_ge(hid_ready, l * FFN + (i - 1))
                        act.activation(gelu[0:rows, i % 2, :], g.bank[2 + i % 2][0:rows, :], ACT.Gelu,
                                       bias=vecs[0:rows, 9 + m:10 + m]).then_inc(gelu_ready, 1)

        @block.vector
        def _(dve):
            dve.wait_ge(made, 1)
            for free, n in ((vecs_free, 1), (xr_ready, 4), (proj_used, 1), (inv_used, 2)):
                dve.sem_inc(free, n)
            PER_PAIR = GROUPS * 5 + 4 * 4
            with dve.Fori(0, LAYERS) as l:
                dve.wait_ge(vecs_loaded, l * 16 + 16)
                for k in range(4):
                    ins = dve.tensor_scalar(table[:, k, :], base[:, k, :], vecs[:, k:k + 1], None, ALU.mult)
                ins.then_inc(tabled, 1)
                wait_apart(dve, tabled, l + 1, dve_passed)
                with dve.Fori(0, PAIRS) as hp:
                    it = l * PAIRS + hp
                    own = Chain(dve, dve_own, it * PER_PAIR)
                    for c in range(GROUPS):
                        dve.wait_ge(proj_ready, it * 4 + (c + 1))
                        for k in (1, 3, 0, 2):
                            if k == 0:
                                dve.wait_ge(sq_ready, it * 4 + (c + 1))
                            ins = dve.tensor_tensor(term[:, k, :, :], g.bank[k][:, :].rearrange("p (b t) -> p b t", t=T),
                                                    table[:, k, :].unsqueeze(1).to_broadcast([P, SPG, T]), ALU.mult)
                            if k != 2:
                                own.add(ins)
                        ins.then_inc(proj_used, 1)
                        own.settle()
                        own.add(dve.tensor_tensor(term[:, 0, :, :], term[:, 0, :, :], term[:, 1, :, :], ALU.add))
                        dve.wait_ge(proj_used, it * 4 + (c + 2))
                        own.settle(behind=1)
                        own.add(dve.tensor_tensor(term[:, 2, :, :], term[:, 2, :, :], term[:, 3, :, :], ALU.add))
                        dve.wait_ge(inv_ready, it * 4 + (c + 1))
                        own.settle(behind=1)
                        dve.tensor_tensor(q_rot[:, tok(c)], term[:, 0, :, :].rearrange("p b t -> p (b t)"), inv[:, c % 2, 0, :], ALU.mult)
                        own.settle()
                        dve.tensor_tensor(k_rot[:, seqs(c), W:], term[:, 2, :, :],
                                          inv[:, c % 2, 1, :].rearrange("p (b t) -> p b t", t=T), ALU.mult).then_inc(qk_ready, 1)
                        dve.wait_ge(qk_ready, it * 4 + (c + 1))
                        dve.sem_inc(inv_used, 1)

                    def scores(idx):
                        dve.wait_ge(s_ready, it * 4 + (idx + 1))
                        zi = z[:, idx, :, :, :]
                        own.step(dve.tensor_tensor(zi, g.bank[idx][:, :].rearrange("p (b s k) -> p b s k", s=2, k=2 * W),
                                                   mask[:, :, :].unsqueeze(1).to_broadcast([P, SEQS, 2, 2 * W]), ALU.add))
                        rows = zi.rearrange("p b s k -> p (b s) k")
                        own.step(dve.tensor_reduce(most[:, idx, :], rows, AX.X, ALU.max))
                        dve.tensor_tensor(rows, rows, spread(most[:, idx, :], 2 * W), ALU.subtract).then_inc(z_ready, 1)

                    def normalize(idx):
                        dve.wait_ge(e_ready, it * 4 + (idx + 1))
                        rows = z[:, idx, :, :, :].rearrange("p b s k -> p (b s) k")
                        own.step(dve.tensor_reduce(norm[:, idx, 0, :], rows, AX.X, ALU.add))
                        own.step(dve.reciprocal(norm[:, idx, 1, :], norm[:, idx, 0, :]))
                        dve.tensor_tensor(rows, rows, spread(norm[:, idx, 1, :], 2 * W), ALU.mult).then_inc(p_ready, 1)
                    scores(0)
                    for idx in range(1, 4):
                        scores(idx)
                        normalize(idx - 1)
                    normalize(3)
                    assert own.count == PER_PAIR, own.count
                for c in range(GROUPS):
                    dve.wait_ge(wo_ready, l * GROUPS + (c + 1))
                    xr = g.xn[:, TPG * c:TPG * (c + 1), :]
                    dve.tensor_tensor(xr, xr, g.bank[4 + c][:, :].rearrange("p (n d) -> p n d", d=D), ALU.add).then_inc(xr_ready, 1)
                for c in range(GROUPS):
                    dve.wait_ge(mean_ready, l * GROUPS + (c + 1))
                    dve.tensor_tensor(xc[:, tok(c)].rearrange("p (b t) -> p b t", t=T), xs[:, seqs(c), W:],
                                      g.bank[c][:, :].rearrange("p (b t) -> p b t", t=T), ALU.subtract).then_inc(xc_ready, 1)
                for c in range(GROUPS):
                    dve.wait_ge(rstd_ready, l * GROUPS + (c + 1))
                    dve.wait_ge(xc_ready, l * GROUPS + GROUPS)
                    h = g.xnT[:, tok(c)]
                    dve.tensor_tensor(h, xc[:, tok(c)], rstd[:, TPG * c:TPG * (c + 1), :].rearrange("p n c -> p (n c)"), ALU.mult).then_inc(normed, 1)
                    dve.wait_ge(normed, l * GROUPS + (c + 1))
                    dve.tensor_scalar(h, h, vecs[:, 4:5], vecs[:, 5:6], ALU.mult, ALU.add).then_inc(h_ready, 1)
                for c in range(GROUPS):
                    for m in range(CHUNKS):
                        i = CHUNKS * c + m
                        rows = P if m < CHUNKS - 1 else LAST
                        dve.wait_ge(gelu_ready, l * FFN + (i + 1))
                        if c >= 2 and m == 0:
                            dve.wait_ge(down_ready, l * GROUPS + (c - 1))
                        dve.scalar_tensor_tensor(out=hid[0:rows, c % 2, m, :], in0=g.bank[i % 2][0:rows, :],
                                                 scalar=vecs[0:rows, 6 + m:7 + m], in1=gelu[0:rows, i % 2, :],
                                                 op0=ALU.add, op1=ALU.mult).then_inc(hid_ready, 1)
                    if c >= 1:
                        add_down(dve, l, c - 1)
                add_down(dve, l, GROUPS - 1)
                dve.wait_ge(hid_ready, l * FFN + FFN)
                dve.sem_inc(vecs_free, 1)

    with ExitStack() as ctx:
        sem = ctx.enter_context(Signals(nc, "local_sum"))
        added = sem("added")
        block = ctx.enter_context(nc.Block())

        @block.vector
        def _(dve):
            dve.tensor_tensor(g.x[:, :, :], g.x[:, :, :], g.xn[:, :, :], ALU.add).then_inc(added, 1)
            dve.wait_ge(added, 1)


def store(nc, g, out_dram):
    with ExitStack() as ctx:
        stored = ctx.enter_context(nc.semaphore("stored"))
        block = ctx.enter_context(nc.Block())

        @block.sync
        def _(sp):
            sp.dma_start(out_dram.rearrange("(n p) d -> p n d", p=P), g.x[:, :, :]).then_inc(stored, 16)
            sp.wait_ge(stored, 16)


STAGES = (0, 1, 2, 3, 4, 5, 6, 7)


def build(nc, d_in, out_dram):
    g = Shared()
    with ExitStack() as ctx:
        def sb(n, shape):
            return ctx.enter_context(nc.sbuf_tensor(n, shape, F32))
        g.x, g.xn = sb("x", [P, TILES, D]), sb("xn", [P, TILES, D])
        g.xnT = sb("xnT", [P, N])
        g.ident, g.eps, g.one = sb("ident", [P, P]), sb("eps", [P, 1]), sb("one", [P, 1])
        g.bank = [ctx.enter_context(nc.psum_tensor(f"bank{i}", [P, 512], F32)) for i in range(8)]
        g.weights, g.weights_due = ctx.enter_context(nc.semaphore("weights")), 0
        set_up(nc, g, d_in["x"])
        if 0 in STAGES:
            mamba(nc, g, "mamba0", None, d_in["m0"])
        if 1 in STAGES:
            moe(nc, g, "moe0", d_in["f0"], 16, 9, lambda j: j if j < 8 else None, True, True, False)
        if 2 in STAGES:
            rotor_memory(nc, g, d_in["r1"])
        if 3 in STAGES:
            local_stack(nc, g, d_in["a1"])
        if 4 in STAGES:
            delta_rule(nc, g, d_in["g2"])
        if 5 in STAGES:
            moe(nc, g, "moe2", d_in["f2"], 8, 8, lambda j: j, True, False, False)
        if 6 in STAGES:
            mamba(nc, g, "mamba3", None, d_in["m3"])
        if 7 in STAGES:
            moe(nc, g, "moe3", d_in["f3"], 8, 32, lambda j: j // 4, False, False, True)
        store(nc, g, out_dram)


def lay_out(inputs):
    i = {k: np.asarray(v) for k, v in inputs.items()}

    def rows(a, n=P):
        return a.reshape(-1, n, *a.shape[1:]).swapaxes(0, 1)

    def everywhere(a):
        return np.broadcast_to(a[None], (P,) + a.shape)

    def mamba_side(p, names):
        w_x = i[p + names["w_x"]]
        out = {"w_in": i[p + "W_in"], "conv_w": rows(i[p + "conv_w"][:, 0, :]), "conv_b": rows(i[p + "conv_b"]),
               "w_bc": rows(w_x[:, -32:]), "b_dt": rows(i[p + "b_dt"]), "skip": rows(i[p + names["skip"]]),
               "w_out": rows(i[p + "W_out"])}
        a_log = i[p + "A_log"]
        out["a_log"] = rows(a_log) if a_log.ndim == 2 else np.broadcast_to(a_log, (P, 2, 16))
        if w_x.shape[1] == 33:
            out["w_dt"], out["w_dt_col"] = i[p + "W_dt"], rows(w_x[:, 0])
        else:
            out["w_dt"] = rows(i[p + "W_dt"])
        return out

    turned_half = np.concatenate([np.arange(32, 64), np.arange(32)])
    wq, wk, wv = (i["L1_ffn_Wqkv"][:, :, 1024 * n:1024 * (n + 1)].reshape(6, D, 8, 2, 64) for n in range(3))
    w_layer = np.stack([wq, wq[..., turned_half], wk, wk[..., turned_half], wv], 3).reshape(6, D, 8, 5 * P)
    scales = []
    for a in (i["L1_ffn_q_scale"], i["L1_ffn_k_scale"]):
        scales += [np.concatenate([a, a], 1), np.concatenate([a[:, turned_half]] * 2, 1)]
    b1 = np.zeros((6, 2, 3 * P), np.float32)
    b1[:, :, :341] = i["L1_ffn_b1"].reshape(6, 2, 341)
    w_down = np.zeros((6, 3 * P, D), np.float32)
    w_down[:, :341], w_down[:, 341] = i["L1_ffn_W2"], i["L1_ffn_b2"]
    return {
        "a1": {
            "base": rotary_tables(), "w_layer": w_layer,
            "vecs": np.stack(scales + [i["L1_ffn_ln_g"], i["L1_ffn_ln_b"]]
                             + [b1[:, k, P * m:P * (m + 1)] for k in range(2) for m in range(3)], 2),
            "w_o": i["L1_ffn_Wo"].reshape(6, 8, P, D).swapaxes(1, 2), "w_up": i["L1_ffn_W1"],
            "w_down": w_down.reshape(6, 3, P, D).swapaxes(1, 2),
        },
        "m0": mamba_side("L0_attn_", {"w_x": "W_xproj", "skip": "Dp"}),
        "m3": mamba_side("L3_attn_", {"w_x": "W_x", "skip": "D"}),
        "f0": {
            "gate_w": i["L0_ffn_gate_w"].T, "gate_b": everywhere(i["L0_ffn_expert_bias"]),
            "w1": np.concatenate([i["L0_ffn_w1"].reshape(-1, D), i["L0_ffn_sw1"]]).T.reshape(D, 9, P),
            "w3": np.concatenate([i["L0_ffn_w3"].reshape(-1, D), i["L0_ffn_sw3"]]).T.reshape(D, 9, P),
            "w2": rows(np.concatenate([i["L0_ffn_w2"].swapaxes(1, 2).reshape(-1, D), i["L0_ffn_sw2"].T])),
            "b1": rows(np.concatenate([i["L0_ffn_b1"].reshape(-1), i["L0_ffn_sb1"]])),
            "b3": rows(np.concatenate([i["L0_ffn_b3"].reshape(-1), i["L0_ffn_sb3"]])),
            "b2": np.concatenate([i["L0_ffn_b2"], i["L0_ffn_sb2"][None]]),
        },
        "f2": {
            "gate_w": i["L2_ffn_Wg"].T, "gate_b": everywhere(i["L2_ffn_bg"]),
            "w2": i["L2_ffn_We"].transpose(2, 0, 1), "b2": i["L2_ffn_be"],
        },
        "f3": {
            "gate_w": i["L3_ffn_gate_w"], "dom": i["L3_ffn_dom"].T,
            "w1": i["L3_ffn_W1"].transpose(1, 0, 2).reshape(D, 32, P),
            "w3": i["L3_ffn_W3"].transpose(1, 0, 2).reshape(D, 32, P),
            "w2": rows(i["L3_ffn_W2"].reshape(-1, D)),
        },
        "r1": {"w_v": i["L1_attn_Wv"].T, "w_o": i["L1_attn_Wo"].T, "freqs": i["L1_attn_freqs"][:, None]},
        "g2": {
            "w_ab": np.concatenate([i["L2_attn_a_w"], i["L2_attn_b_w"]]).T,
            "ab_bias": everywhere(np.concatenate([i["L2_attn_dt_bias"], np.zeros(8, np.float32)])),
            "a_log": everywhere(i["L2_attn_A_log"]), "norm_w": i["L2_attn_norm_w"][:, None],
            "w_qkv": i["L2_attn_qkv_w"].reshape(3, 8, P, D).transpose(3, 1, 0, 2),
            "taps": i["L2_attn_conv_w"].reshape(3, 8, P, 4).transpose(2, 1, 0, 3),
            "w_z": i["L2_attn_z_w"].reshape(8, P, D).transpose(2, 0, 1),
            "w_o": i["L2_attn_out_w"].reshape(D, 8, P).transpose(2, 1, 0),
        },
    }


def kernel(**inputs):
    import concourse.bacc as bacc
    from concourse.bass_utils import run_bass_kernel_spmd

    nc = bacc.Bacc("TRN2", target_bir_lowering=False, num_devices=1)
    arrays = {"x": np.ascontiguousarray(np.asarray(inputs["L0_attn_x"]).reshape(N, D))}
    d_in = {"x": nc.dram_tensor("x_dram", [N, D], F32, kind="ExternalInput").ap()}
    arrays = {"x_dram": arrays["x"]}
    for side, tensors in lay_out(inputs).items():
        d_in[side] = {}
        for name, a in tensors.items():
            a = np.ascontiguousarray(a)
            arrays[f"{side}_{name}_dram"] = a
            d_in[side][name] = nc.dram_tensor(f"{side}_{name}_dram", a.shape, F32, kind="ExternalInput").ap()
    out = nc.dram_tensor("out_dram", [N, D], F32, kind="ExternalOutput").ap()
    build(nc, d_in, out)
    r = run_bass_kernel_spmd(nc, [arrays], core_ids=[0])
    return r.results[0]["out_dram"].reshape(BATCH, T, D)
```

```python
from contextlib import ExitStack

import numpy as np

import concourse.bass as bass
from concourse import mybir

F32 = mybir.dt.float32
BF16 = mybir.dt.bfloat16
I32 = mybir.dt.int32
U32 = mybir.dt.uint32
ALU = mybir.AluOpType
ACT = mybir.ActivationFunctionType
AX = mybir.AxisListType

LN_EXP = "natural_log_exp_and_others"
P = 128
BATCH = 8
T = 256
D = 128
N = BATCH * T
TILES = N // P
GROUP = 512
GROUPS = N // GROUP
TPG = GROUP // P
SPG = GROUP // T
EPS = 1e-5


class Shared:
    pass


class Chain:

    def __init__(self, eng, sem, base=0):
        self.eng, self.sem, self.base, self.count = eng, sem, base, 0

    def add(self, ins):
        ins.then_inc(self.sem, 1)
        self.count += 1

    def settle(self, behind=0):
        self.eng.wait_ge(self.sem, self.base + self.count - behind)

    def step(self, ins):
        self.add(ins)
        self.settle()


class Signals:

    def __init__(self, nc, tag):
        self.nc, self.tag, self.stack, self.all = nc, tag, ExitStack(), []

    def __enter__(self):
        return self

    def __call__(self, name):
        self.all.append(self.stack.enter_context(self.nc.semaphore(f"{self.tag}_{name}")))
        return self.all[-1]

    def __exit__(self, *_):
        with self.nc.Block() as block:
            @block.sync
            def _(sp):
                for s in self.all:
                    sp.sem_clear(s)
        self.stack.close()


def tok(c):
    return slice(c * GROUP, (c + 1) * GROUP)


def spread(ap, n):
    return ap.unsqueeze(2).to_broadcast([ap.shape[0], ap.shape[1], n])


def wait_apart(eng, sem, value, passed):
    eng.wait_ge(sem, value)
    eng.sem_inc(passed, 1)


def set_up(nc, g, x_dram):
    with ExitStack() as ctx:
        sem = ctx.enter_context(Signals(nc, "setup"))
        loaded, filled = sem("loaded"), sem("filled")
        block = ctx.enter_context(nc.Block())

        @block.sync
        def _(sp):
            sp.dma_start(g.x[:, :, :], x_dram.rearrange("(n p) d -> p n d", p=P)).then_inc(loaded, 16)
            sp.wait_ge(loaded, 16)

        @block.gpsimd
        def _(pool):
            pool.memset(g.ident[:, :], 0.0).then_inc(filled, 1)
            pool.memset(g.eps[:, :], EPS).then_inc(filled, 1)
            pool.memset(g.one[:, :], 1.0).then_inc(filled, 1)
            pool.wait_ge(filled, 3)
            pool.affine_select(out=g.ident[:, :], in_=g.ident[:, :], compare_op=ALU.not_equal, fill=1.0, base=0,
                               pattern=[[-1, P]], channel_multiplier=1).then_inc(filled, 1)


def norm_and_turn(nc, g, tag, loads):
    with ExitStack() as ctx:
        sem = ctx.enter_context(Signals(nc, tag))
        st = ctx.enter_context(nc.sbuf_tensor(f"{tag}_stats", [P, 5, TILES], F32))
        xc = ctx.enter_context(nc.sbuf_tensor(f"{tag}_xc", [P, TILES, D], F32))
        sq = ctx.enter_context(nc.sbuf_tensor(f"{tag}_sq", [P, TILES, D], F32))
        centred, squared, var_ready, rstd_ready = sem("centred"), sem("squared"), sem("var"), sem("rstd")
        normed, turned, dve_own, act_own = sem("normed"), sem("turned"), sem("dve"), sem("act")
        block = ctx.enter_context(nc.Block())

        @block.sync
        def _(sp):
            for dst, src in loads:
                sp.dma_start(dst, src).then_inc(g.weights, 16)
                g.weights_due += 16

        @block.vector
        def _(dve):
            own = Chain(dve, dve_own)
            own.step(dve.tensor_reduce(st[:, 0, :], g.x[:, :, :], AX.X, ALU.add))
            own.step(dve.tensor_scalar(st[:, 1, :], st[:, 0, :], -1.0 / D, None, ALU.mult))
            dve.tensor_tensor(xc[:, :, :], g.x[:, :, :], spread(st[:, 1, :], D), ALU.add).then_inc(centred, 1)
            dve.wait_ge(squared, 1)
            dve.tensor_reduce(st[:, 2, :], sq[:, :, :], AX.X, ALU.add).then_inc(var_ready, 1)
            dve.wait_ge(rstd_ready, 1)
            for c in range(GROUPS):
                t = slice(TPG * c, TPG * (c + 1))
                dve.tensor_tensor(g.xn[:, t, :], xc[:, t, :], spread(st[:, 4, t], D), ALU.mult).then_inc(normed, 1)

        @block.scalar
        def _(act):
            act.preload_act_table_set(LN_EXP)
            act.wait_ge(centred, 1)
            act.activation(sq[:, :, :], xc[:, :, :], ACT.Square).then_inc(squared, 1)
            act.wait_ge(var_ready, 1)
            act.activation(st[:, 3, :], st[:, 2, :], ACT.Ln, bias=g.eps[:, 0:1], scale=1.0 / D).then_inc(act_own, 1)
            act.wait_ge(act_own, 1)
            act.activation(st[:, 4, :], st[:, 3, :], ACT.Exp, scale=-0.5).then_inc(rstd_ready, 1)
            for c in range(GROUPS):
                act.wait_ge(turned, c + 1)
                act.activation(g.xnT[:, tok(c)], g.bank[c][:, :], ACT.Copy)

        @block.tensor
        def _(pe):
            for c in range(GROUPS):
                pe.wait_ge(normed, c + 1)
                for i in range(TPG):
                    mm = pe.transpose(g.bank[c][:, i * P:(i + 1) * P], g.xn[:, TPG * c + i, :], g.ident[:, :])
                mm.then_inc(turned, 1)


def mamba(nc, g, tag, w, d_in):
    HALVES, STATES, TAPS = 2, 16, 4
    rank_one_dt = "w_dt_col" in d_in
    with ExitStack() as ctx:
        sem = ctx.enter_context(Signals(nc, tag))

        def sb(n, shape, dt=F32):
            return ctx.enter_context(nc.sbuf_tensor(f"{tag}_{n}", shape, dt))
        w_in = sb("w_in", [P, 4 * P])
        conv_w, conv_b = sb("conv_w", [P, HALVES, TAPS]), sb("conv_b", [P, HALVES])
        w_bc = sb("w_bc", [P, HALVES, 2 * STATES])
        w_dt = sb("w_dt", [1, HALVES * P] if rank_one_dt else [P, HALVES, HALVES * P])
        w_dtc = sb("w_dtc", [P, HALVES])
        b_dt, a_log, skip = sb("b_dt", [P, HALVES]), sb("a_log", [P, HALVES, STATES]), sb("skip", [P, HALVES])
        w_out = sb("w_out", [P, HALVES, D])
        loads = [(w_in[:, :], d_in["w_in"]), (conv_w[:, :, :], d_in["conv_w"]), (conv_b[:, :], d_in["conv_b"]),
                 (w_bc[:, :, :], d_in["w_bc"]), (b_dt[:, :], d_in["b_dt"]), (a_log[:, :, :], d_in["a_log"]),
                 (skip[:, :], d_in["skip"]), (w_out[:, :, :], d_in["w_out"])]
        if rank_one_dt:
            loads += [(w_dt[:, :], d_in["w_dt"]), (w_dtc[:, :], d_in["w_dt_col"])]
        else:
            loads += [(w_dt[:, :, :], d_in["w_dt"])]
        norm_and_turn(nc, g, tag + "_ln", loads)

        xpad = sb("xpad", [P, HALVES, BATCH, T + TAPS - 1])
        cv = sb("cv", [P, HALVES, N])
        u = sb("u", [P, HALVES, N])
        sz = sb("sz", [P, HALVES, N])
        dt = sb("dt", [P, HALVES, N])
        du = sb("du", [P, HALVES, N])
        bc3 = sb("bc3", [3 * 32, N], BF16)
        part = sb("part", [32, 2, N], BF16)
        rest = sb("rest", [32, 2, N])
        dt_row = sb("dt_row", [1, N])
        pick = sb("pick", [3 * 32, 2 * STATES, P], BF16)
        a_neg = sb("a_neg", [P, HALVES, STATES])
        decay = sb("decay", [P, 2, HALVES, SPG, T])
        dbu = sb("dbu", [P, HALVES, GROUP])
        state = sb("state", [P, HALVES, GROUP])
        hc = sb("hc", [P, 2, HALVES, GROUP])
        y = sb("y", [P, HALVES, GROUP])

        prepared, picked = sem("prepared"), sem("picked")
        proj_ready, proj_used, conv_ready, u_ready = sem("proj_ready"), sem("proj_used"), sem("conv_ready"), sem("u_ready")
        bc_ready, bc_split, bc_moved = sem("bc_ready"), sem("bc_split"), sem("bc_moved")
        row_ready, row_copied, dt_psum, dt_biased = sem("row_ready"), sem("row_copied"), sem("dt_psum"), sem("dt_biased")
        log_ready, a_exp, scan_inputs = sem("log_ready"), sem("a_exp"), sem("scan_inputs")
        spread_ready, spread_used = sem("spread_ready"), sem("spread_used")
        decay_ready, decay_used = sem("decay_ready"), sem("decay_used")
        hc_ready, hc_used, sum_ready, sum_used = sem("hc_ready"), sem("hc_used"), sem("sum_ready"), sem("sum_used")
        y_ready, out_ready, out_used = sem("y_ready"), sem("out_ready"), sem("out_used")
        dve_own, act_own, act_passed = sem("dve"), sem("act"), sem("act_passed")
        block = ctx.enter_context(nc.Block())

        @block.gpsimd
        def _(pool):
            pool.memset(pick[:, :, :], 0.0).then_inc(picked, 1)
            for k in range(3):
                pool.wait_ge(picked, k + 1)
                pool.affine_select(out=pick[:, :, :], in_=pick[:, :, :], compare_op=ALU.not_equal, fill=1.0,
                                   base=-32 * k, pattern=[[-1, 2 * STATES], [0, P]],
                                   channel_multiplier=1).then_inc(picked, 1)

        @block.tensor
        def _(pe):
            pe.wait_ge(g.weights, g.weights_due)
            for i in range(4 * GROUPS):
                m, c = divmod(i, GROUPS)
                if i >= 8:
                    pe.wait_ge(proj_used, i - 7)
                pe.matmul(g.bank[i % 8][:, :], w_in[:, m * P:(m + 1) * P], g.xnT[:, tok(c)],
                          start=True, stop=True).then_inc(proj_ready, 1)
            pe.wait_ge(u_ready, HALVES)
            for c in range(GROUPS):
                pe.wait_ge(proj_used, 9 + c)
                for h in range(HALVES):
                    mm = pe.matmul(g.bank[c][0:2 * STATES, :], w_bc[:, h, :], u[:, h, tok(c)],
                                   start=(h == 0), stop=(h == 1))
                mm.then_inc(bc_ready, 1)
            pe.wait_ge(proj_used, 4 * GROUPS)
            if rank_one_dt:
                for c in range(GROUPS):
                    for h in range(HALVES):
                        mm = pe.matmul(g.bank[4 + c][0:1, :], w_dtc[:, h:h + 1], u[:, h, tok(c)],
                                       start=(h == 0), stop=(h == 1))
                    mm.then_inc(row_ready, 1)
            pe.wait_ge(bc_split, 1)
            for i in range(HALVES * GROUPS):
                h, c = divmod(i, GROUPS)
                if rank_one_dt:
                    pe.wait_ge(row_copied, GROUPS)
                    pe.matmul(g.bank[i][:, :], w_dt[0:1, h * P:(h + 1) * P], dt_row[0:1, tok(c)],
                              start=True, stop=True).then_inc(dt_psum, 1)
                else:
                    for k in range(HALVES):
                        mm = pe.matmul(g.bank[i][:, :], w_dt[:, k, h * P:(h + 1) * P], u[:, k, tok(c)],
                                       start=(k == 0), stop=(k == 1))
                    mm.then_inc(dt_psum, 1)
            pe.wait_ge(dt_biased, HALVES * GROUPS)
            pe.wait_ge(bc_moved, 2)
            pe.wait_ge(picked, 4)
            with pe.Fori(0, GROUPS) as c:
                def sum_state(s):
                    pe.wait_ge(hc_ready, c * STATES + (s + 1))
                    if s == 0:
                        pe.wait_ge(sum_used, c + 1)
                    for h in range(HALVES):
                        mm = pe.matmul(g.bank[4 + h][:, :], g.ident[:, :], hc[:, s % 2, h, :],
                                       start=(s == 0), stop=(s == STATES - 1))
                    mm.then_inc(hc_used, 1)
                    if s == STATES - 1:
                        pe.wait_ge(hc_used, c * STATES + (s + 3))
                        pe.sem_inc(sum_ready, 1)
                for s in range(STATES):
                    b = s % 2
                    pe.wait_ge(spread_used, c * STATES + (s + 1))
                    pe.matmul(g.bank[b][:, :], pick[:, s, :], bc3[:, bass.ts(c, GROUP)], start=True, stop=True)
                    pe.matmul(g.bank[2 + b][:, :], pick[:, STATES + s, :], bc3[:, bass.ts(c, GROUP)],
                              start=True, stop=True).then_inc(spread_ready, 1)
                    if s >= 1:
                        sum_state(s - 1)
                sum_state(STATES - 1)
                pe.wait_ge(y_ready, c + 1)
                pe.wait_ge(out_used, c + 1)
                for i in range(TPG):
                    for h in range(HALVES):
                        mm = pe.matmul(g.bank[6][:, i * P:(i + 1) * P], y[:, h, i * P:(i + 1) * P], w_out[:, h, :],
                                       start=(h == 0), stop=(h == 1))
                mm.then_inc(out_ready, 1)

        @block.scalar
        def _(act):
            own = Chain(act, act_own)
            act.wait_ge(prepared, 1)
            for i in range(4 * GROUPS):
                m, c = divmod(i, GROUPS)
                act.wait_ge(proj_ready, i + 1)
                if m < 2:
                    act.activation(xpad[:, m, SPG * c:SPG * (c + 1), TAPS - 1:],
                                   g.bank[i % 8][:, :].rearrange("p (b t) -> p b t", t=T), ACT.Copy).then_inc(proj_used, 1)
                else:
                    act.activation(sz[:, m - 2, tok(c)], g.bank[i % 8][:, :], ACT.Silu).then_inc(proj_used, 1)
            for h in range(HALVES):
                act.wait_ge(conv_ready, h + 1)
                act.activation(u[:, h, :], cv[:, h, :], ACT.Silu, bias=conv_b[:, h:h + 1]).then_inc(u_ready, 1)
            if rank_one_dt:
                for c in range(GROUPS):
                    act.wait_ge(row_ready, c + 1)
                    act.activation(dt_row[0:1, tok(c)], g.bank[4 + c][0:1, :], ACT.Copy).then_inc(row_copied, 1)
            act.wait_ge(bc_split, 1)
            act.activation(bc3[32:64, :], part[:, 1, :], ACT.Copy).then_inc(bc_moved, 1)
            for i in range(HALVES * GROUPS):
                h, c = divmod(i, GROUPS)
                act.wait_ge(dt_psum, i + 1)
                act.activation(dt[:, h, tok(c)], g.bank[i][:, :], ACT.Identity, bias=b_dt[:, h:h + 1]).then_inc(dt_biased, 1)
            act.preload_act_table_set(LN_EXP)
            for h in range(HALVES):
                act.wait_ge(dt_biased, GROUPS * (h + 1))
                own.step(act.activation(cv[:, h, :], dt[:, h, :], ACT.Abs))
                own.step(act.activation(cv[:, h, :], cv[:, h, :], ACT.Exp, scale=-1.0))
                act.activation(cv[:, h, :], cv[:, h, :], ACT.Ln, bias=g.one[:, 0:1]).then_inc(log_ready, 1)
            act.activation(a_neg[:, :, :], a_log[:, :, :], ACT.Exp).then_inc(a_exp, 1)
            act.wait_ge(scan_inputs, 1)
            with act.Fori(0, GROUPS) as c:
                for s in range(STATES):
                    wait_apart(act, decay_used, c * STATES + (s + 1), act_passed)
                    for h in range(HALVES):
                        ins = act.activation(
                            decay[:, s % 2, h, :, 1:T],
                            dt[:, h, bass.ts(c, GROUP)].rearrange("p (b t) -> p b t", t=T)[:, :, 1:T],
                            ACT.Exp, scale=a_neg[:, h, s:s + 1])
                    ins.then_inc(decay_ready, 1)

        @block.vector
        def _(dve):
            own = Chain(dve, dve_own)
            own.add(dve.memset(xpad[:, :, :, 0:TAPS - 1], 0.0))
            own.add(dve.memset(decay[:, :, :, :, 0:1], 0.0))
            own.settle()
            dve.sem_inc(prepared, 1)
            for h in range(HALVES):
                dve.wait_ge(proj_used, GROUPS * (h + 1))
                cvh = cv[:, h, :].rearrange("p (b t) -> p b t", t=T)
                own.step(dve.tensor_scalar(cvh, xpad[:, h, :, 0:T], conv_w[:, h, 0:1], None, ALU.mult))
                for k in range(1, TAPS):
                    ins = dve.scalar_tensor_tensor(out=cvh, in0=xpad[:, h, :, k:k + T], scalar=conv_w[:, h, k:k + 1],
                                                   in1=cvh, op0=ALU.mult, op1=ALU.add)
                    if k < TAPS - 1:
                        own.step(ins)
                ins.then_inc(conv_ready, 1)
            for c in range(GROUPS):
                dve.wait_ge(bc_ready, c + 1)
                own.step(dve.tensor_copy(bc3[0:32, tok(c)], g.bank[c][0:32, :]))
                own.add(dve.tensor_tensor(rest[:, 0, tok(c)], g.bank[c][0:32, :], bc3[0:32, tok(c)], ALU.subtract))
            own.settle()
            own.step(dve.tensor_copy(part[:, 1, :], rest[:, 0, :]))
            dve.tensor_tensor(bc3[64:96, :], rest[:, 0, :], part[:, 1, :], ALU.subtract).then_inc(bc_split, 1)
            dve.wait_ge(bc_split, 1)
            dve.sem_inc(bc_moved, 1)
            for h in range(HALVES):
                dve.wait_ge(log_ready, h + 1)
                own.step(dve.scalar_tensor_tensor(out=dt[:, h, :], in0=dt[:, h, :], scalar=0.0, in1=cv[:, h, :],
                                                  op0=ALU.max, op1=ALU.add))
                own.add(dve.tensor_tensor(du[:, h, :], dt[:, h, :], u[:, h, :], ALU.mult))
            dve.wait_ge(a_exp, 1)
            own.step(dve.tensor_scalar(a_neg[:, :, :], a_neg[:, :, :], -1.0, None, ALU.mult))
            dve.sem_inc(scan_inputs, 1)
            for free, n in ((decay_used, 2), (spread_used, 2), (hc_used, 2), (sum_used, 1), (out_used, 1)):
                dve.sem_inc(free, n)
            STEPS_PER_GROUP = 4 * STATES + HALVES
            with dve.Fori(0, GROUPS) as c:
                own = Chain(dve, dve_own, c * STEPS_PER_GROUP + own.count)
                for s in range(STATES):
                    b = s % 2
                    dve.wait_ge(spread_ready, c * STATES + (s + 1))
                    for h in range(HALVES):
                        own.add(dve.tensor_tensor(dbu[:, h, :], du[:, h, bass.ts(c, GROUP)], g.bank[b][:, :], ALU.mult))
                    dve.wait_ge(decay_ready, c * STATES + (s + 1))
                    for h in range(HALVES):
                        own.settle(behind=1)
                        own.add(dve.tensor_tensor_scan(state[:, h, :], decay[:, b, h, :, :].rearrange("p b t -> p (b t)"),
                                                       dbu[:, h, :], 0.0, ALU.mult, ALU.add))
                    dve.wait_ge(hc_used, c * STATES + (s + 1))
                    for h in range(HALVES):
                        own.settle(behind=1 - h)
                        if h == 1:
                            dve.sem_inc(decay_used, 1)
                        ins = dve.tensor_tensor(hc[:, b, h, :], state[:, h, :], g.bank[2 + b][:, :], ALU.mult)
                    ins.then_inc(hc_ready, 1)
                    dve.wait_ge(hc_ready, c * STATES + (s + 1))
                    dve.sem_inc(spread_used, 1)
                dve.wait_ge(sum_ready, c + 1)
                for h in range(HALVES):
                    own.add(dve.scalar_tensor_tensor(out=state[:, h, :], in0=u[:, h, bass.ts(c, GROUP)],
                                                     scalar=skip[:, h:h + 1], in1=g.bank[4 + h][:, :],
                                                     op0=ALU.mult, op1=ALU.add))
                own.settle()
                dve.sem_inc(sum_used, 1)
                for h in range(HALVES):
                    ins = dve.tensor_tensor(y[:, h, :], state[:, h, :], sz[:, h, bass.ts(c, GROUP)], ALU.mult)
                ins.then_inc(y_ready, 1)
                dve.wait_ge(out_ready, c + 1)
                x_c = g.x[:, bass.ts(c, TPG), :]
                dve.tensor_tensor(x_c, x_c, g.bank[6][:, :].rearrange("p (n d) -> p n d", d=D), ALU.add).then_inc(out_used, 1)
                assert own.count == STEPS_PER_GROUP


def route(nc, g, tag, experts, gates, gates_t, gates3, gate_w, bias, sigmoid_scores):
    E = experts
    with ExitStack() as ctx:
        sem = ctx.enter_context(Signals(nc, tag))

        def sb(n, shape, dt=F32):
            return ctx.enter_context(nc.sbuf_tensor(f"{tag}_{n}", shape, dt))
        raw, ranked = sb("raw", [P, TILES, E]), sb("ranked", [P, TILES, E])
        top, top_index = sb("top", [P, TILES, 8]), sb("top_index", [P, TILES, 8], U32)
        index = sb("index", [P, TILES, 8])
        number = sb("number", [P, TILES, E])
        first, second = sb("first", [P, TILES, E]), sb("second", [P, TILES, E])
        soft, weight = sb("soft", [P, TILES, E]), sb("weight", [P, 4, TILES])
        rest, part = sb("rest", [32, N]), sb("part", [32, N], BF16)
        logits, numbered, exp_in, exp_out = sem("logits"), sem("numbered"), sem("exp_in"), sem("exp_out")
        gated, turned, split, own_sem = sem("gated"), sem("turned"), sem("split"), sem("dve")
        block = ctx.enter_context(nc.Block())

        @block.gpsimd
        def _(pool):
            pool.iota(number[:, :, :], pattern=[[0, TILES], [1, E]], base=0, channel_multiplier=0,
                      allow_small_or_imprecise_dtypes=True).then_inc(numbered, 1)

        @block.tensor
        def _(pe):
            pe.wait_ge(g.weights, g.weights_due)
            for t in range(TILES):
                mm = pe.matmul(g.bank[0][:, t * E:(t + 1) * E], g.xnT[:, t * P:(t + 1) * P], gate_w,
                               start=(t == 0), stop=(t == TILES - 1), skip_group_check=True)
            mm.then_inc(logits, 1)
            pe.wait_ge(gated, 1)
            for t in range(TILES):
                mm = pe.transpose(g.bank[1 + t // TPG][0:E, (t % TPG) * P:(t % TPG + 1) * P], gates[:, t, :], g.ident[:, :])
            mm.then_inc(turned, 1)

        @block.scalar
        def _(act):
            act.wait_ge(exp_in, 1)
            if sigmoid_scores:
                act.activation(soft[:, :, :], raw[:, :, :], ACT.Exp, scale=-1.0).then_inc(exp_out, 1)
            else:
                act.activation(weight[:, 1, :], weight[:, 0, :], ACT.Exp).then_inc(exp_out, 1)
            act.wait_ge(split, 1)
            act.activation(gates3[32:64, :], part[:, :], ACT.Copy)

        @block.vector
        def _(dve):
            own = Chain(dve, own_sem)
            own.add(dve.memset(gates3[:, :], 0.0))
            own.add(dve.memset(gates_t[:, :], 1.0))
            own.add(dve.memset(part[:, :], 0.0))
            own.add(dve.memset(rest[:, :], 0.0))
            dve.wait_ge(logits, 1)
            lg = g.bank[0][:, 0:TILES * E].rearrange("p (n e) -> p n e", e=E)
            own.add(dve.tensor_copy(raw[:, :, :], lg))
            own.step(dve.tensor_tensor(ranked[:, :, :], lg, bias.unsqueeze(1).to_broadcast([P, TILES, E]), ALU.add))
            for t in range(TILES):
                own.add(dve.max(top[:, t, :], ranked[:, t, :]))
            own.settle()
            for t in range(TILES):
                own.add(dve.max_index(top_index[:, t, :], top[:, t, :], ranked[:, t, :]))
            own.settle()
            own.step(dve.tensor_copy(index[:, :, :], top_index[:, :, :]))
            dve.wait_ge(numbered, 1)
            own.add(dve.tensor_tensor(first[:, :, :], number[:, :, :], spread(index[:, :, 0], E), ALU.is_equal))
            own.add(dve.tensor_tensor(second[:, :, :], number[:, :, :], spread(index[:, :, 1], E), ALU.is_equal))
            own.settle()
            if sigmoid_scores:
                dve.sem_inc(exp_in, 1)
                own.step(dve.tensor_tensor(first[:, :, :], first[:, :, :], second[:, :, :], ALU.add))
                dve.wait_ge(exp_out, 1)
                own.step(dve.tensor_scalar(soft[:, :, :], soft[:, :, :], 1.0, None, ALU.add))
                own.step(dve.reciprocal(soft[:, :, :], soft[:, :, :]))
                own.step(dve.tensor_tensor(soft[:, :, :], soft[:, :, :], first[:, :, :], ALU.mult))
                own.step(dve.tensor_reduce(weight[:, 0, :], soft[:, :, :], AX.X, ALU.add))
                own.step(dve.tensor_scalar(weight[:, 1, :], weight[:, 0, :], 1e-10, None, ALU.add))
                own.step(dve.reciprocal(weight[:, 2, :], weight[:, 1, :]))
                own.step(dve.tensor_tensor(gates[:, :, :], soft[:, :, :], spread(weight[:, 2, :], E), ALU.mult))
            else:
                own.step(dve.tensor_tensor(weight[:, 0, :], top[:, :, 1], top[:, :, 0], ALU.subtract))
                dve.sem_inc(exp_in, 1)
                dve.wait_ge(exp_out, 1)
                own.step(dve.tensor_scalar(weight[:, 2, :], weight[:, 1, :], 1.0, None, ALU.add))
                own.step(dve.reciprocal(weight[:, 3, :], weight[:, 2, :]))
                own.step(dve.tensor_tensor(weight[:, 2, :], weight[:, 1, :], weight[:, 3, :], ALU.mult))
                own.add(dve.tensor_tensor(first[:, :, :], first[:, :, :], spread(weight[:, 3, :], E), ALU.mult))
                own.step(dve.tensor_tensor(second[:, :, :], second[:, :, :], spread(weight[:, 2, :], E), ALU.mult))
                own.step(dve.tensor_tensor(gates[:, :, :], first[:, :, :], second[:, :, :], ALU.add))
            dve.sem_inc(gated, 1)
            dve.wait_ge(turned, 1)
            for c in range(GROUPS):
                own.add(dve.tensor_copy(gates_t[0:E, tok(c)], g.bank[1 + c][0:E, :]))
            own.settle()
            own.step(dve.tensor_copy(gates3[0:E, :], gates_t[0:E, :]))
            own.step(dve.tensor_tensor(rest[0:E, :], gates_t[0:E, :], gates3[0:E, :], ALU.subtract))
            own.step(dve.tensor_copy(part[0:E, :], rest[0:E, :]))
            dve.tensor_tensor(gates3[64:96, :], rest[:, :], part[:, :], ALU.subtract).then_inc(split, 1)


def moe(nc, g, tag, d_in, experts, chunks, gate_of, biased, sigmoid_scores, domains):
    E = experts
    gated_mlp = "w1" in d_in
    SETS = max((gate_of(j) for j in range(chunks) if gate_of(j) is not None)) + 1
    HALF_SETS = SETS * 2 == E
    with ExitStack() as ctx:
        sem = ctx.enter_context(Signals(nc, tag))

        def sb(n, shape, dt=F32):
            return ctx.enter_context(nc.sbuf_tensor(f"{tag}_{n}", shape, dt))
        gate_w, gate_b = sb("gate_w", [P, E]), sb("gate_b", [P, E])
        w2 = sb("w2", [P, chunks, D])
        loads = [(gate_w[:, :], d_in["gate_w"]), (w2[:, :, :], d_in["w2"])]
        if "gate_b" in d_in:
            loads.append((gate_b[:, :], d_in["gate_b"]))
        if gated_mlp:
            w1, w3 = sb("w1", [P, chunks, P]), sb("w3", [P, chunks, P])
            loads += [(w1[:, :, :], d_in["w1"]), (w3[:, :, :], d_in["w3"])]
            b1, b3 = sb("b1", [P, chunks]), sb("b3", [P, chunks])
            if domains:
                dom = sb("dom", [P, E])
                loads.append((dom[:, :], d_in["dom"]))
            else:
                loads += [(b1[:, :], d_in["b1"]), (b3[:, :], d_in["b3"])]
        B_ROWS = 0
        if biased:
            B_ROWS = d_in["b2"].shape[0]
            b2 = sb("b2", [B_ROWS, D])
            loads.append((b2[:, :], d_in["b2"]))
        norm_and_turn(nc, g, tag + "_ln", loads)

        gates, gates_t = sb("gates", [P, TILES, E]), sb("gates_t", [32, N])
        gates3 = sb("gates3", [96, N], BF16)
        pick = sb("pick", [96, SETS, P], BF16)
        zero_b = sem("no_bias")
        if "gate_b" not in d_in:
            with nc.Block() as block:
                @block.gpsimd
                def _(pool):
                    pool.memset(gate_b[:, :], 0.0).then_inc(zero_b, 1)
        route(nc, g, tag + "_route", E, gates, gates_t, gates3, gate_w[:, :], gate_b[:, :], sigmoid_scores)

        silu = sb("silu", [P, 2, GROUP])
        prod = sb("prod", [P, 2, GROUP])
        gated = sb("gated", [P, 2, GROUP])
        gt_c = sb("gt_c", [32, GROUP])
        picked, hidden_ready, silu_ready, hidden_used = sem("picked"), sem("hidden_ready"), sem("silu_ready"), sem("hidden_used")
        spread_ready, spread_used, gated_ready, gated_used = sem("spread_ready"), sem("spread_used"), sem("gated_ready"), sem("gated_used")
        sum_ready, sum_used, gt_ready, gt_used = sem("sum_ready"), sem("sum_used"), sem("gt_ready"), sem("gt_used")
        dom_ready, dom_copied, dve_own, act_passed = sem("dom_ready"), sem("dom_copied"), sem("dve"), sem("act_passed")
        spread_at = {}
        for j in range(chunks):
            if gate_of(j) is not None:
                spread_at[j] = gate_of(j)
        last_use = {s: max(j for j in spread_at if spread_at[j] == s) for s in range(SETS)}
        assert SETS % 2 == 0 and chunks >= 2
        block = ctx.enter_context(nc.Block())

        @block.gpsimd
        def _(pool):
            pool.memset(pick[:, :, :], 0.0).then_inc(picked, 1)
            for k in range(3):
                pool.wait_ge(picked, k + 1)
                if HALF_SETS:
                    out = pick[:, :, :].rearrange("k s (h p) -> k s h p", h=2)
                    pattern = [[-2, SETS], [-1, 2], [0, P // 2]]
                else:
                    out, pattern = pick[:, :, :], [[-1, SETS], [0, P]]
                pool.affine_select(out=out, in_=out, compare_op=ALU.not_equal, fill=1.0, base=-32 * k,
                                   pattern=pattern, channel_multiplier=1).then_inc(picked, 1)

        @block.tensor
        def _(pe):
            if domains:
                for k, w in enumerate((w1, w3)):
                    for j in range(chunks):
                        e = gate_of(j)
                        mm = pe.matmul(g.bank[7][:, k * chunks + j:k * chunks + j + 1], w[:, j, :], dom[:, e:e + 1],
                                       start=(j == 0 and k == 0), stop=(j == chunks - 1 and k == 1), skip_group_check=True)
                mm.then_inc(dom_ready, 1)
            pe.wait_ge(picked, 4)
            with pe.Fori(0, GROUPS) as c:
                def add_chunk(j):
                    pe.wait_ge(gated_ready, c * chunks + (j + 1))
                    if j == 0:
                        pe.wait_ge(sum_used, c + 1)
                    for i in range(TPG):
                        mm = pe.matmul(g.bank[6][:, i * P:(i + 1) * P], gated[:, j % 2, i * P:(i + 1) * P],
                                       w2[:, j, :], start=(j == 0 and i == 0),
                                       stop=(not biased and j == chunks - 1), skip_group_check=True)
                    mm.then_inc(gated_used, 1)
                for j in range(chunks):
                    b = j % 2
                    if j in spread_at and (j == 0 or spread_at[j] != spread_at.get(j - 1)):
                        s = spread_at[j]
                        pe.wait_ge(spread_used, c * SETS + (s + 1))
                        pe.matmul(g.bank[4 + s % 2][:, :], pick[:, s, :], gates3[:, bass.ts(c, GROUP)],
                                  start=True, stop=True).then_inc(spread_ready, 1)
                    if gated_mlp:
                        pe.wait_ge(hidden_used, c * chunks + (j + 1))
                        pe.matmul(g.bank[b][:, :], w1[:, j, :], g.xnT[:, bass.ts(c, GROUP)], start=True, stop=True)
                        pe.matmul(g.bank[2 + b][:, :], w3[:, j, :], g.xnT[:, bass.ts(c, GROUP)],
                                  start=True, stop=True).then_inc(hidden_ready, 1)
                    if j >= 1:
                        add_chunk(j - 1)
                add_chunk(chunks - 1)
                if biased:
                    pe.wait_ge(gt_ready, c + 1)
                    for i in range(TPG):
                        mm = pe.matmul(g.bank[6][:, i * P:(i + 1) * P], gt_c[0:B_ROWS, i * P:(i + 1) * P], b2[:, :],
                                       start=False, stop=True, skip_group_check=True)
                    mm.then_inc(sum_ready, 1)
                else:
                    pe.wait_ge(gated_used, c * chunks + (chunks + 2))
                    pe.sem_inc(sum_ready, 1)

        @block.scalar
        def _(act):
            if domains:
                act.wait_ge(dom_ready, 1)
                act.activation(b1[:, :], g.bank[7][:, 0:chunks], ACT.Copy).then_inc(dom_copied, 1)
                act.activation(b3[:, :], g.bank[7][:, chunks:2 * chunks], ACT.Copy).then_inc(dom_copied, 1)
                act.wait_ge(dom_copied, 2)
            with act.Fori(0, GROUPS) as c:
                if biased:
                    wait_apart(act, gt_used, c + 1, act_passed)
                    act.activation(gt_c[:, :], gates_t[:, bass.ts(c, GROUP)], ACT.Copy).then_inc(gt_ready, 1)
                if gated_mlp:
                    for j in range(chunks):
                        act.wait_ge(hidden_used, c * chunks + (j + 1))
                        act.wait_ge(hidden_ready, c * chunks + (j + 1))
                        act.activation(silu[:, j % 2, :], g.bank[j % 2][:, :], ACT.Silu,
                                       bias=b1[:, j:j + 1]).then_inc(silu_ready, 1)

        @block.vector
        def _(dve):
            for free, n in ((spread_used, 2), (hidden_used, 2), (gated_used, 2), (sum_used, 1), (gt_used, 1)):
                dve.sem_inc(free, n)
            if domains:
                dve.wait_ge(dom_copied, 2)
            with dve.Fori(0, GROUPS) as c:
                for j in range(chunks):
                    b = j % 2
                    if gated_mlp:
                        dve.wait_ge(silu_ready, c * chunks + (j + 1))
                        if j >= 2:
                            dve.wait_ge(gated_ready, c * chunks + (j - 1))
                        if j not in spread_at:
                            dve.wait_ge(gated_used, c * chunks + (j + 1))
                        source = prod[:, b, :] if j in spread_at else gated[:, b, :]
                        dve.scalar_tensor_tensor(out=source, in0=g.bank[2 + b][:, :], scalar=b3[:, j:j + 1],
                                                 in1=silu[:, b, :], op0=ALU.add, op1=ALU.mult).then_inc(hidden_used, 1)
                        dve.wait_ge(hidden_used, c * chunks + (j + 3))
                    else:
                        source = g.xnT[:, bass.ts(c, GROUP)]
                    if j in spread_at:
                        s = spread_at[j]
                        dve.wait_ge(spread_ready, c * SETS + (s + 1))
                        dve.wait_ge(gated_used, c * chunks + (j + 1))
                        dve.tensor_tensor(gated[:, b, :], source, g.bank[4 + s % 2][:, :], ALU.mult).then_inc(gated_ready, 1)
                        if last_use[s] == j:
                            dve.wait_ge(gated_ready, c * chunks + (j + 1))
                            dve.sem_inc(spread_used, 1)
                    else:
                        dve.sem_inc(gated_ready, 1)
                dve.wait_ge(sum_ready, c + 1)
                x_c = g.x[:, bass.ts(c, TPG), :]
                dve.tensor_tensor(x_c, x_c, g.bank[6][:, :].rearrange("p (n d) -> p n d", d=D), ALU.add).then_inc(sum_used, 1)
                if biased:
                    dve.sem_inc(gt_used, 1)


def two_pi_parts():
    parts, rest = [], 2 * np.pi
    for bits in (8, 11, 24):
        unit = 2.0 ** (np.floor(np.log2(rest)) + 1 - bits)
        parts.append(float(np.floor(rest / unit) * unit))
        rest -= parts[-1]
    return parts


def rotor_memory(nc, g, d_in):
    TWO_PI = two_pi_parts()
    ROUND = 1.5 * 2.0 ** 23
    PI_DOWN = 3.1415925
    with ExitStack() as ctx:
        sem = ctx.enter_context(Signals(nc, "rotor"))

        def sb(n, shape, dt=F32):
            return ctx.enter_context(nc.sbuf_tensor(f"rotor_{n}", shape, dt))
        w_v, w_o, freqs = sb("w_v", [P, P]), sb("w_o", [P, P]), sb("freqs", [P, 1])
        norm_and_turn(nc, g, "rotor_ln", [(w_v[:, :], d_in["w_v"]), (w_o[:, :], d_in["w_o"]), (freqs[:, :], d_in["freqs"])])
        time, theta = sb("time", [P, T]), sb("theta", [P, T])
        turns, angle = sb("turns", [P, 2, T]), sb("angle", [P, 2, T])
        table = sb("table", [P, 2, T])
        keep = sb("keep", [P, SPG, T])
        term, total = sb("term", [P, 2, N]), sb("total", [P, 2, N])
        found = sb("found", [P, N])
        timed, angles, tables = sem("timed"), sem("angles"), sem("tables")
        v_ready, found_ready, out_ready, dve_own = sem("v_ready"), sem("found_ready"), sem("out_ready"), sem("dve")
        block = ctx.enter_context(nc.Block())

        @block.gpsimd
        def _(pool):
            pool.iota(time[:, :], pattern=[[1, T]], base=0, channel_multiplier=0,
                      allow_small_or_imprecise_dtypes=True).then_inc(timed, 1)

        @block.scalar
        def _(act):
            act.wait_ge(angles, 1)
            act.activation(table[:, :, :], angle[:, :, :], ACT.Sin).then_inc(tables, 1)

        @block.tensor
        def _(pe):
            pe.wait_ge(g.weights, g.weights_due)
            for c in range(GROUPS):
                pe.matmul(g.bank[c][:, :], w_v[:, :], g.xnT[:, tok(c)], start=True, stop=True).then_inc(v_ready, 1)
            for c in range(GROUPS):
                pe.wait_ge(found_ready, c + 1)
                for i in range(TPG):
                    mm = pe.matmul(g.bank[4 + c][:, i * P:(i + 1) * P], found[:, c * GROUP + i * P:c * GROUP + (i + 1) * P],
                                   w_o[:, :], start=True, stop=True)
                mm.then_inc(out_ready, 1)

        @block.vector
        def _(dve):
            own = Chain(dve, dve_own)
            own.step(dve.memset(keep[:, :, :], 1.0))
            own.add(dve.memset(keep[:, :, 0:1], 0.0))
            dve.wait_ge(timed, 1)
            dve.wait_ge(g.weights, g.weights_due)
            own.step(dve.tensor_scalar(theta[:, :], time[:, :], freqs[:, 0:1], None, ALU.mult))
            for q in range(2):
                own.add(dve.tensor_scalar(turns[:, q, :], theta[:, :], 1 / (2 * np.pi), 0.25 * q, ALU.mult, ALU.add))
            own.settle()
            own.step(dve.tensor_scalar(turns[:, :, :], turns[:, :, :], ROUND, None, ALU.add))
            own.step(dve.tensor_scalar(turns[:, :, :], turns[:, :, :], ROUND, None, ALU.subtract))
            theta2 = theta[:, :].unsqueeze(1).to_broadcast([P, 2, T])
            for k, part in enumerate(TWO_PI):
                own.step(dve.scalar_tensor_tensor(out=angle[:, :, :], in0=turns[:, :, :], scalar=-part,
                                                  in1=theta2 if k == 0 else angle[:, :, :], op0=ALU.mult, op1=ALU.add))
            own.step(dve.tensor_scalar(angle[:, 1, :], angle[:, 1, :], np.pi / 2, None, ALU.add))
            dve.tensor_scalar(angle[:, :, :], angle[:, :, :], PI_DOWN, -PI_DOWN, ALU.min, ALU.max).then_inc(angles, 1)
            dve.wait_ge(tables, 1)
            for c in range(GROUPS):
                dve.wait_ge(v_ready, c + 1)
                v = g.bank[c][:, :].rearrange("p (b t) -> p b t", t=T)

                def per_seq(buf, q):
                    return buf[:, q, tok(c)].rearrange("p (b t) -> p b t", t=T)
                tables2 = [table[:, q, :].unsqueeze(1).to_broadcast([P, SPG, T]) for q in range(2)]
                for q in range(2):
                    own.add(dve.tensor_tensor(per_seq(term, q), v, tables2[q], ALU.mult))
                for q in range(2):
                    own.settle(behind=1)
                    own.add(dve.tensor_tensor_scan(total[:, q, tok(c)], keep[:, :, :].rearrange("p b t -> p (b t)"),
                                                   term[:, q, tok(c)], 0.0, ALU.mult, ALU.add))
                for q in range(2):
                    own.settle(behind=1)
                    own.add(dve.tensor_tensor(per_seq(term, q), per_seq(total, q), tables2[q], ALU.mult))
                own.settle()
                dve.tensor_tensor(found[:, tok(c)], term[:, 0, tok(c)], term[:, 1, tok(c)], ALU.add).then_inc(found_ready, 1)
            for c in range(GROUPS):
                dve.wait_ge(out_ready, c + 1)
                x_c = g.x[:, TPG * c:TPG * (c + 1), :]
                dve.tensor_tensor(x_c, x_c, g.bank[4 + c][:, :].rearrange("p (n d) -> p n d", d=D), ALU.add)


def delta_rule(nc, g, d_in):
    HEADS, TAPS, C, QUAD, LEVELS, DUO = 8, 4, P, 4, 7, 2
    QUADS = TILES // QUAD
    with ExitStack() as ctx:
        sem = ctx.enter_context(Signals(nc, "delta"))

        def sb(n, shape, dt=F32):
            return ctx.enter_context(nc.sbuf_tensor(f"delta_{n}", shape, dt))
        w_qkv, w_z, w_o = sb("w_qkv", [P, HEADS, 3, P]), sb("w_z", [P, HEADS, P]), sb("w_o", [P, HEADS, D])
        taps = sb("taps", [P, HEADS, 3, TAPS])
        w_ab, ab_bias = sb("w_ab", [P, 2 * HEADS]), sb("ab_bias", [P, 2 * HEADS])
        a_log, norm_w = sb("a_log", [P, HEADS]), sb("norm_w", [P, 1])
        norm_and_turn(nc, g, "delta_ln", [
            (w_ab[:, :], d_in["w_ab"]), (ab_bias[:, :], d_in["ab_bias"]), (a_log[:, :], d_in["a_log"]),
            (norm_w[:, :], d_in["norm_w"]), (taps[:, :, :, :], d_in["taps"]), (w_qkv[:, :, :, :], d_in["w_qkv"]),
            (w_z[:, :, :], d_in["w_z"]), (w_o[:, :, :], d_in["w_o"])])
        beta = sb("beta", [P, TILES, HEADS])
        alpha3 = sb("alpha3", [96, N], BF16)

        with ExitStack() as inner:
            sem1 = inner.enter_context(Signals(nc, "delta_ab"))

            def sb1(n, shape, dt=F32):
                return inner.enter_context(nc.sbuf_tensor(f"delta_ab_{n}", shape, dt))
            ab, soft = sb1("ab", [P, TILES, 2 * HEADS]), sb1("soft", [P, TILES, HEADS])
            rate, alpha = sb1("rate", [P, HEADS]), sb1("alpha", [P, TILES, HEADS])
            sig = sb1("sig", [P, TILES, HEADS])
            alpha_t, rest, part = sb1("alpha_t", [32, N]), sb1("rest", [32, N]), sb1("part", [32, N], BF16)
            projected, biased, softened, rated = sem1("projected"), sem1("biased"), sem1("softened"), sem1("rated")
            alpha_ready, turned, split = sem1("alpha_ready"), sem1("turned"), sem1("split")
            act_own, dve_own = sem1("act"), sem1("dve")
            block = inner.enter_context(nc.Block())

            @block.tensor
            def _(pe):
                pe.wait_ge(g.weights, g.weights_due)
                for t in range(TILES):
                    mm = pe.matmul(g.bank[0][:, t * 16:(t + 1) * 16], g.xnT[:, t * P:(t + 1) * P], w_ab[:, :],
                                   start=(t == 0), stop=(t == TILES - 1), skip_group_check=True)
                mm.then_inc(projected, 1)
                pe.wait_ge(alpha_ready, 1)
                for t in range(TILES):
                    mm = pe.transpose(g.bank[1 + t // TPG][0:HEADS, (t % TPG) * P:(t % TPG + 1) * P], alpha[:, t, :],
                                      g.ident[:, :])
                mm.then_inc(turned, 1)

            @block.scalar
            def _(act):
                own = Chain(act, act_own)
                act.preload_act_table_set(LN_EXP)
                act.wait_ge(g.weights, g.weights_due)
                own.add(act.activation(rate[:, :], a_log[:, :], ACT.Exp))
                act.wait_ge(biased, 1)
                own.add(act.activation(sig[:, :, :], ab[:, :, HEADS:], ACT.Exp, scale=-1.0))
                own.step(act.activation(soft[:, :, :], ab[:, :, 0:HEADS], ACT.Abs))
                own.step(act.activation(soft[:, :, :], soft[:, :, :], ACT.Exp, scale=-1.0))
                act.activation(soft[:, :, :], soft[:, :, :], ACT.Ln, bias=g.one[:, 0:1]).then_inc(softened, 1)
                act.wait_ge(rated, 1)
                act.activation(alpha[:, :, :], soft[:, :, :], ACT.Exp, scale=-1.0).then_inc(alpha_ready, 1)
                act.wait_ge(split, 1)
                act.activation(alpha3[32:64, :], part[:, :], ACT.Copy)

            @block.vector
            def _(dve):
                own = Chain(dve, dve_own)
                own.add(dve.memset(alpha_t[:, :], 0.0))
                dve.wait_ge(projected, 1)
                dve.wait_ge(g.weights, g.weights_due)
                dve.tensor_tensor(ab[:, :, :], g.bank[0][:, 0:16 * TILES].rearrange("p (n e) -> p n e", e=16),
                                  ab_bias[:, :].unsqueeze(1).to_broadcast([P, TILES, 16]), ALU.add).then_inc(biased, 1)
                dve.wait_ge(softened, 1)
                own.step(dve.scalar_tensor_tensor(out=soft[:, :, :], in0=ab[:, :, 0:HEADS], scalar=0.0,
                                                  in1=soft[:, :, :], op0=ALU.max, op1=ALU.add))
                dve.tensor_tensor(soft[:, :, :], soft[:, :, :], rate[:, :].unsqueeze(1).to_broadcast([P, TILES, HEADS]),
                                  ALU.mult).then_inc(rated, 1)
                own.step(dve.tensor_scalar(sig[:, :, :], sig[:, :, :], 1.0, None, ALU.add))
                own.add(dve.reciprocal(beta[:, :, :], sig[:, :, :]))
                dve.wait_ge(turned, 1)
                for c in range(GROUPS):
                    own.add(dve.tensor_copy(alpha_t[0:HEADS, tok(c)], g.bank[1 + c][0:HEADS, :]))
                own.settle()
                own.step(dve.tensor_copy(alpha3[0:32, :], alpha_t[:, :]))
                own.step(dve.tensor_tensor(rest[:, :], alpha_t[:, :], alpha3[0:32, :], ALU.subtract))
                own.step(dve.tensor_copy(part[:, :], rest[:, :]))
                dve.tensor_tensor(alpha3[64:96, :], rest[:, :], part[:, :], ALU.subtract).then_inc(split, 1)

        pick = sb("pick", [96, HEADS, P], BF16)
        pick_h = sb("pick_h", [96, P], BF16)
        w_h, wz_h, wo_h = sb("w_h", [P, 3, P]), sb("wz_h", [P, P]), sb("wo_h", [P, D])
        taps_h, beta_h = sb("taps_h", [P, 3, TAPS]), sb("beta_h", [P, TILES])
        joint = sb("joint", [P, LEVELS, C])
        pad = sb("pad", [P, 3, BATCH, T + TAPS - 1])
        qkv = sb("qkv", [P, 3, N])
        alpha_in = sb("alpha_in", [P, TILES, C])
        alpha_first = sb("alpha_first", [P, TILES, C])
        grow = sb("grow", [P, TILES, C])
        kq_g = sb("kq_g", [P, 2, BATCH, C])
        diag, db = sb("diag", [P, DUO, QUAD, C]), sb("db", [P, DUO, QUAD, C])
        lt, at = sb("lt", [P, DUO, QUAD, C]), sb("at", [P, DUO, QUAD, C])
        lt_n = sb("lt_n", [P, DUO, QUAD, C])
        xi, xt, px = sb("xi", [P, DUO, QUAD, C]), sb("xt", [P, DUO, QUAD, C]), sb("px", [P, DUO, QUAD, C])
        v_tok, k_tok = sb("v_tok", [P, DUO, QUAD, C]), sb("k_tok", [P, DUO, 2, C])
        w_sol, s_one = sb("w_sol", [P, DUO, QUAD, C]), sb("s_one", [P, DUO, 2, C])
        sz, o_sq = sb("sz", [P, DUO, QUAD, C]), sb("o_sq", [P, DUO, QUAD, C])
        o_n, o_t = sb("o_n", [P, DUO, QUAD, C]), sb("o_t", [P, DUO, QUAD, C])
        stat = sb("stat", [P, DUO, 3, QUAD])
        eps_o = sb("eps_o", [P, 1])
        picked, masks = sem("picked"), sem("masks")
        staged, pe_head, dve_head, act_head = sem("staged"), sem("pe_head"), sem("dve_head"), sem("act_head")
        pads_zero = sem("pads_zero")
        proj_ready, proj_used, conv_ready = sem("proj_ready"), sem("proj_used"), sem("conv_ready")
        a_ready, a_copied, kq_ready = sem("a_ready"), sem("a_copied"), sem("kq_ready")
        scores_ready, lt_ready, at_ready = sem("scores_ready"), sem("lt_ready"), sem("at_ready")
        masked, masked_used = sem("masked"), sem("masked_used")
        p_ready, p_copied, xp_ready, x_ready, xpt_ready, xt_ready = (
            sem("p_ready"), sem("p_copied"), sem("xp_ready"), sem("x_ready"), sem("xpt_ready"), sem("xt_ready"))
        turned, tok_ready = sem("turned"), sem("tok_ready")
        ks_ready, rhs_ready = sem("ks_ready"), sem("rhs_ready")
        w_ready, w_copied, s_ready, s_copied = sem("w_ready"), sem("w_copied"), sem("s_ready"), sem("s_copied")
        z_ready, sz_ready, o_ready = sem("z_ready"), sem("sz_ready"), sem("o_ready")
        sq_ready, var_ready, rstd_ready, on_ready = sem("sq_ready"), sem("var_ready"), sem("rstd_ready"), sem("on_ready")
        ot_ready, ot_copied, out_ready, out_added = sem("ot_ready"), sem("ot_copied"), sem("out_ready"), sem("out_added")
        pool_own, dve_own, act_own = sem("pool"), sem("dve"), sem("act")
        HALVES = QUADS // DUO
        R = HALVES * DUO
        block = ctx.enter_context(nc.Block())

        def flat(buf, d):
            return buf[:, d, :, :].rearrange("p a c -> p (a c)")

        @block.gpsimd
        def _(pool):
            own = Chain(pool, pool_own)
            own.step(pool.memset(pick[:, :, :], 0.0))
            for k in range(3):
                own.step(pool.affine_select(out=pick[:, :, :], in_=pick[:, :, :], compare_op=ALU.not_equal, fill=1.0,
                                            base=-32 * k, pattern=[[-1, HEADS], [0, P]], channel_multiplier=1))
            own.step(pool.memset(joint[:, :, :], 0.0))
            for lv in range(LEVELS):
                n = 1 << lv
                view = joint[:, lv, :].rearrange("p (a two r) -> p a two r", two=2, r=n)[:, :, 1, :]
                own.step(pool.memset(view, 1.0))
                own.step(pool.affine_select(out=view, in_=view, compare_op=ALU.is_ge, fill=0.0, base=0,
                                            pattern=[[-2 * n, C // (2 * n)], [0, n]], channel_multiplier=1))
                own.step(pool.affine_select(out=view, in_=view, compare_op=ALU.is_gt, fill=0.0, base=n,
                                            pattern=[[2 * n, C // (2 * n)], [0, n]], channel_multiplier=-1))
            SETUP = own.count
            PER_HEAD = 6
            with pool.Fori(0, HEADS) as h:
                own = Chain(pool, pool_own, h * PER_HEAD + SETUP)
                for done in (pe_head, dve_head, act_head):
                    pool.wait_ge(done, h + 1)
                own.add(pool.tensor_copy(w_h[:, :, :], w_qkv[:, bass.ts(h, 1), :, :].rearrange("p a m c -> p (a m) c")))
                own.add(pool.tensor_copy(wz_h[:, :], w_z[:, bass.ts(h, 1), :].rearrange("p a c -> p (a c)")))
                own.add(pool.tensor_copy(wo_h[:, :], w_o[:, bass.ts(h, 1), :].rearrange("p a c -> p (a c)")))
                own.add(pool.tensor_copy(taps_h[:, :, :], taps[:, bass.ts(h, 1), :, :].rearrange("p a m c -> p (a m) c")))
                own.add(pool.tensor_copy(beta_h[:, :], beta[:, :, bass.ts(h, 1)].rearrange("p a c -> p (a c)")))
                own.step(pool.tensor_copy(pick_h[:, :], pick[:, bass.ts(h, 1), :].rearrange("p a c -> p (a c)")))
                pool.sem_inc(staged, 1)
                for half in range(HALVES):
                    for lv in range(LEVELS):
                        for d in range(DUO):
                            n = DUO * half + d
                            if lv == 0:
                                pool.wait_ge(lt_ready, h * R + (n + 1))
                            pool.wait_ge(masked_used, h * (R * LEVELS) + (half * DUO * LEVELS + lv * DUO + d + 1))
                            pool.tensor_tensor(lt_n[:, d, :, :], lt[:, d, :, :],
                                               joint[:, lv, :].unsqueeze(1).to_broadcast([P, QUAD, C]),
                                               ALU.mult).then_inc(masked, 1)

        @block.tensor
        def _(pe):
            def chunks(bank, lhs, rhs, signal, which=range(4), start=None, stop=True):
                for i in which:
                    mm = pe.matmul(bank[:, i * C:(i + 1) * C], lhs(i), rhs(i), start=True if start is None else start(i),
                                   stop=stop)
                mm.then_inc(signal, 1)

            with pe.Fori(0, HEADS) as h:
                pe.wait_ge(staged, h + 1)
                for i in range(3 * GROUPS):
                    m, c = divmod(i, GROUPS)
                    if i >= 8:
                        pe.wait_ge(proj_used, h * (3 * GROUPS) + (i - 7))
                    pe.matmul(g.bank[i % 8][:, :], w_h[:, m, :], g.xnT[:, tok(c)], start=True, stop=True).then_inc(proj_ready, 1)
                for c in range(GROUPS):
                    pe.wait_ge(proj_used, h * (3 * GROUPS) + (5 + c))
                    pe.matmul(g.bank[4 + c][:, :], pick_h[:, :], alpha3[:, tok(c)], start=True, stop=True).then_inc(a_ready, 1)
                pe.wait_ge(conv_ready, h * 3 + 3)
                pe.wait_ge(kq_ready, h + 1)
                pe.wait_ge(proj_used, h * (3 * GROUPS) + 3 * GROUPS)
                pe.wait_ge(a_copied, h * GROUPS + GROUPS)
                for half in range(HALVES):
                    for d in range(DUO):
                        at0 = (DUO * half + d) * GROUP

                        def seg(m, i, at0=at0):
                            return qkv[:, m, at0 + i * C:at0 + (i + 1) * C]
                        if half:
                            pe.wait_ge(out_added, h * R + DUO * (half - 1) + d + 1)
                        chunks(g.bank[d], lambda i: seg(1, i), lambda i: seg(1, i), scores_ready)
                        chunks(g.bank[2 + d], lambda i: seg(1, i), lambda i: seg(0, i), scores_ready)
                        for i in range(4):
                            mm = pe.transpose(g.bank[4 + d][:, i * C:(i + 1) * C], seg(2, i), g.ident[:, :])
                        mm.then_inc(turned, 1)
                        for i in (0, 2):
                            mm = pe.transpose(g.bank[6 + d][:, (i // 2) * C:(i // 2 + 1) * C], seg(1, i), g.ident[:, :])
                        mm.then_inc(turned, 1)
                    for lv in range(LEVELS):
                        for d in range(DUO):
                            n = R * LEVELS
                            it = half * DUO * LEVELS + lv * DUO + d
                            pe.wait_ge(masked, h * n + (it + 1))
                            if lv == 0:
                                pe.wait_ge(at_ready, h * R + (DUO * half + d + 1))
                                for i in range(4):
                                    mm = pe.transpose(g.bank[d][:, i * C:(i + 1) * C], lt_n[:, d, i, :], g.ident[:, :])
                                mm.then_inc(p_ready, 1)
                            else:
                                pe.wait_ge(x_ready, h * (R * (LEVELS - 1)) + (half * DUO * (LEVELS - 1) + (lv - 1) * DUO + d + 1))
                                chunks(g.bank[d], lambda i, d=d: lt_n[:, d, i, :], lambda i, d=d: xi[:, d, i, :], p_ready)
                        if lv == 0:
                            continue
                        for d in range(DUO):
                            it = half * DUO * LEVELS + lv * DUO + d
                            pe.wait_ge(p_copied, h * (R * LEVELS) + (it + 1))
                            pe.wait_ge(xt_ready, h * (R * LEVELS) + (it - DUO + 1))
                            if lv < LEVELS - 1:
                                chunks(g.bank[2 + d], lambda i, d=d: xt[:, d, i, :], lambda i, d=d: px[:, d, i, :], xp_ready)
                            if lv == 1:
                                pe.wait_ge(tok_ready, h * (2 * R) + (2 * (DUO * half + d) + 2))
                            chunks(g.bank[4 + d], lambda i, d=d: px[:, d, i, :], lambda i, d=d: xt[:, d, i, :], xpt_ready)
                    for d in range(DUO):
                        it = half * DUO * LEVELS + (LEVELS - 1) * DUO + d
                        pe.wait_ge(xt_ready, h * (R * LEVELS) + (it + 1))
                        chunks(g.bank[d], lambda i, d=d: xt[:, d, i, :], lambda i, d=d: v_tok[:, d, i, :], w_ready, (0, 2))
                    for d in range(DUO):
                        n = DUO * half + d
                        pe.wait_ge(w_copied, h * (2 * R) + (2 * DUO * half + d + 1))
                        chunks(g.bank[2 + d], lambda i, d=d: k_tok[:, d, i, :], lambda i, d=d: w_sol[:, d, 2 * i, :], s_ready, (0, 1))
                    for d in range(DUO):
                        n = DUO * half + d
                        pe.wait_ge(s_copied, h * R + (n + 1))
                        chunks(g.bank[4 + d], lambda i, n=n: kq_g[:, 1, 2 * n + i, :], lambda i, d=d: s_one[:, d, i, :],
                               ks_ready, (0, 1))
                    for d in range(DUO):
                        n = DUO * half + d
                        chunks(g.bank[6 + d], lambda i, n=n: g.xnT[:, (4 * n + i) * P:(4 * n + i + 1) * P], lambda i: wz_h[:, :], z_ready)
                    for d in range(DUO):
                        n = DUO * half + d
                        pe.wait_ge(rhs_ready, h * R + (n + 1))
                        chunks(g.bank[d], lambda i, d=d: xt[:, d, i, :], lambda i, d=d: v_tok[:, d, i, :], w_ready, (1, 3))
                    for d in range(DUO):
                        n = DUO * half + d
                        pe.wait_ge(w_copied, h * (2 * R) + (2 * DUO * half + DUO + d + 1))
                        for i in range(4):
                            mm = pe.matmul(g.bank[2 + d][:, i * C:(i + 1) * C], at[:, d, i, :], w_sol[:, d, i, :],
                                           start=True, stop=(i % 2 == 0))
                            if i % 2:
                                mm = pe.matmul(g.bank[2 + d][:, i * C:(i + 1) * C], kq_g[:, 0, 2 * n + i // 2, :],
                                               s_one[:, d, i // 2, :], start=False, stop=True)
                        mm.then_inc(o_ready, 1)
                    for d in range(DUO):
                        n = DUO * half + d
                        pe.wait_ge(on_ready, h * R + (n + 1))
                        for i in range(4):
                            mm = pe.transpose(g.bank[4 + d][:, i * C:(i + 1) * C], o_n[:, d, i, :], g.ident[:, :])
                        mm.then_inc(ot_ready, 1)
                    for d in range(DUO):
                        n = DUO * half + d
                        pe.wait_ge(ot_copied, h * R + (n + 1))
                        chunks(g.bank[d], lambda i, d=d: o_t[:, d, i, :], lambda i: wo_h[:, :], out_ready)
                pe.wait_ge(out_added, h * R + R)
                pe.sem_inc(pe_head, 1)

        @block.scalar
        def _(act):
            act.wait_ge(pads_zero, 1)
            act.sem_inc(act_head, 1)
            with act.Fori(0, HEADS) as h:
                for i in range(3 * GROUPS):
                    m, c = divmod(i, GROUPS)
                    act.wait_ge(proj_ready, h * (3 * GROUPS) + (i + 1))
                    act.activation(pad[:, m, SPG * c:SPG * (c + 1), TAPS - 1:],
                                   g.bank[i % 8][:, :].rearrange("p (b t) -> p b t", t=T), ACT.Copy).then_inc(proj_used, 1)
                for c in range(GROUPS):
                    act.wait_ge(a_ready, h * GROUPS + (c + 1))
                    a = g.bank[4 + c][:, :].rearrange("p (n c) -> p n c", c=C)
                    t = slice(TPG * c, TPG * (c + 1))
                    act.activation(alpha_in[:, t, 1:], a[:, :, 1:], ACT.Copy)
                    act.activation(alpha_first[:, t, 0:1], a[:, :, 0:1], ACT.Copy).then_inc(a_copied, 1)
                for half in range(HALVES):
                    for d in range(DUO):
                        n = DUO * half + d
                        act.wait_ge(turned, h * (2 * R) + (2 * n + 2))
                        act.activation(flat(v_tok, d), g.bank[4 + d][:, :], ACT.Copy).then_inc(tok_ready, 1)
                        act.wait_ge(lt_ready, h * R + (n + 1))
                        for i in range(2):
                            ins = act.activation(k_tok[:, d, i, :], g.bank[6 + d][:, i * C:(i + 1) * C], ACT.Copy,
                                                 scale=db[:, d, 2 * i, C - 1:C])
                        ins.then_inc(tok_ready, 1)
                    for lv in range(LEVELS):
                        for d in range(DUO):
                            it = half * DUO * LEVELS + lv * DUO + d
                            act.wait_ge(p_ready, h * (R * LEVELS) + (it + 1))
                            act.activation(flat(px, d), g.bank[d][:, :], ACT.Copy).then_inc(p_copied, 1)
                    for d in range(DUO):
                        act.wait_ge(w_ready, h * (2 * R) + (2 * DUO * half + d + 1))
                        act.activation(w_sol[:, d, 0:4:2, :], g.bank[d][:, :].rearrange("p (a c) -> p a c", c=C)[:, 0:4:2, :],
                                       ACT.Copy).then_inc(w_copied, 1)
                    for d in range(DUO):
                        n = DUO * half + d
                        act.wait_ge(s_ready, h * R + (n + 1))
                        act.activation(flat(s_one, d), g.bank[2 + d][:, 0:2 * C], ACT.Copy).then_inc(s_copied, 1)
                    for d in range(DUO):
                        act.wait_ge(z_ready, h * R + (DUO * half + d + 1))
                        act.activation(flat(sz, d), g.bank[6 + d][:, :], ACT.Silu).then_inc(sz_ready, 1)
                    act.preload_act_table_set(LN_EXP)
                    for d in range(DUO):
                        act.wait_ge(w_ready, h * (2 * R) + (2 * DUO * half + DUO + d + 1))
                        act.activation(w_sol[:, d, 1:4:2, :], g.bank[d][:, :].rearrange("p (a c) -> p a c", c=C)[:, 1:4:2, :],
                                       ACT.Copy).then_inc(w_copied, 1)
                    for d in range(DUO):
                        act.wait_ge(o_ready, h * R + (DUO * half + d + 1))
                        act.activation(flat(o_sq, d), g.bank[2 + d][:, :], ACT.Square).then_inc(sq_ready, 1)
                    for d in range(DUO):
                        n = DUO * half + d
                        act.wait_ge(var_ready, h * R + (n + 1))
                        act.activation(stat[:, d, 1, :], stat[:, d, 0, :], ACT.Ln, bias=eps_o[:, 0:1], scale=1.0 / P).then_inc(act_own, 1)
                        act.wait_ge(act_own, h * R + (n + 1))
                        act.activation(stat[:, d, 2, :], stat[:, d, 1, :], ACT.Exp, scale=-0.5).then_inc(rstd_ready, 1)
                    for d in range(DUO):
                        act.wait_ge(ot_ready, h * R + (DUO * half + d + 1))
                        act.activation(flat(o_t, d), g.bank[4 + d][:, :], ACT.Copy, scale=norm_w[:, 0:1]).then_inc(ot_copied, 1)
                act.wait_ge(ot_copied, h * R + R)
                act.sem_inc(act_head, 1)

        @block.vector
        def _(dve):
            own = Chain(dve, dve_own)
            own.add(dve.memset(pad[:, :, :, 0:TAPS - 1], 0.0))
            own.add(dve.memset(alpha_in[:, :, 0:1], 0.0))
            own.add(dve.memset(alpha_first[:, :, :], 0.0))
            own.add(dve.memset(eps_o[:, :], 1e-6))
            own.settle()
            for free in (pads_zero, dve_head, pe_head):
                dve.sem_inc(free, 1)
            dve.sem_inc(masked_used, DUO)
            SETUP, PER_HEAD = own.count, 27
            with dve.Fori(0, HEADS) as h:
                own = Chain(dve, dve_own, h * PER_HEAD + SETUP)
                dve.wait_ge(staged, h + 1)
                for m in range(3):
                    dve.wait_ge(proj_used, h * (3 * GROUPS) + GROUPS * (m + 1))
                    conv = qkv[:, m, :].rearrange("p (b t) -> p b t", t=T)
                    own.step(dve.tensor_scalar(conv, pad[:, m, :, 0:T], taps_h[:, m, 0:1], None, ALU.mult))
                    for k in range(1, TAPS):
                        own.step(dve.scalar_tensor_tensor(out=conv, in0=pad[:, m, :, k:k + T], scalar=taps_h[:, m, k:k + 1],
                                                          in1=conv, op0=ALU.mult, op1=ALU.add))
                    dve.sem_inc(conv_ready, 1)
                dve.wait_ge(a_copied, h * GROUPS + GROUPS)
                own.step(dve.tensor_tensor_scan(grow[:, :, :].rearrange("p n c -> p (n c)"),
                                                alpha_in[:, :, :].rearrange("p n c -> p (n c)"),
                                                alpha_first[:, :, :].rearrange("p n c -> p (n c)"), 0.0, ALU.mult, ALU.add))
                for m in range(2):
                    own.add(dve.tensor_tensor(kq_g[:, m, :, :], qkv[:, m, :].rearrange("p (b n c) -> p b n c", n=2, c=C)[:, :, 1, :],
                                              grow[:, 1:TILES:2, :], ALU.mult))
                own.settle()
                dve.sem_inc(kq_ready, 1)
                for half in range(HALVES):
                    for d in range(DUO):
                        n = DUO * half + d
                        t = slice(QUAD * n, QUAD * (n + 1))
                        own.step(dve.tensor_tensor(diag[:, d, :, :], g.ident[:, :].unsqueeze(1).to_broadcast([P, QUAD, C]),
                                                   spread(beta_h[:, t], C), ALU.mult))
                        own.step(dve.tensor_tensor_scan(flat(db, d), alpha_in[:, t, :].rearrange("p n c -> p (n c)"),
                                                        flat(diag, d), 0.0, ALU.mult, ALU.add))
                        dve.wait_ge(scores_ready, h * (2 * R) + (2 * n + 2))
                        dve.tensor_tensor(flat(lt, d), flat(db, d), g.bank[d][:, :], ALU.mult).then_inc(lt_ready, 1)
                        dve.tensor_tensor(flat(at, d), flat(db, d), g.bank[2 + d][:, :], ALU.mult).then_inc(at_ready, 1)
                    for lv in range(LEVELS):
                        for d in range(DUO):
                            it = half * DUO * LEVELS + lv * DUO + d
                            xit = half * DUO * (LEVELS - 1) + lv * DUO + d
                            if lv == 0:
                                ident4 = g.ident[:, :].unsqueeze(1).to_broadcast([P, QUAD, C])
                                dve.wait_ge(p_copied, h * (R * LEVELS) + (it + 1))
                                dve.tensor_tensor(xi[:, d, :, :], ident4, px[:, d, :, :], ALU.subtract).then_inc(x_ready, 1)
                                dve.tensor_tensor(xt[:, d, :, :], ident4, lt_n[:, d, :, :], ALU.subtract).then_inc(xt_ready, 1)
                            else:
                                if lv < LEVELS - 1:
                                    dve.wait_ge(xp_ready, h * (R * (LEVELS - 2)) + (half * DUO * (LEVELS - 2) + (lv - 1) * DUO + d + 1))
                                    dve.wait_ge(x_ready, h * (R * (LEVELS - 1)) + (xit - DUO + 1))
                                    dve.tensor_tensor(flat(xi, d), flat(xi, d), g.bank[2 + d][:, :], ALU.subtract).then_inc(x_ready, 1)
                                dve.wait_ge(xpt_ready, h * (R * (LEVELS - 1)) + (half * DUO * (LEVELS - 1) + (lv - 1) * DUO + d + 1))
                                dve.wait_ge(xt_ready, h * (R * LEVELS) + (it - DUO + 1))
                                dve.tensor_tensor(flat(xt, d), flat(xt, d), g.bank[4 + d][:, :], ALU.subtract).then_inc(xt_ready, 1)
                            dve.wait_ge(xt_ready, h * (R * LEVELS) + (it + 1))
                            dve.sem_inc(masked_used, 1)
                    for d in range(DUO):
                        n = DUO * half + d
                        dve.wait_ge(ks_ready, h * R + (n + 1))
                        dve.tensor_tensor(v_tok[:, d, 1:4:2, :], v_tok[:, d, 1:4:2, :],
                                          g.bank[4 + d][:, 0:2 * C].rearrange("p (a c) -> p a c", c=C), ALU.subtract).then_inc(rhs_ready, 1)
                    for d in range(DUO):
                        n = DUO * half + d
                        dve.wait_ge(sq_ready, h * R + (n + 1))
                        dve.tensor_reduce(stat[:, d, 0, :], o_sq[:, d, :, :], AX.X, ALU.add).then_inc(var_ready, 1)
                    for d in range(DUO):
                        n = DUO * half + d
                        dve.wait_ge(rstd_ready, h * R + (n + 1))
                        own.step(dve.tensor_tensor(o_n[:, d, :, :], g.bank[2 + d][:, :].rearrange("p (a c) -> p a c", c=C),
                                                   spread(stat[:, d, 2, :], C), ALU.mult))
                        dve.wait_ge(sz_ready, h * R + (n + 1))
                        dve.tensor_tensor(flat(o_n, d), flat(o_n, d), flat(sz, d), ALU.mult).then_inc(on_ready, 1)
                    for d in range(DUO):
                        n = DUO * half + d
                        dve.wait_ge(out_ready, h * R + (n + 1))
                        x_q = g.x[:, QUAD * n:QUAD * (n + 1), :]
                        dve.tensor_tensor(x_q, x_q, g.bank[d][:, :].rearrange("p (n d) -> p n d", d=D), ALU.add).then_inc(out_added, 1)
                dve.wait_ge(out_added, h * R + R)
                dve.sem_inc(dve_head, 1)
                assert own.count == PER_HEAD, own.count


def rotary_tables():
    half = np.arange(0, 64, 2, dtype=np.float32)
    inv_freq = np.float32(1.0) / np.power(np.float32(10000.0), half / np.float32(64))
    t = np.arange(T, dtype=np.float32)
    freqs = t[:, None] * inv_freq[None, :]
    freqs = np.concatenate([freqs, freqs], -1).T
    base = (half + np.float32(0.4 * 64)) / np.float32(1.4 * 64)
    scale = base[None, :] ** ((t - T // 2) / np.float32(16))[:, None]
    scale = np.concatenate([scale, scale], -1).T
    sign = np.repeat(np.array([-1, 1], np.float32), 32)[:, None]
    cos, sin = np.cos(freqs), np.sin(freqs) * sign
    one = np.stack([8 * cos * scale, cos / scale, 8 * sin * scale, sin / scale], 1).astype(np.float32)
    return np.concatenate([one, one])


def local_stack(nc, g, d_in):
    LAYERS, PAIRS, W, E = 6, 8, 32, 64
    WINDOWS = T // W
    UNITS, CHUNKS = 341, 3
    LAST = UNITS - 2 * P
    SLOTS = PAIRS * GROUPS
    H = 2
    LN_SCALE = 2.0 ** 20
    with ExitStack() as ctx:
        sem = ctx.enter_context(Signals(nc, "local"))

        def sb(n, shape, dt=F32):
            return ctx.enter_context(nc.sbuf_tensor(f"local_{n}", shape, dt))
        base = sb("base", [P, 4, T])
        norm_and_turn(nc, g, "local_ln", [(base[:, :, :], d_in["base"])])
        w_layer = sb("w_layer", [P, PAIRS, 5 * P])
        w_pair = sb("w_pair", [P, 5, P])
        w_o, w_up, w_down = sb("w_o", [P, PAIRS, D]), sb("w_up", [P, 2 * UNITS]), sb("w_down", [P, CHUNKS, D])
        vecs = sb("vecs", [P, 12])
        table = sb("table", [P, 4, T])
        xs = sb("xs", [P, BATCH, W + T])
        q_rot = sb("q_rot", [P, 2, 2 * GROUP])
        k_rot = sb("k_rot", [P, 2, SPG, W + T])
        v_at, v_moved = sb("v_at", [P, TILES, P]), sb("v_moved", [P, TILES, P])
        attn = sb("attn", [P, PAIRS, N])
        sq, lg, inv = sb("sq", [P, 2, GROUP]), sb("lg", [P, 2, GROUP]), sb("inv", [P, 2, GROUP])
        mask = sb("mask", [P, 4, 2 * W])
        z = sb("z", [P, 2, GROUP])
        term = sb("term", [P, 4, SPG, T])
        most, total = sb("most", [P, 2, 2 * TPG]), sb("total", [P, 2, 2, 2 * TPG])
        pt = sb("pt", [P, GROUP])
        same_head, mean_of = sb("same_head", [P, P]), sb("mean_of", [P, P])
        guard, unscale = sb("guard", [P, 1]), sb("unscale", [P, 1])
        gelu, hid = sq, sb("hid", [P, 2, CHUNKS, GROUP])
        xc = attn[:, 1, :]
        rstd = v_at
        made, vecs_loaded, pair_loaded, ffn_loaded = sem("made"), sem("vecs_loaded"), sem("pair_loaded"), sem("ffn_loaded")
        vecs_free, pair_free, ffn_free = sem("vecs_free"), sem("pair_free"), sem("ffn_free")
        staged, tabled = sem("staged"), sem("tabled")
        xr_ready, turned, xs_ready = sem("xr_ready"), sem("turned"), sem("xs_ready")
        proj_ready, rotated, sq_ready, summed = sem("proj_ready"), sem("rotated"), sem("sq_ready"), sem("summed")
        v_ready, v_used, v_shifted = sem("v_ready"), sem("v_used"), sem("v_shifted")
        norm_ready, norm_used, inv_ready = sem("norm_ready"), sem("norm_used"), sem("inv_ready")
        qk_ready, s_ready, z_ready, e_ready = sem("qk_ready"), sem("s_ready"), sem("z_ready"), sem("e_ready")
        total_ready, p_ready = sem("total_ready"), sem("p_ready")
        pt_ready, pt_copied, o_ready, o_copied, wo_ready = (
            sem("pt_ready"), sem("pt_copied"), sem("o_ready"), sem("o_copied"), sem("wo_ready"))
        mean_ready, xc_ready, xsq_ready, var_ready, rstd_ready, h_ready = (
            sem("mean_ready"), sem("xc_ready"), sem("xsq_ready"), sem("var_ready"), sem("rstd_ready"), sem("h_ready"))
        up_ready, gelu_ready, hid_ready, down_ready = sem("up_ready"), sem("gelu_ready"), sem("hid_ready"), sem("down_ready")
        dve_own, act_own, pool_own, act_passed, sp_passed = sem("dve"), sem("act"), sem("pool"), sem("act_passed"), sem("sp_passed")
        pe_passed, dve_passed, pool_passed = sem("pe_passed"), sem("dve_passed"), sem("pool_passed")
        block = ctx.enter_context(nc.Block())
        FFN = GROUPS * CHUNKS
        normed = sem("normed")

        def add_down(dve, l, c):
            dve.wait_ge(down_ready, l * GROUPS + (c + 1))
            xr = g.xn[:, TPG * c:TPG * (c + 1), :]
            dve.tensor_tensor(xr, xr, g.bank[4 + c % 2][:, :].rearrange("p (n d) -> p n d", d=D), ALU.add).then_inc(xr_ready, 1)

        def seqs(c):
            return slice(SPG * c, SPG * (c + 1))

        def slots(eng, l, project, slot, finish):
            first = l * SLOTS
            project(first, 0)
            slot(first, 0, True, None)
            with eng.Fori(0, PAIRS - 1) as hp:
                for j in range(1, GROUPS + 1):
                    slot(first + hp * GROUPS, j, True, hp)
            for j in range(1, GROUPS):
                slot(first + (PAIRS - 1) * GROUPS, j, j < GROUPS - 1, PAIRS - 1)
            finish(first + (PAIRS - 1) * GROUPS, GROUPS - 1)

        @block.sync
        def _(sp):
            sp.wait_ge(made, 1)

            def shift_values(s, c):
                sp.wait_ge(v_used, s + 1)
                t = slice(TPG * c, TPG * (c + 1))
                sp.dma_start(v_moved[W:P, t, :], v_at[0:P - W, t, :]).then_inc(v_shifted, 16)
                sp.dma_start(v_moved[0:W, TPG * c + 1:TPG * (c + 1):2, :], v_at[P - W:P, TPG * c:TPG * (c + 1):2, :]
                             ).then_inc(v_shifted, 16)
                wait_apart(sp, v_shifted, s * 32 + 32, sp_passed)
            with sp.Fori(0, LAYERS) as l:
                wait_apart(sp, vecs_free, l + 1, sp_passed)
                sp.dma_start(vecs[:, :], d_in["vecs"][bass.ts(l, 1), :, :].rearrange("a p n -> (a p) n")).then_inc(vecs_loaded, 16)
                wait_apart(sp, pair_free, l + 1, sp_passed)
                sp.dma_start(w_layer[:, :, :], d_in["w_layer"][bass.ts(l, 1), :, :, :].rearrange("a p n m -> (a p) n m")
                             ).then_inc(pair_loaded, 16)
                wait_apart(sp, ffn_free, l + 1, sp_passed)
                sp.dma_start(w_o[:, :, :], d_in["w_o"][bass.ts(l, 1), :, :, :].rearrange("a p n m -> (a p) n m")).then_inc(ffn_loaded, 16)
                sp.dma_start(w_up[:, :], d_in["w_up"][bass.ts(l, 1), :, :].rearrange("a p n -> (a p) n")).then_inc(ffn_loaded, 16)
                sp.dma_start(w_down[:, :, :], d_in["w_down"][bass.ts(l, 1), :, :, :].rearrange("a p n m -> (a p) n m")
                             ).then_inc(ffn_loaded, 16)
                with sp.Fori(0, PAIRS) as hp:
                    for c in range(GROUPS):
                        shift_values(l * SLOTS + hp * GROUPS + c, c)

        @block.gpsimd
        def _(pool):
            own = Chain(pool, pool_own)
            own.step(pool.memset(xs[:, :, 0:W + 1], 0.0))
            own.step(pool.memset(k_rot[:, :, :, 0:W], 0.0))
            own.step(pool.memset(q_rot[:, :, :], 0.0))
            own.step(pool.memset(v_moved[0:W, :, :], 0.0))
            own.step(pool.memset(same_head[:, :], 0.0))
            own.step(pool.memset(mean_of[:, :], 1.0 / D))
            own.step(pool.memset(guard[:, :], 1e-24 * LN_SCALE))
            own.step(pool.memset(unscale[:, :], 0.5 * float(np.log(LN_SCALE))))
            own.step(pool.memset(hid[64:P, :, CHUNKS - 1, :], 1.0))
            own.step(pool.memset(mask[:, :, :], 0.0))
            own.settle()
            for hh in range(2):
                own.step(pool.memset(same_head[E * hh:E * hh + E, E * hh:E * hh + E], 1.0))
            for quadrant in range(4):
                own.settle()
                m = mask[W * quadrant:W * (quadrant + 1), :, :]
                own.step(pool.affine_select(out=m, in_=m, compare_op=ALU.is_ge, fill=-1e30, base=0,
                                            pattern=[[0, 4], [1, 2 * W]], channel_multiplier=-1))
                own.step(pool.affine_select(out=m, in_=m, compare_op=ALU.is_ge, fill=-1e30, base=W,
                                            pattern=[[0, 4], [-1, 2 * W]], channel_multiplier=1))
            own.step(pool.memset(mask[0:H * W, 0, 0:W], -1e30))
            pool.sem_inc(made, 1)

            def stage(weights):
                pool.tensor_copy(w_pair[:, :, :].rearrange("p a c -> p (a c)"), weights.rearrange("p a c -> p (a c)")).then_inc(staged, GROUPS)

            def add_rotated(s):
                for m in range(2):
                    pool.wait_ge(rotated, s * 4 + (4 + 3 + m))
                    pool.tensor_tensor(term[:, m, :, :], term[:, m, :, :], term[:, 2 + m, :, :], ALU.add).then_inc(summed, 1)

            def slot(b, j, project_next, hp):
                s = b + j
                if j == GROUPS - 1 and project_next:
                    pool.wait_ge(proj_ready, s * 4 + 4)
                    stage(w_layer[:, 1:, :][:, bass.ts(hp, 1), :])
                pool.wait_ge(total_ready, s + 1)
                rows = z[:, j % 2, :].rearrange("p (x k) -> p x k", k=2 * W)
                pool.tensor_tensor(rows, rows, spread(total[:, j % 2, 1, :], 2 * W), ALU.mult).then_inc(p_ready, 1)
                if project_next:
                    add_rotated(s + 1)

            def finish(b, j):
                pool.wait_ge(staged, b + GROUPS)
                pool.sem_inc(pair_free, 1)
            with pool.Fori(0, LAYERS) as l:
                pool.wait_ge(pair_loaded, l * 16 + 16)
                pool.wait_ge(xs_ready, l * 8 + 1)
                stage(w_layer[:, 0:1, :])
                slots(pool, l, lambda b, j: add_rotated(b), slot, finish)

        @block.tensor
        def _(pe):
            pe.wait_ge(made, 1)

            def turn(l, second):
                for c in range(GROUPS):
                    pe.wait_ge(xr_ready, l * 8 + (4 * second + c + 1))
                    for i in range(TPG):
                        mm = pe.transpose(g.bank[c][:, i * P:(i + 1) * P], g.xn[:, TPG * c + i, :], g.ident[:, :])
                    mm.then_inc(turned, 1)

            def project(b, j):
                s, c = b + j, j % GROUPS
                if c == 0:
                    pe.wait_ge(staged, s + GROUPS)
                if j == 0:
                    wait_apart(pe, pt_copied, s + 2, pe_passed)
                else:
                    pe.wait_ge(norm_used, s * 2 + 2)
                    wait_apart(pe, pt_copied, s + 1, pe_passed)
                for i in range(TPG):
                    b_, n = divmod(i, 2)
                    mm = pe.matmul(g.bank[4][:, i * P:(i + 1) * P], xs[:, SPG * c + b_, W + n * P:W + (n + 1) * P],
                                   w_pair[:, 4, :], start=True, stop=True)
                mm.then_inc(v_ready, 1)
                pe.wait_ge(norm_used, s * 2 + 2)
                pe.wait_ge(rotated, s * 4 + 4)
                for m in range(4):
                    pe.matmul(g.bank[m][:, :].rearrange("p (b t) -> p b t", t=T), w_pair[:, m, :], xs[:, seqs(c), W:],
                              start=True, stop=True).then_inc(proj_ready, 1)
                for m in range(2):
                    pe.wait_ge(sq_ready, s * 2 + (m + 1))
                    if m == 0:
                        pe.wait_ge(rotated, s * 4 + 5)
                    else:
                        pe.wait_ge(v_used, s + 1)
                    pe.matmul(g.bank[4 * m][:, :], same_head[:, :], sq[:, m, :], start=True, stop=True).then_inc(norm_ready, 1)

            def score(s, j):
                wait_apart(pe, qk_ready, s * 3 + 3, pe_passed)
                for b in range(SPG):
                    for w in range(WINDOWS):
                        n, half, r = w // 4, w // 2 % 2, w % 2
                        column = ((b * 2 + n) * 2 + half) * 2 * W
                        query = (b * WINDOWS + w) * H * W
                        mm = pe.matmul(g.bank[5][H * W * r:H * W * (r + 1), column:column + 2 * W],
                                       q_rot[:, j % 2, query:query + H * W], k_rot[:, j % 2, b, w * W:(w + 2) * W],
                                       start=True, stop=True)
                mm.then_inc(s_ready, 1)

            def turn_probs(s, j, project_next):
                pe.wait_ge(p_ready, s + 1)
                if project_next:
                    pe.wait_ge(norm_used, s * 2 + 6)
                for i in range(TPG):
                    mm = pe.transpose(g.bank[4][:, i * P:(i + 1) * P], z[:, j % 2, i * P:(i + 1) * P], g.ident[:, :])
                mm.then_inc(pt_ready, 1)

            def weigh_values(s, j):
                pe.wait_ge(pt_copied, s + 3)
                pe.wait_ge(v_shifted, s * 32 + 32)
                wait_apart(pe, o_copied, s + 1, pe_passed)
                for b in range(SPG):
                    for w in range(WINDOWS):
                        n, half, r = w // 4, w // 2 % 2, w % 2
                        keys = slice(64 * half, 64 * half + 64)
                        probs = (b * 2 + n) * P + H * W * r
                        column = ((b * 2 + n) * 2 + r) * H * W
                        mm = pe.matmul(g.bank[6 + half][:, column:column + H * W],
                                       (v_at if r else v_moved)[keys, TPG * (j % GROUPS) + 2 * b + n, :],
                                       pt[keys, probs:probs + H * W], start=True, stop=True)
                mm.then_inc(o_ready, 1)

            def slot(b, j, project_next, hp):
                score(b + j, j)
                if project_next:
                    project(b, j + 1)
                if hp is not None:
                    weigh_values(b + (j - 1), j - 1)
                turn_probs(b + j, j, project_next)

            with pe.Fori(0, LAYERS) as l:
                turn(l, 0)
                wait_apart(pe, xs_ready, l * 8 + 4, pe_passed)
                slots(pe, l, project, slot, lambda b, j: weigh_values(b + j, j))
                pe.wait_ge(ffn_loaded, l * 48 + 48)
                pe.wait_ge(o_copied, l * SLOTS + (SLOTS + 1))
                for c in range(GROUPS):
                    for i in range(TPG):
                        for p in range(PAIRS):
                            t0 = c * GROUP + i * P
                            mm = pe.matmul(g.bank[4 + c][:, i * P:(i + 1) * P], attn[:, p, t0:t0 + P], w_o[:, p, :],
                                           start=(p == 0), stop=(p == PAIRS - 1))
                    mm.then_inc(wo_ready, 1)
                turn(l, 1)
                for c in range(GROUPS):
                    pe.wait_ge(xs_ready, l * 8 + (5 + c))
                    pe.matmul(g.bank[c][:, :].rearrange("p (b t) -> p b t", t=T), mean_of[:, :], xs[:, seqs(c), W:],
                              start=True, stop=True).then_inc(mean_ready, 1)
                for c in range(GROUPS):
                    pe.wait_ge(xsq_ready, l * GROUPS + (c + 1))
                    pe.matmul(g.bank[4 + c][:, :], mean_of[:, :], attn[:, 0, tok(c)], start=True, stop=True).then_inc(var_ready, 1)
                for c in range(GROUPS):
                    pe.wait_ge(h_ready, l * GROUPS + (c + 1))
                    for m in range(CHUNKS):
                        i = CHUNKS * c + m
                        rows = P if m < CHUNKS - 1 else LAST
                        if i >= 2:
                            pe.wait_ge(hid_ready, l * FFN + (i - 1))
                        for k in range(2):
                            mm = pe.matmul(g.bank[2 * k + i % 2][0:rows, :], w_up[:, k * UNITS + m * P:k * UNITS + m * P + rows],
                                           g.xnT[:, tok(c)], start=True, stop=True)
                        mm.then_inc(up_ready, 1)
                    pe.wait_ge(hid_ready, l * FFN + CHUNKS * (c + 1))
                    if c == 0:
                        pe.wait_ge(rstd_ready, l * GROUPS + GROUPS)
                    if c >= 2:
                        pe.wait_ge(xr_ready, l * 8 + (8 + c - 1))
                    for i in range(TPG):
                        for m in range(CHUNKS):
                            rows = P if m < CHUNKS - 1 else LAST + 1
                            mm = pe.matmul(g.bank[4 + c % 2][:, i * P:(i + 1) * P], hid[0:rows, c % 2, m, i * P:(i + 1) * P],
                                           w_down[0:rows, m, :], start=(m == 0), stop=(m == CHUNKS - 1))
                    mm.then_inc(down_ready, 1)
                pe.wait_ge(down_ready, l * GROUPS + GROUPS)
                pe.sem_inc(ffn_free, 1)

        @block.scalar
        def _(act):
            own = Chain(act, act_own)
            act.wait_ge(made, 1)
            for free, n in ((pair_free, 1), (ffn_free, 1), (norm_used, 2), (pt_copied, 2), (o_copied, 1)):
                act.sem_inc(free, n)

            def turn(l, second):
                for c in range(GROUPS):
                    act.wait_ge(turned, l * 8 + (4 * second + c + 1))
                    bank = g.bank[c][:, :].rearrange("p (b t) -> p b t", t=T)
                    act.activation(xs[0:64, seqs(c), W:], bank[0:64, :, :], ACT.Copy)
                    act.activation(xs[64:P, seqs(c), W + 1:], bank[64:P, :, 0:T - 1], ACT.Copy).then_inc(xs_ready, 1)

            def copy_values_and_square(s, j, m):
                if m == 0:
                    act.wait_ge(v_ready, s + 1)
                    t = slice(TPG * (j % GROUPS), TPG * (j % GROUPS + 1))
                    act.activation(v_at[:, t, :].rearrange("p n c -> p (n c)"), g.bank[4][:, :], ACT.Copy).then_inc(v_used, 1)
                act.wait_ge(proj_ready, s * 4 + (m + 1))
                act.activation(sq[:, m, :], g.bank[m][:, :], ACT.Square).then_inc(sq_ready, 1)

            def invert_norms(s):
                for m in range(2):
                    act.wait_ge(norm_ready, s * 2 + (m + 1))
                    act.activation(lg[:, m, :], g.bank[4 * m][:, :], ACT.Ln, bias=guard[:, 0:1], scale=LN_SCALE).then_inc(norm_used, 1)
                    act.wait_ge(norm_used, s * 2 + (2 + m + 1))
                    act.activation(inv[:, m, :], lg[:, m, :], ACT.Exp, bias=unscale[:, 0:1], scale=-0.5).then_inc(inv_ready, 1)

            def project(b, j):
                copy_values_and_square(b + j, j, 0)
                copy_values_and_square(b + j, j, 1)
                invert_norms(b + j)

            def copy_out(s, j, hp):
                wait_apart(act, o_ready, s + 1, act_passed)
                pair = attn[:, hp:hp + 1, tok(j)] if isinstance(hp, int) else attn[:, bass.ts(hp, 1), tok(j)]
                for half in range(2):
                    for hh in range(H):
                        ch = slice(E * hh, E * (hh + 1))
                        tokens = pair[ch, :, :].rearrange("p a (x s r q) -> p (a x) s r q", s=2, r=2, q=W)[:, :, half, :, :]
                        ins = act.activation(tokens, g.bank[6 + half][ch, :].rearrange("p (x r h q) -> p x r h q", r=2, h=H, q=W)[:, :, :, hh, :],
                                             ACT.Copy)
                ins.then_inc(o_copied, 1)

            def slot(b, j, project_next, hp):
                s = b + j
                if project_next:
                    copy_values_and_square(s + 1, j + 1, 0)
                act.wait_ge(z_ready, s + 1)
                act.activation(z[:, j % 2, :], z[:, j % 2, :], ACT.Exp).then_inc(e_ready, 1)
                if project_next:
                    copy_values_and_square(s + 1, j + 1, 1)
                    invert_norms(s + 1)
                act.wait_ge(pt_ready, s + 1)
                act.activation(pt[:, :], g.bank[4][:, :], ACT.Copy).then_inc(pt_copied, 1)
                if hp is not None:
                    copy_out(b + (j - 1), j - 1, hp)

            LN_STEPS = GROUPS * 2
            with act.Fori(0, LAYERS) as l:
                act.preload_act_table_set(LN_EXP)
                turn(l, 0)
                slots(act, l, project, slot, lambda b, j: copy_out(b + j, j, PAIRS - 1))
                turn(l, 1)
                own = Chain(act, act_own, l * LN_STEPS)
                for c in range(GROUPS):
                    act.wait_ge(xc_ready, l * GROUPS + (c + 1))
                    act.activation(attn[:, 0, tok(c)], xc[:, tok(c)], ACT.Square).then_inc(xsq_ready, 1)
                for c in range(GROUPS):
                    act.wait_ge(var_ready, l * GROUPS + (c + 1))
                    own.step(act.activation(lg[:, c % 2, :], g.bank[4 + c][:, :], ACT.Ln, bias=g.eps[:, 0:1]))
                    own.add(act.activation(rstd[:, TPG * c:TPG * (c + 1), :].rearrange("p n c -> p (n c)"), lg[:, c % 2, :],
                                           ACT.Exp, scale=-0.5))
                    own.settle()
                    act.sem_inc(rstd_ready, 1)
                for c in range(GROUPS):
                    for m in range(CHUNKS):
                        i = CHUNKS * c + m
                        rows = P if m < CHUNKS - 1 else LAST
                        act.wait_ge(up_ready, l * FFN + (i + 1))
                        if i >= 2:
                            act.wait_ge(hid_ready, l * FFN + (i - 1))
                        act.activation(gelu[0:rows, i % 2, :], g.bank[2 + i % 2][0:rows, :], ACT.Gelu,
                                       bias=vecs[0:rows, 9 + m:10 + m]).then_inc(gelu_ready, 1)

        @block.vector
        def _(dve):
            dve.wait_ge(made, 1)
            for free, n in ((vecs_free, 1), (xr_ready, 4), (rotated, 4)):
                dve.sem_inc(free, n)
            STEPS = 3

            def times_table(s, k):
                dve.wait_ge(proj_ready, s * 4 + (k + 1))
                if k < 2:
                    dve.wait_ge(sq_ready, s * 2 + (k + 1))
                dve.tensor_tensor(term[:, k, :, :], g.bank[k][:, :].rearrange("p (b t) -> p b t", t=T),
                                  table[:, k, :].unsqueeze(1).to_broadcast([P, SPG, T]), ALU.mult).then_inc(rotated, 1)

            def over_norm(s, j):
                dve.wait_ge(inv_ready, s * 2 + 1)
                dve.wait_ge(summed, s * 2 + 1)
                for hh in range(H):
                    ch = slice(E * hh, E * (hh + 1))
                    dve.tensor_tensor(q_rot[ch, j % 2, :].rearrange("p (x h q) -> p x h q", h=H, q=W)[:, :, hh, :],
                                      term[ch, 0, :, :].rearrange("p b (w q) -> p (b w) q", q=W),
                                      inv[ch, 0, :].rearrange("p (x q) -> p x q", q=W), ALU.mult).then_inc(qk_ready, 1)
                dve.wait_ge(inv_ready, s * 2 + 2)
                dve.wait_ge(summed, s * 2 + 2)
                dve.tensor_tensor(k_rot[:, j % 2, :, W:], term[:, 1, :, :], inv[:, 1, :].rearrange("p (b t) -> p b t", t=T),
                                  ALU.mult).then_inc(qk_ready, 1)

            def project(b, j):
                for k in range(4):
                    times_table(b + j, k)
                over_norm(b + j, j)

            def slot(b, j, project_next, hp):
                s = b + j
                own = Chain(dve, dve_own, s * STEPS)
                rows = z[:, j % 2, :].rearrange("p (x k) -> p x k", k=2 * W)
                most_of, sums, over = most[:, j % 2, :], total[:, j % 2, 0, :], total[:, j % 2, 1, :]
                dve.wait_ge(s_ready, s + 1)
                own.step(dve.tensor_tensor(z[:, j % 2, :].rearrange("p (b k) -> p b k", b=SPG),
                                           g.bank[5][:, :].rearrange("p (b k) -> p b k", b=SPG),
                                           mask[:, :, :].rearrange("p x k -> p (x k)").unsqueeze(1).to_broadcast([P, SPG, GROUP // SPG]),
                                           ALU.add))
                own.step(dve.tensor_reduce(most_of, rows, AX.X, ALU.max))
                dve.tensor_tensor(rows, rows, spread(most_of, 2 * W), ALU.subtract).then_inc(z_ready, 1)
                if project_next:
                    times_table(s + 1, 0)
                dve.wait_ge(e_ready, s + 1)
                own.step(dve.tensor_reduce(sums, rows, AX.X, ALU.add))
                dve.reciprocal(over, sums).then_inc(total_ready, 1)
                if project_next:
                    for k in range(1, 4):
                        times_table(s + 1, k)
                    over_norm(s + 1, j + 1)
                assert own.count == STEPS, own.count

            with dve.Fori(0, LAYERS) as l:
                dve.wait_ge(vecs_loaded, l * 16 + 16)
                for k in range(4):
                    ins = dve.tensor_scalar(table[:, k, :], base[:, k, :], vecs[:, k:k + 1], None, ALU.mult)
                ins.then_inc(tabled, 1)
                wait_apart(dve, tabled, l + 1, dve_passed)
                slots(dve, l, project, slot, lambda b, j: None)
                for c in range(GROUPS):
                    dve.wait_ge(wo_ready, l * GROUPS + (c + 1))
                    xr = g.xn[:, TPG * c:TPG * (c + 1), :]
                    dve.tensor_tensor(xr, xr, g.bank[4 + c][:, :].rearrange("p (n d) -> p n d", d=D), ALU.add).then_inc(xr_ready, 1)
                for c in range(GROUPS):
                    dve.wait_ge(mean_ready, l * GROUPS + (c + 1))
                    dve.tensor_tensor(xc[:, tok(c)].rearrange("p (b t) -> p b t", t=T), xs[:, seqs(c), W:],
                                      g.bank[c][:, :].rearrange("p (b t) -> p b t", t=T), ALU.subtract).then_inc(xc_ready, 1)
                for c in range(GROUPS):
                    dve.wait_ge(rstd_ready, l * GROUPS + (c + 1))
                    dve.wait_ge(xc_ready, l * GROUPS + GROUPS)
                    h = g.xnT[:, tok(c)]
                    dve.tensor_tensor(h, xc[:, tok(c)], rstd[:, TPG * c:TPG * (c + 1), :].rearrange("p n c -> p (n c)"), ALU.mult).then_inc(normed, 1)
                    dve.wait_ge(normed, l * GROUPS + (c + 1))
                    dve.tensor_scalar(h, h, vecs[:, 4:5], vecs[:, 5:6], ALU.mult, ALU.add).then_inc(h_ready, 1)
                for c in range(GROUPS):
                    for m in range(CHUNKS):
                        i = CHUNKS * c + m
                        rows = P if m < CHUNKS - 1 else LAST
                        dve.wait_ge(gelu_ready, l * FFN + (i + 1))
                        if c >= 2 and m == 0:
                            dve.wait_ge(down_ready, l * GROUPS + (c - 1))
                        dve.scalar_tensor_tensor(out=hid[0:rows, c % 2, m, :], in0=g.bank[i % 2][0:rows, :],
                                                 scalar=vecs[0:rows, 6 + m:7 + m], in1=gelu[0:rows, i % 2, :],
                                                 op0=ALU.add, op1=ALU.mult).then_inc(hid_ready, 1)
                    if c >= 1:
                        add_down(dve, l, c - 1)
                add_down(dve, l, GROUPS - 1)
                dve.wait_ge(hid_ready, l * FFN + FFN)
                dve.sem_inc(vecs_free, 1)

    with ExitStack() as ctx:
        sem = ctx.enter_context(Signals(nc, "local_sum"))
        added = sem("added")
        block = ctx.enter_context(nc.Block())

        @block.vector
        def _(dve):
            dve.tensor_tensor(g.x[:, :, :], g.x[:, :, :], g.xn[:, :, :], ALU.add).then_inc(added, 1)
            dve.wait_ge(added, 1)


def store(nc, g, out_dram):
    with ExitStack() as ctx:
        stored = ctx.enter_context(nc.semaphore("stored"))
        block = ctx.enter_context(nc.Block())

        @block.sync
        def _(sp):
            sp.dma_start(out_dram.rearrange("(n p) d -> p n d", p=P), g.x[:, :, :]).then_inc(stored, 16)
            sp.wait_ge(stored, 16)


STAGES = (0, 1, 2, 3, 4, 5, 6, 7)


def build(nc, d_in, out_dram):
    g = Shared()
    with ExitStack() as ctx:
        def sb(n, shape):
            return ctx.enter_context(nc.sbuf_tensor(n, shape, F32))
        g.x, g.xn = sb("x", [P, TILES, D]), sb("xn", [P, TILES, D])
        g.xnT = sb("xnT", [P, N])
        g.ident, g.eps, g.one = sb("ident", [P, P]), sb("eps", [P, 1]), sb("one", [P, 1])
        g.bank = [ctx.enter_context(nc.psum_tensor(f"bank{i}", [P, 512], F32)) for i in range(8)]
        g.weights, g.weights_due = ctx.enter_context(nc.semaphore("weights")), 0
        set_up(nc, g, d_in["x"])
        if 0 in STAGES:
            mamba(nc, g, "mamba0", None, d_in["m0"])
        if 1 in STAGES:
            moe(nc, g, "moe0", d_in["f0"], 16, 9, lambda j: j if j < 8 else None, True, True, False)
        if 2 in STAGES:
            rotor_memory(nc, g, d_in["r1"])
        if 3 in STAGES:
            local_stack(nc, g, d_in["a1"])
        if 4 in STAGES:
            delta_rule(nc, g, d_in["g2"])
        if 5 in STAGES:
            moe(nc, g, "moe2", d_in["f2"], 8, 8, lambda j: j, True, False, False)
        if 6 in STAGES:
            mamba(nc, g, "mamba3", None, d_in["m3"])
        if 7 in STAGES:
            moe(nc, g, "moe3", d_in["f3"], 8, 32, lambda j: j // 4, False, False, True)
        store(nc, g, out_dram)


def lay_out(inputs):
    i = {k: np.asarray(v) for k, v in inputs.items()}

    def rows(a, n=P):
        return a.reshape(-1, n, *a.shape[1:]).swapaxes(0, 1)

    def everywhere(a):
        return np.broadcast_to(a[None], (P,) + a.shape)

    def mamba_side(p, names):
        w_x = i[p + names["w_x"]]
        out = {"w_in": i[p + "W_in"], "conv_w": rows(i[p + "conv_w"][:, 0, :]), "conv_b": rows(i[p + "conv_b"]),
               "w_bc": rows(w_x[:, -32:]), "b_dt": rows(i[p + "b_dt"]), "skip": rows(i[p + names["skip"]]),
               "w_out": rows(i[p + "W_out"])}
        a_log = i[p + "A_log"]
        out["a_log"] = rows(a_log) if a_log.ndim == 2 else np.broadcast_to(a_log, (P, 2, 16))
        if w_x.shape[1] == 33:
            out["w_dt"], out["w_dt_col"] = i[p + "W_dt"], rows(w_x[:, 0])
        else:
            out["w_dt"] = rows(i[p + "W_dt"])
        return out

    turned_half = np.concatenate([np.arange(32, 64), np.arange(32)])
    wq, wk, wv = (i["L1_ffn_Wqkv"][:, :, 1024 * n:1024 * (n + 1)].reshape(6, D, 8, 2, 64) for n in range(3))
    w_layer = np.stack([wq, wk, wq[..., turned_half], wk[..., turned_half], wv], 3).reshape(6, D, 8, 5 * P)
    scales = [np.concatenate([i[f"L1_ffn_{n}_scale"][:, order]] * 2, 1) for order in (np.arange(64), turned_half) for n in "qk"]
    b1 = np.zeros((6, 2, 3 * P), np.float32)
    b1[:, :, :341] = i["L1_ffn_b1"].reshape(6, 2, 341)
    w_down = np.zeros((6, 3 * P, D), np.float32)
    w_down[:, :341], w_down[:, 341] = i["L1_ffn_W2"], i["L1_ffn_b2"]
    return {
        "a1": {
            "base": rotary_tables(), "w_layer": w_layer,
            "vecs": np.stack(scales + [i["L1_ffn_ln_g"], i["L1_ffn_ln_b"]]
                             + [b1[:, k, P * m:P * (m + 1)] for k in range(2) for m in range(3)], 2),
            "w_o": i["L1_ffn_Wo"].reshape(6, 8, P, D).swapaxes(1, 2), "w_up": i["L1_ffn_W1"],
            "w_down": w_down.reshape(6, 3, P, D).swapaxes(1, 2),
        },
        "m0": mamba_side("L0_attn_", {"w_x": "W_xproj", "skip": "Dp"}),
        "m3": mamba_side("L3_attn_", {"w_x": "W_x", "skip": "D"}),
        "f0": {
            "gate_w": i["L0_ffn_gate_w"].T, "gate_b": everywhere(i["L0_ffn_expert_bias"]),
            "w1": np.concatenate([i["L0_ffn_w1"].reshape(-1, D), i["L0_ffn_sw1"]]).T.reshape(D, 9, P),
            "w3": np.concatenate([i["L0_ffn_w3"].reshape(-1, D), i["L0_ffn_sw3"]]).T.reshape(D, 9, P),
            "w2": rows(np.concatenate([i["L0_ffn_w2"].swapaxes(1, 2).reshape(-1, D), i["L0_ffn_sw2"].T])),
            "b1": rows(np.concatenate([i["L0_ffn_b1"].reshape(-1), i["L0_ffn_sb1"]])),
            "b3": rows(np.concatenate([i["L0_ffn_b3"].reshape(-1), i["L0_ffn_sb3"]])),
            "b2": np.concatenate([i["L0_ffn_b2"], i["L0_ffn_sb2"][None]]),
        },
        "f2": {
            "gate_w": i["L2_ffn_Wg"].T, "gate_b": everywhere(i["L2_ffn_bg"]),
            "w2": i["L2_ffn_We"].transpose(2, 0, 1), "b2": i["L2_ffn_be"],
        },
        "f3": {
            "gate_w": i["L3_ffn_gate_w"], "dom": i["L3_ffn_dom"].T,
            "w1": i["L3_ffn_W1"].transpose(1, 0, 2).reshape(D, 32, P),
            "w3": i["L3_ffn_W3"].transpose(1, 0, 2).reshape(D, 32, P),
            "w2": rows(i["L3_ffn_W2"].reshape(-1, D)),
        },
        "r1": {"w_v": i["L1_attn_Wv"].T, "w_o": i["L1_attn_Wo"].T, "freqs": i["L1_attn_freqs"][:, None]},
        "g2": {
            "w_ab": np.concatenate([i["L2_attn_a_w"], i["L2_attn_b_w"]]).T,
            "ab_bias": everywhere(np.concatenate([i["L2_attn_dt_bias"], np.zeros(8, np.float32)])),
            "a_log": everywhere(i["L2_attn_A_log"]), "norm_w": i["L2_attn_norm_w"][:, None],
            "w_qkv": i["L2_attn_qkv_w"].reshape(3, 8, P, D).transpose(3, 1, 0, 2),
            "taps": i["L2_attn_conv_w"].reshape(3, 8, P, 4).transpose(2, 1, 0, 3),
            "w_z": i["L2_attn_z_w"].reshape(8, P, D).transpose(2, 0, 1),
            "w_o": i["L2_attn_out_w"].reshape(D, 8, P).transpose(2, 1, 0),
        },
    }


def kernel(**inputs):
    import concourse.bacc as bacc
    from concourse.bass_utils import run_bass_kernel_spmd

    nc = bacc.Bacc("TRN2", target_bir_lowering=False, num_devices=1)
    arrays = {"x": np.ascontiguousarray(np.asarray(inputs["L0_attn_x"]).reshape(N, D))}
    d_in = {"x": nc.dram_tensor("x_dram", [N, D], F32, kind="ExternalInput").ap()}
    arrays = {"x_dram": arrays["x"]}
    for side, tensors in lay_out(inputs).items():
        d_in[side] = {}
        for name, a in tensors.items():
            a = np.ascontiguousarray(a)
            arrays[f"{side}_{name}_dram"] = a
            d_in[side][name] = nc.dram_tensor(f"{side}_{name}_dram", a.shape, F32, kind="ExternalInput").ap()
    out = nc.dram_tensor("out_dram", [N, D], F32, kind="ExternalOutput").ap()
    build(nc, d_in, out)
    r = run_bass_kernel_spmd(nc, [arrays], core_ids=[0])
    return r.results[0]["out_dram"].reshape(BATCH, T, D)
```

```python
from contextlib import ExitStack

import numpy as np

import concourse.bass as bass
from concourse import mybir

F32 = mybir.dt.float32
BF16 = mybir.dt.bfloat16
I32 = mybir.dt.int32
U32 = mybir.dt.uint32
ALU = mybir.AluOpType
ACT = mybir.ActivationFunctionType
AX = mybir.AxisListType

LN_EXP = "natural_log_exp_and_others"
P = 128
BATCH = 8
T = 256
D = 128
N = BATCH * T
TILES = N // P
GROUP = 512
GROUPS = N // GROUP
TPG = GROUP // P
SPG = GROUP // T
EPS = 1e-5


class Shared:
    pass


class Chain:

    def __init__(self, eng, sem, base=0):
        self.eng, self.sem, self.base, self.count = eng, sem, base, 0

    def add(self, ins):
        ins.then_inc(self.sem, 1)
        self.count += 1

    def settle(self, behind=0):
        self.eng.wait_ge(self.sem, self.base + self.count - behind)

    def step(self, ins):
        self.add(ins)
        self.settle()


class Signals:

    def __init__(self, nc, tag):
        self.nc, self.tag, self.stack, self.all = nc, tag, ExitStack(), []

    def __enter__(self):
        return self

    def __call__(self, name):
        self.all.append(self.stack.enter_context(self.nc.semaphore(f"{self.tag}_{name}")))
        return self.all[-1]

    def __exit__(self, *_):
        with self.nc.Block() as block:
            @block.sync
            def _(sp):
                for s in self.all:
                    sp.sem_clear(s)
        self.stack.close()


def tok(c):
    return slice(c * GROUP, (c + 1) * GROUP)


def spread(ap, n):
    return ap.unsqueeze(2).to_broadcast([ap.shape[0], ap.shape[1], n])


def wait_apart(eng, sem, value, passed):
    eng.wait_ge(sem, value)
    eng.sem_inc(passed, 1)


def set_up(nc, g, x_dram):
    with ExitStack() as ctx:
        sem = ctx.enter_context(Signals(nc, "setup"))
        loaded, filled = sem("loaded"), sem("filled")
        block = ctx.enter_context(nc.Block())

        @block.sync
        def _(sp):
            sp.dma_start(g.x[:, :, :], x_dram.rearrange("(n p) d -> p n d", p=P)).then_inc(loaded, 16)
            sp.wait_ge(loaded, 16)

        @block.gpsimd
        def _(pool):
            pool.memset(g.ident[:, :], 0.0).then_inc(filled, 1)
            pool.memset(g.eps[:, :], EPS).then_inc(filled, 1)
            pool.memset(g.one[:, :], 1.0).then_inc(filled, 1)
            pool.wait_ge(filled, 3)
            pool.affine_select(out=g.ident[:, :], in_=g.ident[:, :], compare_op=ALU.not_equal, fill=1.0, base=0,
                               pattern=[[-1, P]], channel_multiplier=1).then_inc(filled, 1)


def norm_and_turn(nc, g, tag, loads, gate_loads=()):
    with ExitStack() as ctx:
        sem = ctx.enter_context(Signals(nc, tag))
        st = ctx.enter_context(nc.sbuf_tensor(f"{tag}_stats", [P, 5, TILES], F32))
        xc = ctx.enter_context(nc.sbuf_tensor(f"{tag}_xc", [P, TILES, D], F32))
        sq = ctx.enter_context(nc.sbuf_tensor(f"{tag}_sq", [P, TILES, D], F32))
        centred, squared, var_ready, rstd_ready = sem("centred"), sem("squared"), sem("var"), sem("rstd")
        normed, turned, dve_own, act_own = sem("normed"), sem("turned"), sem("dve"), sem("act")
        block = ctx.enter_context(nc.Block())

        @block.sync
        def _(sp):
            for dst, src in gate_loads:
                sp.dma_start(dst, src).then_inc(g.gate_weights, 16)
                g.gate_weights_due += 16
            for dst, src in loads:
                sp.dma_start(dst, src).then_inc(g.weights, 16)
                g.weights_due += 16

        @block.vector
        def _(dve):
            own = Chain(dve, dve_own)
            groups = [slice(TPG * c, TPG * (c + 1)) for c in range(GROUPS)]
            for t in groups:
                own.add(dve.tensor_reduce(st[:, 0, t], g.x[:, t, :], AX.X, ALU.add))
            own.settle()
            own.step(dve.tensor_scalar(st[:, 1, :], st[:, 0, :], -1.0 / D, None, ALU.mult))
            for t in groups:
                dve.tensor_tensor(xc[:, t, :], g.x[:, t, :], spread(st[:, 1, t], D), ALU.add).then_inc(centred, 1)
            for c, t in enumerate(groups):
                dve.wait_ge(squared, c + 1)
                dve.tensor_reduce(st[:, 2, t], sq[:, t, :], AX.X, ALU.add).then_inc(var_ready, 1)
            for c, t in enumerate(groups):
                dve.wait_ge(rstd_ready, c + 1)
                dve.tensor_tensor(g.xn[:, t, :], xc[:, t, :], spread(st[:, 4, t], D), ALU.mult).then_inc(normed, 1)

        @block.scalar
        def _(act):
            act.preload_act_table_set(LN_EXP)
            groups = [slice(TPG * c, TPG * (c + 1)) for c in range(GROUPS)]
            for c, t in enumerate(groups):
                act.wait_ge(centred, c + 1)
                act.activation(sq[:, t, :], xc[:, t, :], ACT.Square).then_inc(squared, 1)
            for c, t in enumerate(groups):
                act.wait_ge(var_ready, c + 1)
                act.activation(st[:, 3, t], st[:, 2, t], ACT.Ln, bias=g.eps[:, 0:1], scale=1.0 / D).then_inc(act_own, 1)
                act.wait_ge(act_own, c + 1)
                act.activation(st[:, 4, t], st[:, 3, t], ACT.Exp, scale=-0.5).then_inc(rstd_ready, 1)
            for c in range(GROUPS):
                act.wait_ge(turned, c + 1)
                act.activation(g.xnT[:, tok(c)], g.bank[c][:, :], ACT.Copy)

        @block.tensor
        def _(pe):
            for c in range(GROUPS):
                pe.wait_ge(normed, c + 1)
                for i in range(TPG):
                    mm = pe.transpose(g.bank[c][:, i * P:(i + 1) * P], g.xn[:, TPG * c + i, :], g.ident[:, :])
                mm.then_inc(turned, 1)


def mamba(nc, g, tag, w, d_in):
    HALVES, STATES, TAPS = 2, 16, 4
    rank_one_dt = "w_dt_col" in d_in
    with ExitStack() as ctx:
        sem = ctx.enter_context(Signals(nc, tag))

        def sb(n, shape, dt=F32):
            return ctx.enter_context(nc.sbuf_tensor(f"{tag}_{n}", shape, dt))
        w_in = sb("w_in", [P, 4 * P])
        conv_w, conv_b = sb("conv_w", [P, HALVES, TAPS]), sb("conv_b", [P, HALVES])
        w_bc = sb("w_bc", [P, HALVES, 2 * STATES])
        w_dt = sb("w_dt", [1, HALVES * P] if rank_one_dt else [P, HALVES, HALVES * P])
        w_dtc = sb("w_dtc", [P, HALVES])
        b_dt, a_log, skip = sb("b_dt", [P, HALVES]), sb("a_log", [P, HALVES, STATES]), sb("skip", [P, HALVES])
        w_out = sb("w_out", [P, HALVES, D])
        loads = [(w_in[:, :], d_in["w_in"]), (conv_w[:, :, :], d_in["conv_w"]), (conv_b[:, :], d_in["conv_b"]),
                 (w_bc[:, :, :], d_in["w_bc"]), (b_dt[:, :], d_in["b_dt"]), (a_log[:, :, :], d_in["a_log"]),
                 (skip[:, :], d_in["skip"]), (w_out[:, :, :], d_in["w_out"])]
        if rank_one_dt:
            loads += [(w_dt[:, :], d_in["w_dt"]), (w_dtc[:, :], d_in["w_dt_col"])]
        else:
            loads += [(w_dt[:, :, :], d_in["w_dt"])]
        norm_and_turn(nc, g, tag + "_ln", loads)

        xpad = sb("xpad", [P, HALVES, BATCH, T + TAPS - 1])
        cv = sb("cv", [P, HALVES, N])
        u = sb("u", [P, HALVES, N])
        sz = sb("sz", [P, HALVES, N])
        dt = sb("dt", [P, HALVES, N])
        du = sb("du", [P, HALVES, N])
        bc3 = sb("bc3", [3 * 32, N], BF16)
        part = sb("part", [32, 2, N], BF16)
        rest = sb("rest", [32, 2, N])
        dt_row = sb("dt_row", [1, N])
        pick = sb("pick", [3 * 32, 2 * STATES, P], BF16)
        a_neg = sb("a_neg", [P, HALVES, STATES])
        decay = sb("decay", [P, 2, HALVES, SPG, T])
        dbu = sb("dbu", [P, 2, HALVES, GROUP])
        state = sb("state", [P, 2, HALVES, GROUP])
        c_all = sb("c_all", [P, 2, GROUP])
        hc = sb("hc", [P, 2, HALVES, GROUP])
        y = dbu[:, 1, :, :]

        prepared, picked = sem("prepared"), sem("picked")
        proj_ready, proj_used, conv_ready, u_ready = sem("proj_ready"), sem("proj_used"), sem("conv_ready"), sem("u_ready")
        bc_ready, bc_split, bc_moved = sem("bc_ready"), sem("bc_split"), sem("bc_moved")
        row_ready, row_copied, dt_psum, dt_biased = sem("row_ready"), sem("row_copied"), sem("dt_psum"), sem("dt_biased")
        log_ready, a_exp, scan_inputs = sem("log_ready"), sem("a_exp"), sem("scan_inputs")
        spread_ready, spread_used = sem("spread_ready"), sem("spread_used")
        decay_ready, scanned, c_copied = sem("decay_ready"), sem("scanned"), sem("c_copied")
        hc_ready, hc_used, sum_ready, sum_used = sem("hc_ready"), sem("hc_used"), sem("sum_ready"), sem("sum_used")
        y_ready, out_ready, out_used = sem("y_ready"), sem("out_ready"), sem("out_used")
        dve_own, act_own, act_passed = sem("dve"), sem("act"), sem("act_passed")
        block = ctx.enter_context(nc.Block())

        @block.gpsimd
        def _(pool):
            pool.memset(pick[:, :, :], 0.0).then_inc(picked, 1)
            for k in range(3):
                pool.wait_ge(picked, k + 1)
                pool.affine_select(out=pick[:, :, :], in_=pick[:, :, :], compare_op=ALU.not_equal, fill=1.0,
                                   base=-32 * k, pattern=[[-1, 2 * STATES], [0, P]],
                                   channel_multiplier=1).then_inc(picked, 1)
            with pool.Fori(0, GROUPS) as c:
                for s in range(STATES):
                    b = s % 2
                    pool.wait_ge(c_copied, c * STATES + (2 + s + 1))
                    pool.wait_ge(hc_used, c * STATES + (s + 1))
                    for h in range(HALVES):
                        pool.wait_ge(scanned, c * (HALVES * STATES) + (2 * HALVES + HALVES * s + h + 1))
                        ins = pool.tensor_tensor(hc[:, b, h, :], state[:, b, h, :], c_all[:, b, :], ALU.mult)
                    ins.then_inc(hc_ready, 1)

        @block.tensor
        def _(pe):
            pe.wait_ge(g.weights, g.weights_due)
            for i in range(4 * GROUPS):
                m, c = divmod(i, GROUPS)
                if i >= 8:
                    pe.wait_ge(proj_used, i - 7)
                pe.matmul(g.bank[i % 8][:, :], w_in[:, m * P:(m + 1) * P], g.xnT[:, tok(c)],
                          start=True, stop=True).then_inc(proj_ready, 1)
            pe.wait_ge(u_ready, HALVES)
            for c in range(GROUPS):
                pe.wait_ge(proj_used, 9 + c)
                for h in range(HALVES):
                    mm = pe.matmul(g.bank[c][0:2 * STATES, :], w_bc[:, h, :], u[:, h, tok(c)],
                                   start=(h == 0), stop=(h == 1))
                mm.then_inc(bc_ready, 1)
            pe.wait_ge(proj_used, 4 * GROUPS)
            if rank_one_dt:
                for c in range(GROUPS):
                    for h in range(HALVES):
                        mm = pe.matmul(g.bank[4 + c][0:1, :], w_dtc[:, h:h + 1], u[:, h, tok(c)],
                                       start=(h == 0), stop=(h == 1))
                    mm.then_inc(row_ready, 1)
            pe.wait_ge(bc_split, 1)
            for i in range(HALVES * GROUPS):
                h, c = divmod(i, GROUPS)
                if rank_one_dt:
                    pe.wait_ge(row_copied, GROUPS)
                    pe.matmul(g.bank[i][:, :], w_dt[0:1, h * P:(h + 1) * P], dt_row[0:1, tok(c)],
                              start=True, stop=True).then_inc(dt_psum, 1)
                else:
                    for k in range(HALVES):
                        mm = pe.matmul(g.bank[i][:, :], w_dt[:, k, h * P:(h + 1) * P], u[:, k, tok(c)],
                                       start=(k == 0), stop=(k == 1))
                    mm.then_inc(dt_psum, 1)
            pe.wait_ge(dt_biased, HALVES * GROUPS)
            pe.wait_ge(bc_moved, 2)
            pe.wait_ge(picked, 4)
            with pe.Fori(0, GROUPS) as c:
                def sum_state(s):
                    pe.wait_ge(hc_ready, c * STATES + (2 + s + 1))
                    if s == 0:
                        pe.wait_ge(sum_used, c + 1)
                    for h in range(HALVES):
                        mm = pe.matmul(g.bank[4 + h][:, :], g.ident[:, :], hc[:, s % 2, h, :],
                                       start=(s == 0), stop=(s == STATES - 1))
                    mm.then_inc(hc_used, 1)
                    if s == STATES - 1:
                        pe.wait_ge(hc_used, c * STATES + (s + 3))
                        pe.sem_inc(sum_ready, 1)
                for s in range(STATES):
                    b = s % 2
                    pe.wait_ge(spread_used, c * STATES + (s + 1))
                    pe.wait_ge(c_copied, c * STATES + (s + 1))
                    pe.matmul(g.bank[b][:, :], pick[:, s, :], bc3[:, bass.ts(c, GROUP)], start=True, stop=True)
                    pe.matmul(g.bank[2 + b][:, :], pick[:, STATES + s, :], bc3[:, bass.ts(c, GROUP)],
                              start=True, stop=True).then_inc(spread_ready, 1)
                    if s >= 2:
                        sum_state(s - 2)
                sum_state(STATES - 2)
                sum_state(STATES - 1)
                pe.wait_ge(y_ready, c + 1)
                pe.wait_ge(out_used, c + 1)
                for i in range(TPG):
                    for h in range(HALVES):
                        mm = pe.matmul(g.bank[6][:, i * P:(i + 1) * P], y[:, h, i * P:(i + 1) * P], w_out[:, h, :],
                                       start=(h == 0), stop=(h == 1))
                mm.then_inc(out_ready, 1)

        @block.scalar
        def _(act):
            own = Chain(act, act_own)
            act.wait_ge(prepared, 1)
            for i in range(4 * GROUPS):
                m, c = divmod(i, GROUPS)
                act.wait_ge(proj_ready, i + 1)
                if m < 2:
                    act.activation(xpad[:, m, SPG * c:SPG * (c + 1), TAPS - 1:],
                                   g.bank[i % 8][:, :].rearrange("p (b t) -> p b t", t=T), ACT.Copy).then_inc(proj_used, 1)
                else:
                    act.activation(sz[:, m - 2, tok(c)], g.bank[i % 8][:, :], ACT.Silu).then_inc(proj_used, 1)
            for h in range(HALVES):
                act.wait_ge(conv_ready, h + 1)
                act.activation(u[:, h, :], cv[:, h, :], ACT.Silu, bias=conv_b[:, h:h + 1]).then_inc(u_ready, 1)
            if rank_one_dt:
                for c in range(GROUPS):
                    act.wait_ge(row_ready, c + 1)
                    act.activation(dt_row[0:1, tok(c)], g.bank[4 + c][0:1, :], ACT.Copy).then_inc(row_copied, 1)
            act.wait_ge(bc_split, 1)
            act.activation(bc3[32:64, :], part[:, 1, :], ACT.Copy).then_inc(bc_moved, 1)
            for i in range(HALVES * GROUPS):
                h, c = divmod(i, GROUPS)
                act.wait_ge(dt_psum, i + 1)
                act.activation(dt[:, h, tok(c)], g.bank[i][:, :], ACT.Identity, bias=b_dt[:, h:h + 1]).then_inc(dt_biased, 1)
            act.preload_act_table_set(LN_EXP)
            for h in range(HALVES):
                act.wait_ge(dt_biased, GROUPS * (h + 1))
                own.step(act.activation(cv[:, h, :], dt[:, h, :], ACT.Abs))
                own.step(act.activation(cv[:, h, :], cv[:, h, :], ACT.Exp, scale=-1.0))
                act.activation(cv[:, h, :], cv[:, h, :], ACT.Ln, bias=g.one[:, 0:1]).then_inc(log_ready, 1)
            act.activation(a_neg[:, :, :], a_log[:, :, :], ACT.Exp).then_inc(a_exp, 1)
            act.sem_inc(c_copied, 2)
            act.wait_ge(scan_inputs, 1)
            with act.Fori(0, GROUPS) as c:
                for s in range(STATES):
                    wait_apart(act, scanned, c * (HALVES * STATES) + (HALVES * s + 2), act_passed)
                    for h in range(HALVES):
                        ins = act.activation(
                            decay[:, s % 2, h, :, 1:T],
                            dt[:, h, bass.ts(c, GROUP)].rearrange("p (b t) -> p b t", t=T)[:, :, 1:T],
                            ACT.Exp, scale=a_neg[:, h, s:s + 1])
                    ins.then_inc(decay_ready, 1)
                    act.wait_ge(spread_ready, c * STATES + (s + 1))
                    act.wait_ge(hc_ready, c * STATES + (s + 1))
                    act.activation(c_all[:, s % 2, :], g.bank[2 + s % 2][:, :], ACT.Copy).then_inc(c_copied, 1)

        @block.vector
        def _(dve):
            own = Chain(dve, dve_own)
            own.add(dve.memset(xpad[:, :, :, 0:TAPS - 1], 0.0))
            own.add(dve.memset(decay[:, :, :, :, 0:1], 0.0))
            own.settle()
            dve.sem_inc(prepared, 1)
            for h in range(HALVES):
                dve.wait_ge(proj_used, GROUPS * (h + 1))
                cvh = cv[:, h, :].rearrange("p (b t) -> p b t", t=T)
                own.step(dve.tensor_scalar(cvh, xpad[:, h, :, 0:T], conv_w[:, h, 0:1], None, ALU.mult))
                for k in range(1, TAPS):
                    ins = dve.scalar_tensor_tensor(out=cvh, in0=xpad[:, h, :, k:k + T], scalar=conv_w[:, h, k:k + 1],
                                                   in1=cvh, op0=ALU.mult, op1=ALU.add)
                    if k < TAPS - 1:
                        own.step(ins)
                ins.then_inc(conv_ready, 1)
            for c in range(GROUPS):
                dve.wait_ge(bc_ready, c + 1)
                own.step(dve.tensor_copy(bc3[0:32, tok(c)], g.bank[c][0:32, :]))
                own.add(dve.tensor_tensor(rest[:, 0, tok(c)], g.bank[c][0:32, :], bc3[0:32, tok(c)], ALU.subtract))
            own.settle()
            own.step(dve.tensor_copy(part[:, 1, :], rest[:, 0, :]))
            dve.tensor_tensor(bc3[64:96, :], rest[:, 0, :], part[:, 1, :], ALU.subtract).then_inc(bc_split, 1)
            dve.wait_ge(bc_split, 1)
            dve.sem_inc(bc_moved, 1)
            for h in range(HALVES):
                dve.wait_ge(log_ready, h + 1)
                own.step(dve.scalar_tensor_tensor(out=dt[:, h, :], in0=dt[:, h, :], scalar=0.0, in1=cv[:, h, :],
                                                  op0=ALU.max, op1=ALU.add))
                own.add(dve.tensor_tensor(du[:, h, :], dt[:, h, :], u[:, h, :], ALU.mult))
            dve.wait_ge(a_exp, 1)
            own.step(dve.tensor_scalar(a_neg[:, :, :], a_neg[:, :, :], -1.0, None, ALU.mult))
            dve.sem_inc(scan_inputs, 1)
            for free, n in ((scanned, 2 * HALVES), (spread_used, 2), (hc_ready, 2), (hc_used, 2), (sum_used, 1), (out_used, 1)):
                dve.sem_inc(free, n)
            STEPS_PER_GROUP = 2 * STATES + HALVES
            with dve.Fori(0, GROUPS) as c:
                own = Chain(dve, dve_own, c * STEPS_PER_GROUP + own.count)
                for s in range(STATES):
                    b = s % 2
                    dve.wait_ge(spread_ready, c * STATES + (s + 1))
                    dve.wait_ge(scanned, c * (HALVES * STATES) + (HALVES * s + 2))
                    for h in range(HALVES):
                        own.add(dve.tensor_tensor(dbu[:, b, h, :], du[:, h, bass.ts(c, GROUP)], g.bank[b][:, :], ALU.mult))
                    dve.wait_ge(decay_ready, c * STATES + (s + 1))
                    dve.wait_ge(hc_ready, c * STATES + (s + 1))
                    for h in range(HALVES):
                        own.settle(behind=1 - h)
                        if h == 1:
                            dve.sem_inc(spread_used, 1)
                        dve.tensor_tensor_scan(state[:, b, h, :], decay[:, b, h, :, :].rearrange("p b t -> p (b t)"),
                                               dbu[:, b, h, :], 0.0, ALU.mult, ALU.add).then_inc(scanned, 1)
                dve.wait_ge(sum_ready, c + 1)
                for h in range(HALVES):
                    own.add(dve.scalar_tensor_tensor(out=state[:, 0, h, :], in0=u[:, h, bass.ts(c, GROUP)],
                                                     scalar=skip[:, h:h + 1], in1=g.bank[4 + h][:, :],
                                                     op0=ALU.mult, op1=ALU.add))
                own.settle()
                dve.sem_inc(sum_used, 1)
                for h in range(HALVES):
                    ins = dve.tensor_tensor(y[:, h, :], state[:, 0, h, :], sz[:, h, bass.ts(c, GROUP)], ALU.mult)
                ins.then_inc(y_ready, 1)
                dve.wait_ge(out_ready, c + 1)
                x_c = g.x[:, bass.ts(c, TPG), :]
                dve.tensor_tensor(x_c, x_c, g.bank[6][:, :].rearrange("p (n d) -> p n d", d=D), ALU.add).then_inc(out_used, 1)
                assert own.count == STEPS_PER_GROUP


def route(nc, g, tag, experts, gates, gates_t, gates3, gate_w, bias, sigmoid_scores):
    E = experts
    with ExitStack() as ctx:
        sem = ctx.enter_context(Signals(nc, tag))

        def sb(n, shape, dt=F32):
            return ctx.enter_context(nc.sbuf_tensor(f"{tag}_{n}", shape, dt))
        raw, ranked = sb("raw", [P, TILES, E]), sb("ranked", [P, TILES, E])
        top, top_index = sb("top", [P, TILES, 8]), sb("top_index", [P, TILES, 8], U32)
        index = sb("index", [P, TILES, 8])
        number = sb("number", [P, TILES, E])
        first, second = sb("first", [P, TILES, E]), sb("second", [P, TILES, E])
        soft, weight = sb("soft", [P, TILES, E]), sb("weight", [P, 4, TILES])
        rest, part = sb("rest", [32, N]), sb("part", [32, N], BF16)
        logits, numbered, exp_in, exp_out = sem("logits"), sem("numbered"), sem("exp_in"), sem("exp_out")
        gated, turned, split, own_sem = sem("gated"), sem("turned"), sem("split"), sem("dve")
        block = ctx.enter_context(nc.Block())

        @block.gpsimd
        def _(pool):
            pool.iota(number[:, :, :], pattern=[[0, TILES], [1, E]], base=0, channel_multiplier=0,
                      allow_small_or_imprecise_dtypes=True).then_inc(numbered, 1)

        @block.tensor
        def _(pe):
            pe.wait_ge(g.gate_weights, g.gate_weights_due)
            for t in range(TILES):
                mm = pe.matmul(g.bank[0][:, t * E:(t + 1) * E], g.xnT[:, t * P:(t + 1) * P], gate_w,
                               start=(t == 0), stop=(t == TILES - 1), skip_group_check=True)
            mm.then_inc(logits, 1)
            pe.wait_ge(gated, 1)
            for t in range(TILES):
                mm = pe.transpose(g.bank[1 + t // TPG][0:E, (t % TPG) * P:(t % TPG + 1) * P], gates[:, t, :], g.ident[:, :])
            mm.then_inc(turned, 1)

        @block.scalar
        def _(act):
            act.wait_ge(exp_in, 1)
            if sigmoid_scores:
                act.activation(soft[:, :, :], raw[:, :, :], ACT.Exp, scale=-1.0).then_inc(exp_out, 1)
            else:
                act.activation(weight[:, 1, :], weight[:, 0, :], ACT.Exp).then_inc(exp_out, 1)
            act.wait_ge(split, 1)
            act.activation(gates3[32:64, :], part[:, :], ACT.Copy)

        @block.vector
        def _(dve):
            own = Chain(dve, own_sem)
            own.add(dve.memset(gates3[:, :], 0.0))
            own.add(dve.memset(gates_t[:, :], 1.0))
            own.add(dve.memset(part[:, :], 0.0))
            own.add(dve.memset(rest[:, :], 0.0))
            dve.wait_ge(logits, 1)
            lg = g.bank[0][:, 0:TILES * E].rearrange("p (n e) -> p n e", e=E)
            own.add(dve.tensor_copy(raw[:, :, :], lg))
            own.step(dve.tensor_tensor(ranked[:, :, :], lg, bias.unsqueeze(1).to_broadcast([P, TILES, E]), ALU.add))
            for t in range(TILES):
                own.add(dve.max(top[:, t, :], ranked[:, t, :]))
            own.settle()
            for t in range(TILES):
                own.add(dve.max_index(top_index[:, t, :], top[:, t, :], ranked[:, t, :]))
            own.settle()
            own.step(dve.tensor_copy(index[:, :, :], top_index[:, :, :]))
            dve.wait_ge(numbered, 1)
            own.add(dve.tensor_tensor(first[:, :, :], number[:, :, :], spread(index[:, :, 0], E), ALU.is_equal))
            own.add(dve.tensor_tensor(second[:, :, :], number[:, :, :], spread(index[:, :, 1], E), ALU.is_equal))
            own.settle()
            if sigmoid_scores:
                dve.sem_inc(exp_in, 1)
                own.step(dve.tensor_tensor(first[:, :, :], first[:, :, :], second[:, :, :], ALU.add))
                dve.wait_ge(exp_out, 1)
                own.step(dve.tensor_scalar(soft[:, :, :], soft[:, :, :], 1.0, None, ALU.add))
                own.step(dve.reciprocal(soft[:, :, :], soft[:, :, :]))
                own.step(dve.tensor_tensor(soft[:, :, :], soft[:, :, :], first[:, :, :], ALU.mult))
                own.step(dve.tensor_reduce(weight[:, 0, :], soft[:, :, :], AX.X, ALU.add))
                own.step(dve.tensor_scalar(weight[:, 1, :], weight[:, 0, :], 1e-10, None, ALU.add))
                own.step(dve.reciprocal(weight[:, 2, :], weight[:, 1, :]))
                own.step(dve.tensor_tensor(gates[:, :, :], soft[:, :, :], spread(weight[:, 2, :], E), ALU.mult))
            else:
                own.step(dve.tensor_tensor(weight[:, 0, :], top[:, :, 1], top[:, :, 0], ALU.subtract))
                dve.sem_inc(exp_in, 1)
                dve.wait_ge(exp_out, 1)
                own.step(dve.tensor_scalar(weight[:, 2, :], weight[:, 1, :], 1.0, None, ALU.add))
                own.step(dve.reciprocal(weight[:, 3, :], weight[:, 2, :]))
                own.step(dve.tensor_tensor(weight[:, 2, :], weight[:, 1, :], weight[:, 3, :], ALU.mult))
                own.add(dve.tensor_tensor(first[:, :, :], first[:, :, :], spread(weight[:, 3, :], E), ALU.mult))
                own.step(dve.tensor_tensor(second[:, :, :], second[:, :, :], spread(weight[:, 2, :], E), ALU.mult))
                own.step(dve.tensor_tensor(gates[:, :, :], first[:, :, :], second[:, :, :], ALU.add))
            dve.sem_inc(gated, 1)
            dve.wait_ge(turned, 1)
            for c in range(GROUPS):
                own.add(dve.tensor_copy(gates_t[0:E, tok(c)], g.bank[1 + c][0:E, :]))
            own.settle()
            own.step(dve.tensor_copy(gates3[0:E, :], gates_t[0:E, :]))
            own.step(dve.tensor_tensor(rest[0:E, :], gates_t[0:E, :], gates3[0:E, :], ALU.subtract))
            own.step(dve.tensor_copy(part[0:E, :], rest[0:E, :]))
            dve.tensor_tensor(gates3[64:96, :], rest[:, :], part[:, :], ALU.subtract).then_inc(split, 1)


def moe(nc, g, tag, d_in, experts, chunks, gate_of, biased, sigmoid_scores, domains):
    E = experts
    gated_mlp = "w1" in d_in
    SETS = max((gate_of(j) for j in range(chunks) if gate_of(j) is not None)) + 1
    HALF_SETS = SETS * 2 == E
    with ExitStack() as ctx:
        sem = ctx.enter_context(Signals(nc, tag))

        def sb(n, shape, dt=F32):
            return ctx.enter_context(nc.sbuf_tensor(f"{tag}_{n}", shape, dt))
        gate_w, gate_b = sb("gate_w", [P, E]), sb("gate_b", [P, E])
        w2 = sb("w2", [P, chunks, D])
        gate_loads, loads = [(gate_w[:, :], d_in["gate_w"])], [(w2[:, :, :], d_in["w2"])]
        if "gate_b" in d_in:
            gate_loads.append((gate_b[:, :], d_in["gate_b"]))
        if gated_mlp:
            w1, w3 = sb("w1", [P, chunks, P]), sb("w3", [P, chunks, P])
            loads += [(w1[:, :, :], d_in["w1"]), (w3[:, :, :], d_in["w3"])]
            b1, b3 = sb("b1", [P, chunks]), sb("b3", [P, chunks])
            if domains:
                dom = sb("dom", [P, E])
                loads.append((dom[:, :], d_in["dom"]))
            else:
                loads += [(b1[:, :], d_in["b1"]), (b3[:, :], d_in["b3"])]
        B_ROWS = 0
        if biased:
            B_ROWS = d_in["b2"].shape[0]
            b2 = sb("b2", [B_ROWS, D])
            loads.append((b2[:, :], d_in["b2"]))
        norm_and_turn(nc, g, tag + "_ln", loads, gate_loads)

        gates, gates_t = sb("gates", [P, TILES, E]), sb("gates_t", [32, N])
        gates3 = sb("gates3", [96, N], BF16)
        pick = sb("pick", [96, SETS, P], BF16)
        zero_b = sem("no_bias")
        if "gate_b" not in d_in:
            with nc.Block() as block:
                @block.gpsimd
                def _(pool):
                    pool.memset(gate_b[:, :], 0.0).then_inc(zero_b, 1)
        route(nc, g, tag + "_route", E, gates, gates_t, gates3, gate_w[:, :], gate_b[:, :], sigmoid_scores)

        silu = sb("silu", [P, 2, GROUP])
        prod = sb("prod", [P, 2, GROUP])
        gated = sb("gated", [P, 2, GROUP])
        gt_c = sb("gt_c", [32, GROUP])
        picked, hidden_ready, silu_ready, hidden_used = sem("picked"), sem("hidden_ready"), sem("silu_ready"), sem("hidden_used")
        spread_ready, spread_used, gated_ready, gated_used = sem("spread_ready"), sem("spread_used"), sem("gated_ready"), sem("gated_used")
        sum_ready, sum_used, gt_ready, gt_used = sem("sum_ready"), sem("sum_used"), sem("gt_ready"), sem("gt_used")
        dom_ready, dom_copied, act_passed = sem("dom_ready"), sem("dom_copied"), sem("act_passed")
        spread_at = {}
        for j in range(chunks):
            if gate_of(j) is not None:
                spread_at[j] = gate_of(j)
        last_use = {s: max(j for j in spread_at if spread_at[j] == s) for s in range(SETS)}
        assert SETS % 2 == 0 and chunks >= 2
        block = ctx.enter_context(nc.Block())

        @block.gpsimd
        def _(pool):
            pool.memset(pick[:, :, :], 0.0).then_inc(picked, 1)
            for k in range(3):
                pool.wait_ge(picked, k + 1)
                if HALF_SETS:
                    out = pick[:, :, :].rearrange("k s (h p) -> k s h p", h=2)
                    pattern = [[-2, SETS], [-1, 2], [0, P // 2]]
                else:
                    out, pattern = pick[:, :, :], [[-1, SETS], [0, P]]
                pool.affine_select(out=out, in_=out, compare_op=ALU.not_equal, fill=1.0, base=-32 * k,
                                   pattern=pattern, channel_multiplier=1).then_inc(picked, 1)

        @block.tensor
        def _(pe):
            pe.wait_ge(g.weights, g.weights_due)
            if domains:
                for k, w in enumerate((w1, w3)):
                    for j in range(chunks):
                        e = gate_of(j)
                        mm = pe.matmul(g.bank[7][:, k * chunks + j:k * chunks + j + 1], w[:, j, :], dom[:, e:e + 1],
                                       start=(j == 0 and k == 0), stop=(j == chunks - 1 and k == 1), skip_group_check=True)
                mm.then_inc(dom_ready, 1)
            pe.wait_ge(picked, 4)
            with pe.Fori(0, GROUPS) as c:
                def add_chunk(j):
                    pe.wait_ge(gated_ready, c * chunks + (j + 1))
                    if j == 0:
                        pe.wait_ge(sum_used, c + 1)
                    for i in range(TPG):
                        mm = pe.matmul(g.bank[6][:, i * P:(i + 1) * P], gated[:, j % 2, i * P:(i + 1) * P],
                                       w2[:, j, :], start=(j == 0 and i == 0),
                                       stop=(not biased and j == chunks - 1), skip_group_check=True)
                    mm.then_inc(gated_used, 1)
                for j in range(chunks):
                    b = j % 2
                    if j in spread_at and (j == 0 or spread_at[j] != spread_at.get(j - 1)):
                        s = spread_at[j]
                        pe.wait_ge(spread_used, c * SETS + (s + 1))
                        pe.matmul(g.bank[4 + s % 2][:, :], pick[:, s, :], gates3[:, bass.ts(c, GROUP)],
                                  start=True, stop=True).then_inc(spread_ready, 1)
                    if gated_mlp:
                        pe.wait_ge(hidden_used, c * chunks + (j + 1))
                        pe.matmul(g.bank[b][:, :], w1[:, j, :], g.xnT[:, bass.ts(c, GROUP)], start=True, stop=True)
                        pe.matmul(g.bank[2 + b][:, :], w3[:, j, :], g.xnT[:, bass.ts(c, GROUP)],
                                  start=True, stop=True).then_inc(hidden_ready, 1)
                    if j >= 1:
                        add_chunk(j - 1)
                add_chunk(chunks - 1)
                if biased:
                    pe.wait_ge(gt_ready, c + 1)
                    for i in range(TPG):
                        mm = pe.matmul(g.bank[6][:, i * P:(i + 1) * P], gt_c[0:B_ROWS, i * P:(i + 1) * P], b2[:, :],
                                       start=False, stop=True, skip_group_check=True)
                    mm.then_inc(sum_ready, 1)
                else:
                    pe.wait_ge(gated_used, c * chunks + (chunks + 2))
                    pe.sem_inc(sum_ready, 1)

        @block.scalar
        def _(act):
            act.wait_ge(g.weights, g.weights_due)
            if domains:
                act.wait_ge(dom_ready, 1)
                act.activation(b1[:, :], g.bank[7][:, 0:chunks], ACT.Copy).then_inc(dom_copied, 1)
                act.activation(b3[:, :], g.bank[7][:, chunks:2 * chunks], ACT.Copy).then_inc(dom_copied, 1)
                act.wait_ge(dom_copied, 2)
            with act.Fori(0, GROUPS) as c:
                if biased:
                    wait_apart(act, gt_used, c + 1, act_passed)
                    act.activation(gt_c[:, :], gates_t[:, bass.ts(c, GROUP)], ACT.Copy).then_inc(gt_ready, 1)
                if gated_mlp:
                    for j in range(chunks):
                        act.wait_ge(hidden_used, c * chunks + (j + 1))
                        act.wait_ge(hidden_ready, c * chunks + (j + 1))
                        act.activation(silu[:, j % 2, :], g.bank[j % 2][:, :], ACT.Silu,
                                       bias=b1[:, j:j + 1]).then_inc(silu_ready, 1)

        @block.vector
        def _(dve):
            for free, n in ((spread_used, 2), (hidden_used, 2), (gated_used, 2), (sum_used, 1), (gt_used, 1)):
                dve.sem_inc(free, n)
            dve.wait_ge(g.weights, g.weights_due)
            if domains:
                dve.wait_ge(dom_copied, 2)
            with dve.Fori(0, GROUPS) as c:
                for j in range(chunks):
                    b = j % 2
                    if gated_mlp:
                        dve.wait_ge(silu_ready, c * chunks + (j + 1))
                        if j >= 2:
                            dve.wait_ge(gated_ready, c * chunks + (j - 1))
                        if j not in spread_at:
                            dve.wait_ge(gated_used, c * chunks + (j + 1))
                        source = prod[:, b, :] if j in spread_at else gated[:, b, :]
                        dve.scalar_tensor_tensor(out=source, in0=g.bank[2 + b][:, :], scalar=b3[:, j:j + 1],
                                                 in1=silu[:, b, :], op0=ALU.add, op1=ALU.mult).then_inc(hidden_used, 1)
                        dve.wait_ge(hidden_used, c * chunks + (j + 3))
                    else:
                        source = g.xnT[:, bass.ts(c, GROUP)]
                    if j in spread_at:
                        s = spread_at[j]
                        dve.wait_ge(spread_ready, c * SETS + (s + 1))
                        dve.wait_ge(gated_used, c * chunks + (j + 1))
                        dve.tensor_tensor(gated[:, b, :], source, g.bank[4 + s % 2][:, :], ALU.mult).then_inc(gated_ready, 1)
                        if last_use[s] == j:
                            dve.wait_ge(gated_ready, c * chunks + (j + 1))
                            dve.sem_inc(spread_used, 1)
                    else:
                        dve.sem_inc(gated_ready, 1)
                dve.wait_ge(sum_ready, c + 1)
                x_c = g.x[:, bass.ts(c, TPG), :]
                dve.tensor_tensor(x_c, x_c, g.bank[6][:, :].rearrange("p (n d) -> p n d", d=D), ALU.add).then_inc(sum_used, 1)
                if biased:
                    dve.sem_inc(gt_used, 1)


def two_pi_parts():
    parts, rest = [], 2 * np.pi
    for bits in (8, 11, 24):
        unit = 2.0 ** (np.floor(np.log2(rest)) + 1 - bits)
        parts.append(float(np.floor(rest / unit) * unit))
        rest -= parts[-1]
    return parts


def rotor_memory(nc, g, d_in):
    TWO_PI = two_pi_parts()
    ROUND = 1.5 * 2.0 ** 23
    PI_DOWN = 3.1415925
    with ExitStack() as ctx:
        sem = ctx.enter_context(Signals(nc, "rotor"))

        def sb(n, shape, dt=F32):
            return ctx.enter_context(nc.sbuf_tensor(f"rotor_{n}", shape, dt))
        w_v, w_o, freqs = sb("w_v", [P, P]), sb("w_o", [P, P]), sb("freqs", [P, 1])
        norm_and_turn(nc, g, "rotor_ln", [(w_v[:, :], d_in["w_v"]), (w_o[:, :], d_in["w_o"]), (freqs[:, :], d_in["freqs"])])
        time, theta = sb("time", [P, T]), sb("theta", [P, T])
        turns, angle = sb("turns", [P, 2, T]), sb("angle", [P, 2, T])
        table = sb("table", [P, 2, T])
        keep = sb("keep", [P, SPG, T])
        term, total = sb("term", [P, 2, N]), sb("total", [P, 2, N])
        found = sb("found", [P, N])
        timed, angles, tables = sem("timed"), sem("angles"), sem("tables")
        v_ready, found_ready, out_ready, dve_own = sem("v_ready"), sem("found_ready"), sem("out_ready"), sem("dve")
        block = ctx.enter_context(nc.Block())

        @block.gpsimd
        def _(pool):
            pool.iota(time[:, :], pattern=[[1, T]], base=0, channel_multiplier=0,
                      allow_small_or_imprecise_dtypes=True).then_inc(timed, 1)

        @block.scalar
        def _(act):
            act.wait_ge(angles, 1)
            act.activation(table[:, :, :], angle[:, :, :], ACT.Sin).then_inc(tables, 1)

        @block.tensor
        def _(pe):
            pe.wait_ge(g.weights, g.weights_due)
            for c in range(GROUPS):
                pe.matmul(g.bank[c][:, :], w_v[:, :], g.xnT[:, tok(c)], start=True, stop=True).then_inc(v_ready, 1)
            for c in range(GROUPS):
                pe.wait_ge(found_ready, c + 1)
                for i in range(TPG):
                    mm = pe.matmul(g.bank[4 + c][:, i * P:(i + 1) * P], found[:, c * GROUP + i * P:c * GROUP + (i + 1) * P],
                                   w_o[:, :], start=True, stop=True)
                mm.then_inc(out_ready, 1)

        @block.vector
        def _(dve):
            own = Chain(dve, dve_own)
            own.step(dve.memset(keep[:, :, :], 1.0))
            own.add(dve.memset(keep[:, :, 0:1], 0.0))
            dve.wait_ge(timed, 1)
            dve.wait_ge(g.weights, g.weights_due)
            own.step(dve.tensor_scalar(theta[:, :], time[:, :], freqs[:, 0:1], None, ALU.mult))
            for q in range(2):
                own.add(dve.tensor_scalar(turns[:, q, :], theta[:, :], 1 / (2 * np.pi), 0.25 * q, ALU.mult, ALU.add))
            own.settle()
            own.step(dve.tensor_scalar(turns[:, :, :], turns[:, :, :], ROUND, None, ALU.add))
            own.step(dve.tensor_scalar(turns[:, :, :], turns[:, :, :], ROUND, None, ALU.subtract))
            theta2 = theta[:, :].unsqueeze(1).to_broadcast([P, 2, T])
            for k, part in enumerate(TWO_PI):
                own.step(dve.scalar_tensor_tensor(out=angle[:, :, :], in0=turns[:, :, :], scalar=-part,
                                                  in1=theta2 if k == 0 else angle[:, :, :], op0=ALU.mult, op1=ALU.add))
            own.step(dve.tensor_scalar(angle[:, 1, :], angle[:, 1, :], np.pi / 2, None, ALU.add))
            dve.tensor_scalar(angle[:, :, :], angle[:, :, :], PI_DOWN, -PI_DOWN, ALU.min, ALU.max).then_inc(angles, 1)
            dve.wait_ge(tables, 1)
            for c in range(GROUPS):
                dve.wait_ge(v_ready, c + 1)
                v = g.bank[c][:, :].rearrange("p (b t) -> p b t", t=T)

                def per_seq(buf, q):
                    return buf[:, q, tok(c)].rearrange("p (b t) -> p b t", t=T)
                tables2 = [table[:, q, :].unsqueeze(1).to_broadcast([P, SPG, T]) for q in range(2)]
                for q in range(2):
                    own.add(dve.tensor_tensor(per_seq(term, q), v, tables2[q], ALU.mult))
                for q in range(2):
                    own.settle(behind=1)
                    own.add(dve.tensor_tensor_scan(total[:, q, tok(c)], keep[:, :, :].rearrange("p b t -> p (b t)"),
                                                   term[:, q, tok(c)], 0.0, ALU.mult, ALU.add))
                for q in range(2):
                    own.settle(behind=1)
                    own.add(dve.tensor_tensor(per_seq(term, q), per_seq(total, q), tables2[q], ALU.mult))
                own.settle()
                dve.tensor_tensor(found[:, tok(c)], term[:, 0, tok(c)], term[:, 1, tok(c)], ALU.add).then_inc(found_ready, 1)
            for c in range(GROUPS):
                dve.wait_ge(out_ready, c + 1)
                x_c = g.x[:, TPG * c:TPG * (c + 1), :]
                dve.tensor_tensor(x_c, x_c, g.bank[4 + c][:, :].rearrange("p (n d) -> p n d", d=D), ALU.add)


def delta_rule(nc, g, d_in):
    HEADS, TAPS, C, QUAD, LEVELS, DUO = 8, 4, P, 4, 7, 2
    QUADS = TILES // QUAD
    with ExitStack() as ctx:
        sem = ctx.enter_context(Signals(nc, "delta"))

        def sb(n, shape, dt=F32):
            return ctx.enter_context(nc.sbuf_tensor(f"delta_{n}", shape, dt))
        w_qkv, w_z, w_o = sb("w_qkv", [P, HEADS + 1, 3, P]), sb("w_z", [P, HEADS, P]), sb("w_o", [P, HEADS, D])
        taps = sb("taps", [P, HEADS + 1, 3, TAPS])
        w_ab, ab_bias = sb("w_ab", [P, 2 * HEADS]), sb("ab_bias", [P, 2 * HEADS])
        a_log, norm_w = sb("a_log", [P, HEADS]), sb("norm_w", [P, 1])
        norm_and_turn(nc, g, "delta_ln", [
            (w_ab[:, :], d_in["w_ab"]), (ab_bias[:, :], d_in["ab_bias"]), (a_log[:, :], d_in["a_log"]),
            (norm_w[:, :], d_in["norm_w"]), (taps[:, 0:HEADS, :, :], d_in["taps"]), (w_qkv[:, 0:HEADS, :, :], d_in["w_qkv"]),
            (w_z[:, :, :], d_in["w_z"]), (w_o[:, :, :], d_in["w_o"])])
        beta = sb("beta", [P, TILES, HEADS])
        alpha3 = sb("alpha3", [96, N], BF16)

        with ExitStack() as inner:
            sem1 = inner.enter_context(Signals(nc, "delta_ab"))

            def sb1(n, shape, dt=F32):
                return inner.enter_context(nc.sbuf_tensor(f"delta_ab_{n}", shape, dt))
            ab, soft = sb1("ab", [P, TILES, 2 * HEADS]), sb1("soft", [P, TILES, HEADS])
            rate, alpha = sb1("rate", [P, HEADS]), sb1("alpha", [P, TILES, HEADS])
            sig = sb1("sig", [P, TILES, HEADS])
            alpha_t, rest, part = sb1("alpha_t", [32, N]), sb1("rest", [32, N]), sb1("part", [32, N], BF16)
            projected, biased, softened, rated = sem1("projected"), sem1("biased"), sem1("softened"), sem1("rated")
            alpha_ready, turned, split = sem1("alpha_ready"), sem1("turned"), sem1("split")
            act_own, dve_own = sem1("act"), sem1("dve")
            block = inner.enter_context(nc.Block())

            @block.tensor
            def _(pe):
                pe.wait_ge(g.weights, g.weights_due)
                for t in range(TILES):
                    mm = pe.matmul(g.bank[0][:, t * 16:(t + 1) * 16], g.xnT[:, t * P:(t + 1) * P], w_ab[:, :],
                                   start=(t == 0), stop=(t == TILES - 1), skip_group_check=True)
                mm.then_inc(projected, 1)
                pe.wait_ge(alpha_ready, 1)
                for t in range(TILES):
                    mm = pe.transpose(g.bank[1 + t // TPG][0:HEADS, (t % TPG) * P:(t % TPG + 1) * P], alpha[:, t, :],
                                      g.ident[:, :])
                mm.then_inc(turned, 1)

            @block.scalar
            def _(act):
                own = Chain(act, act_own)
                act.preload_act_table_set(LN_EXP)
                act.wait_ge(g.weights, g.weights_due)
                own.add(act.activation(rate[:, :], a_log[:, :], ACT.Exp))
                act.wait_ge(biased, 1)
                own.add(act.activation(sig[:, :, :], ab[:, :, HEADS:], ACT.Exp, scale=-1.0))
                own.step(act.activation(soft[:, :, :], ab[:, :, 0:HEADS], ACT.Abs))
                own.step(act.activation(soft[:, :, :], soft[:, :, :], ACT.Exp, scale=-1.0))
                act.activation(soft[:, :, :], soft[:, :, :], ACT.Ln, bias=g.one[:, 0:1]).then_inc(softened, 1)
                act.wait_ge(rated, 1)
                act.activation(alpha[:, :, :], soft[:, :, :], ACT.Exp, scale=-1.0).then_inc(alpha_ready, 1)
                act.wait_ge(split, 1)
                act.activation(alpha3[32:64, :], part[:, :], ACT.Copy)

            @block.vector
            def _(dve):
                own = Chain(dve, dve_own)
                own.add(dve.memset(alpha_t[:, :], 0.0))
                dve.wait_ge(projected, 1)
                dve.wait_ge(g.weights, g.weights_due)
                dve.tensor_tensor(ab[:, :, :], g.bank[0][:, 0:16 * TILES].rearrange("p (n e) -> p n e", e=16),
                                  ab_bias[:, :].unsqueeze(1).to_broadcast([P, TILES, 16]), ALU.add).then_inc(biased, 1)
                dve.wait_ge(softened, 1)
                own.step(dve.scalar_tensor_tensor(out=soft[:, :, :], in0=ab[:, :, 0:HEADS], scalar=0.0,
                                                  in1=soft[:, :, :], op0=ALU.max, op1=ALU.add))
                dve.tensor_tensor(soft[:, :, :], soft[:, :, :], rate[:, :].unsqueeze(1).to_broadcast([P, TILES, HEADS]),
                                  ALU.mult).then_inc(rated, 1)
                own.step(dve.tensor_scalar(sig[:, :, :], sig[:, :, :], 1.0, None, ALU.add))
                own.add(dve.reciprocal(beta[:, :, :], sig[:, :, :]))
                dve.wait_ge(turned, 1)
                for c in range(GROUPS):
                    own.add(dve.tensor_copy(alpha_t[0:HEADS, tok(c)], g.bank[1 + c][0:HEADS, :]))
                own.settle()
                own.step(dve.tensor_copy(alpha3[0:32, :], alpha_t[:, :]))
                own.step(dve.tensor_tensor(rest[:, :], alpha_t[:, :], alpha3[0:32, :], ALU.subtract))
                own.step(dve.tensor_copy(part[:, :], rest[:, :]))
                dve.tensor_tensor(alpha3[64:96, :], rest[:, :], part[:, :], ALU.subtract).then_inc(split, 1)

        pick = sb("pick", [96, HEADS + 1, P], BF16)
        pick_h = sb("pick_h", [96, P], BF16)
        w_h, wz_h, wo_h = sb("w_h", [P, 3, P]), sb("wz_h", [P, P]), sb("wo_h", [P, D])
        taps_h, beta_h = sb("taps_h", [P, 3, TAPS]), sb("beta_h", [P, TILES])
        joint = sb("joint", [P, LEVELS, C])
        pad = sb("pad", [P, 3, BATCH, T + TAPS - 1])
        qkv = sb("qkv", [P, 3, N])
        alpha_in = sb("alpha_in", [P, TILES, C])
        alpha_first = sb("alpha_first", [P, TILES, C])
        grow = sb("grow", [P, TILES, C])
        kq_g = sb("kq_g", [P, 2, BATCH, C])
        diag, db = sb("diag", [P, DUO, QUAD, C]), sb("db", [P, DUO, QUAD, C])
        lt, at = sb("lt", [P, DUO, QUAD, C]), sb("at", [P, DUO, QUAD, C])
        lt_n = sb("lt_n", [P, DUO, QUAD, C])
        xi, xt, px = sb("xi", [P, DUO, QUAD, C]), sb("xt", [P, DUO, QUAD, C]), sb("px", [P, DUO, QUAD, C])
        v_tok, k_tok = sb("v_tok", [P, DUO, QUAD, C]), sb("k_tok", [P, DUO, 2, C])
        w_sol, s_one = sb("w_sol", [P, DUO, QUAD, C]), sb("s_one", [P, DUO, 2, C])
        sz, o_sq = sb("sz", [P, DUO, QUAD, C]), sb("o_sq", [P, DUO, QUAD, C])
        o_n, o_t = sb("o_n", [P, DUO, QUAD, C]), sb("o_t", [P, DUO, QUAD, C])
        stat = sb("stat", [P, DUO, 3, QUAD])
        eps_o = sb("eps_o", [P, 1])
        staged, staged_in, pe_head, dve_head = sem("staged"), sem("staged_in"), sem("pe_head"), sem("dve_head")
        pads_zero = sem("pads_zero")
        proj_ready, proj_used, conv_ready = sem("proj_ready"), sem("proj_used"), sem("conv_ready")
        a_ready, a_copied, kq_ready = sem("a_ready"), sem("a_copied"), sem("kq_ready")
        scores_ready, lt_ready, at_ready = sem("scores_ready"), sem("lt_ready"), sem("at_ready")
        masked, masked_used = sem("masked"), sem("masked_used")
        p_ready, p_copied, xp_ready, x_ready, xpt_ready, xt_ready = (
            sem("p_ready"), sem("p_copied"), sem("xp_ready"), sem("x_ready"), sem("xpt_ready"), sem("xt_ready"))
        turned, tok_ready = sem("turned"), sem("tok_ready")
        ks_ready, rhs_ready = sem("ks_ready"), sem("rhs_ready")
        w_ready, w_copied, s_ready, s_copied = sem("w_ready"), sem("w_copied"), sem("s_ready"), sem("s_copied")
        z_ready, sz_ready, o_ready = sem("z_ready"), sem("sz_ready"), sem("o_ready")
        sq_ready, var_ready, rstd_ready, on_ready = sem("sq_ready"), sem("var_ready"), sem("rstd_ready"), sem("on_ready")
        ot_ready, ot_copied, out_ready, out_added = sem("ot_ready"), sem("ot_copied"), sem("out_ready"), sem("out_added")
        pool_own, dve_own, act_own = sem("pool"), sem("dve"), sem("act")
        HALVES = QUADS // DUO
        R = HALVES * DUO
        block = ctx.enter_context(nc.Block())

        def projection(i):
            half, rest = divmod(i, 3 * GROUPS // HALVES)
            return rest // 2, half * (GROUPS // HALVES) + rest % 2

        def flat(buf, d):
            return buf[:, d, :, :].rearrange("p a c -> p (a c)")

        @block.gpsimd
        def _(pool):
            own = Chain(pool, pool_own)
            own.step(pool.memset(pick[:, :, :], 0.0))
            for k in range(3):
                own.step(pool.affine_select(out=pick[:, :, :], in_=pick[:, :, :], compare_op=ALU.not_equal, fill=1.0,
                                            base=-32 * k, pattern=[[-1, HEADS + 1], [0, P]], channel_multiplier=1))
            own.step(pool.memset(joint[:, :, :], 0.0))
            for lv in range(LEVELS):
                n = 1 << lv
                view = joint[:, lv, :].rearrange("p (a two r) -> p a two r", two=2, r=n)[:, :, 1, :]
                own.step(pool.memset(view, 1.0))
                own.step(pool.affine_select(out=view, in_=view, compare_op=ALU.is_ge, fill=0.0, base=0,
                                            pattern=[[-2 * n, C // (2 * n)], [0, n]], channel_multiplier=1))
                own.step(pool.affine_select(out=view, in_=view, compare_op=ALU.is_gt, fill=0.0, base=n,
                                            pattern=[[2 * n, C // (2 * n)], [0, n]], channel_multiplier=-1))
            own.step(pool.memset(w_qkv[:, HEADS, :, :], 0.0))
            own.step(pool.memset(taps[:, HEADS, :, :], 0.0))

            def stage_in(w, t, p):
                own.add(pool.tensor_copy(w_h[:, :, :], w.rearrange("p a m c -> p (a m) c")))
                own.add(pool.tensor_copy(pick_h[:, :], p.rearrange("p a c -> p (a c)")))
                own.step(pool.tensor_copy(taps_h[:, :, :], t.rearrange("p a m c -> p (a m) c")))
                pool.sem_inc(staged_in, 1)
            pool.wait_ge(g.weights, g.weights_due)
            stage_in(w_qkv[:, 0:1, :, :], taps[:, 0:1, :, :], pick[:, 0:1, :])
            SETUP = own.count
            PER_HEAD = 6
            with pool.Fori(0, HEADS) as h:
                own = Chain(pool, pool_own, h * PER_HEAD + SETUP)
                for done in (pe_head, dve_head):
                    pool.wait_ge(done, h + 1)
                own.add(pool.tensor_copy(wz_h[:, :], w_z[:, bass.ts(h, 1), :].rearrange("p a c -> p (a c)")))
                own.add(pool.tensor_copy(wo_h[:, :], w_o[:, bass.ts(h, 1), :].rearrange("p a c -> p (a c)")))
                own.step(pool.tensor_copy(beta_h[:, :], beta[:, :, bass.ts(h, 1)].rearrange("p a c -> p (a c)")))
                pool.sem_inc(staged, 1)
                for half in range(HALVES):
                    for lv in range(LEVELS):
                        for d in range(DUO):
                            n = DUO * half + d
                            if lv == 0:
                                pool.wait_ge(lt_ready, h * R + (n + 1))
                            pool.wait_ge(masked_used, h * (R * LEVELS) + (half * DUO * LEVELS + lv * DUO + d + 1))
                            pool.tensor_tensor(lt_n[:, d, :, :], lt[:, d, :, :],
                                               joint[:, lv, :].unsqueeze(1).to_broadcast([P, QUAD, C]),
                                               ALU.mult).then_inc(masked, 1)
                pool.wait_ge(a_ready, h * GROUPS + GROUPS)
                pool.wait_ge(conv_ready, h * HALVES + HALVES)
                stage_in(w_qkv[:, 1:, :, :][:, bass.ts(h, 1), :, :], taps[:, 1:, :, :][:, bass.ts(h, 1), :, :],
                         pick[:, 1:, :][:, bass.ts(h, 1), :])

        @block.tensor
        def _(pe):
            def chunks(bank, lhs, rhs, signal, which=range(4), start=None, stop=True):
                for i in which:
                    mm = pe.matmul(bank[:, i * C:(i + 1) * C], lhs(i), rhs(i), start=True if start is None else start(i),
                                   stop=stop)
                mm.then_inc(signal, 1)

            with pe.Fori(0, HEADS) as h:
                pe.wait_ge(staged_in, h + 1)
                for i in range(4 * GROUPS):
                    if i == 6:
                        pe.wait_ge(dve_head, h + 1)
                    if i >= 8:
                        pe.wait_ge(proj_used, h * (3 * GROUPS) + (i - 7))
                    bank = g.bank[(i + 2) % 8]
                    if i < 3 * GROUPS:
                        m, c = projection(i)
                        pe.matmul(bank[:, :], w_h[:, m, :], g.xnT[:, tok(c)], start=True, stop=True).then_inc(proj_ready, 1)
                    else:
                        pe.matmul(bank[:, :], pick_h[:, :], alpha3[:, tok(i - 3 * GROUPS)], start=True, stop=True).then_inc(a_ready, 1)
                pe.wait_ge(proj_used, h * (3 * GROUPS) + 3 * GROUPS)
                pe.wait_ge(a_copied, h * GROUPS + GROUPS)
                for half in range(HALVES):
                    pe.wait_ge(conv_ready, h * HALVES + (half + 1))
                    for d in range(DUO):
                        at0 = (DUO * half + d) * GROUP

                        def seg(m, i, at0=at0):
                            return qkv[:, m, at0 + i * C:at0 + (i + 1) * C]
                        if half:
                            pe.wait_ge(out_added, h * R + DUO * (half - 1) + d + 1)
                        chunks(g.bank[d], lambda i: seg(1, i), lambda i: seg(1, i), scores_ready)
                        chunks(g.bank[2 + d], lambda i: seg(1, i), lambda i: seg(0, i), scores_ready)
                        for i in range(4):
                            mm = pe.transpose(g.bank[4 + d][:, i * C:(i + 1) * C], seg(2, i), g.ident[:, :])
                        mm.then_inc(turned, 1)
                        for i in (0, 2):
                            mm = pe.transpose(g.bank[6 + d][:, (i // 2) * C:(i // 2 + 1) * C], seg(1, i), g.ident[:, :])
                        mm.then_inc(turned, 1)
                    for lv in range(LEVELS):
                        for d in range(DUO):
                            n = R * LEVELS
                            it = half * DUO * LEVELS + lv * DUO + d
                            pe.wait_ge(masked, h * n + (it + 1))
                            if lv == 0:
                                pe.wait_ge(at_ready, h * R + (DUO * half + d + 1))
                                for i in range(4):
                                    mm = pe.transpose(g.bank[d][:, i * C:(i + 1) * C], lt_n[:, d, i, :], g.ident[:, :])
                                mm.then_inc(p_ready, 1)
                            else:
                                pe.wait_ge(x_ready, h * (R * (LEVELS - 1)) + (half * DUO * (LEVELS - 1) + (lv - 1) * DUO + d + 1))
                                chunks(g.bank[d], lambda i, d=d: lt_n[:, d, i, :], lambda i, d=d: xi[:, d, i, :], p_ready)
                        if lv == 0:
                            continue
                        if lv in (2, 3):
                            z0 = TPG * (DUO * half + lv - 2)
                            if lv == 2:
                                pe.wait_ge(staged, h + 1)
                            chunks(g.bank[4 + lv], lambda i, z0=z0: g.xnT[:, (z0 + i) * P:(z0 + i + 1) * P], lambda i: wz_h[:, :], z_ready)
                        for d in range(DUO):
                            it = half * DUO * LEVELS + lv * DUO + d
                            pe.wait_ge(p_copied, h * (R * LEVELS) + (it + 1))
                            pe.wait_ge(xt_ready, h * (R * LEVELS) + (it - DUO + 1))
                            if lv < LEVELS - 1:
                                chunks(g.bank[2 + d], lambda i, d=d: xt[:, d, i, :], lambda i, d=d: px[:, d, i, :], xp_ready)
                            if lv == 1:
                                pe.wait_ge(tok_ready, h * (2 * R) + (2 * (DUO * half + d) + 2))
                            chunks(g.bank[4 + d], lambda i, d=d: px[:, d, i, :], lambda i, d=d: xt[:, d, i, :], xpt_ready)
                    for d in range(DUO):
                        it = half * DUO * LEVELS + (LEVELS - 1) * DUO + d
                        pe.wait_ge(xt_ready, h * (R * LEVELS) + (it + 1))
                        chunks(g.bank[d], lambda i, d=d: xt[:, d, i, :], lambda i, d=d: v_tok[:, d, i, :], w_ready, (0, 2))
                    for d in range(DUO):
                        n = DUO * half + d
                        pe.wait_ge(w_copied, h * (2 * R) + (2 * DUO * half + d + 1))
                        chunks(g.bank[2 + d], lambda i, d=d: k_tok[:, d, i, :], lambda i, d=d: w_sol[:, d, 2 * i, :], s_ready, (0, 1))
                    for d in range(DUO):
                        n = DUO * half + d
                        pe.wait_ge(s_copied, h * R + (n + 1))
                        pe.wait_ge(kq_ready, h * HALVES + (half + 1))
                        chunks(g.bank[4 + d], lambda i, n=n: kq_g[:, 1, 2 * n + i, :], lambda i, d=d: s_one[:, d, i, :],
                               ks_ready, (0, 1))
                    for d in range(DUO):
                        n = DUO * half + d
                        pe.wait_ge(rhs_ready, h * R + (n + 1))
                        chunks(g.bank[d], lambda i, d=d: xt[:, d, i, :], lambda i, d=d: v_tok[:, d, i, :], w_ready, (1, 3))
                    for d in range(DUO):
                        n = DUO * half + d
                        pe.wait_ge(w_copied, h * (2 * R) + (2 * DUO * half + DUO + d + 1))
                        for i in range(4):
                            mm = pe.matmul(g.bank[2 + d][:, i * C:(i + 1) * C], at[:, d, i, :], w_sol[:, d, i, :],
                                           start=True, stop=(i % 2 == 0))
                            if i % 2:
                                mm = pe.matmul(g.bank[2 + d][:, i * C:(i + 1) * C], kq_g[:, 0, 2 * n + i // 2, :],
                                               s_one[:, d, i // 2, :], start=False, stop=True)
                        mm.then_inc(o_ready, 1)
                    for d in range(DUO):
                        n = DUO * half + d
                        pe.wait_ge(on_ready, h * R + (n + 1))
                        for i in range(4):
                            mm = pe.transpose(g.bank[4 + d][:, i * C:(i + 1) * C], o_n[:, d, i, :], g.ident[:, :])
                        mm.then_inc(ot_ready, 1)
                    for d in range(DUO):
                        n = DUO * half + d
                        pe.wait_ge(ot_copied, h * R + (n + 1))
                        chunks(g.bank[d], lambda i, d=d: o_t[:, d, i, :], lambda i: wo_h[:, :], out_ready)
                pe.wait_ge(out_ready, h * R + R)
                pe.sem_inc(pe_head, 1)

        @block.scalar
        def _(act):
            act.wait_ge(pads_zero, 1)
            with act.Fori(0, HEADS) as h:
                for i in range(3 * GROUPS):
                    m, c = projection(i)
                    act.wait_ge(proj_ready, h * (3 * GROUPS) + (i + 1))
                    act.activation(pad[:, m, SPG * c:SPG * (c + 1), TAPS - 1:],
                                   g.bank[(i + 2) % 8][:, :].rearrange("p (b t) -> p b t", t=T), ACT.Copy).then_inc(proj_used, 1)
                for c in range(GROUPS):
                    act.wait_ge(a_ready, h * GROUPS + (c + 1))
                    a = g.bank[(3 * GROUPS + c + 2) % 8][:, :].rearrange("p (n c) -> p n c", c=C)
                    t = slice(TPG * c, TPG * (c + 1))
                    act.activation(alpha_in[:, t, 1:], a[:, :, 1:], ACT.Copy)
                    act.activation(alpha_first[:, t, 0:1], a[:, :, 0:1], ACT.Copy).then_inc(a_copied, 1)
                for half in range(HALVES):
                    for d in range(DUO):
                        n = DUO * half + d
                        act.wait_ge(turned, h * (2 * R) + (2 * n + 2))
                        act.activation(flat(v_tok, d), g.bank[4 + d][:, :], ACT.Copy).then_inc(tok_ready, 1)
                        act.wait_ge(lt_ready, h * R + (n + 1))
                        for i in range(2):
                            ins = act.activation(k_tok[:, d, i, :], g.bank[6 + d][:, i * C:(i + 1) * C], ACT.Copy,
                                                 scale=db[:, d, 2 * i, C - 1:C])
                        ins.then_inc(tok_ready, 1)
                    for lv in range(LEVELS):
                        for d in range(DUO):
                            it = half * DUO * LEVELS + lv * DUO + d
                            act.wait_ge(p_ready, h * (R * LEVELS) + (it + 1))
                            act.activation(flat(px, d), g.bank[d][:, :], ACT.Copy).then_inc(p_copied, 1)
                        if lv == 3:
                            for d in range(DUO):
                                act.wait_ge(z_ready, h * R + (DUO * half + d + 1))
                                act.activation(flat(sz, d), g.bank[6 + d][:, :], ACT.Silu).then_inc(sz_ready, 1)
                    for d in range(DUO):
                        act.wait_ge(w_ready, h * (2 * R) + (2 * DUO * half + d + 1))
                        act.activation(w_sol[:, d, 0:4:2, :], g.bank[d][:, :].rearrange("p (a c) -> p a c", c=C)[:, 0:4:2, :],
                                       ACT.Copy).then_inc(w_copied, 1)
                    for d in range(DUO):
                        n = DUO * half + d
                        act.wait_ge(s_ready, h * R + (n + 1))
                        act.activation(flat(s_one, d), g.bank[2 + d][:, 0:2 * C], ACT.Copy).then_inc(s_copied, 1)
                    act.preload_act_table_set(LN_EXP)
                    for d in range(DUO):
                        act.wait_ge(w_ready, h * (2 * R) + (2 * DUO * half + DUO + d + 1))
                        act.activation(w_sol[:, d, 1:4:2, :], g.bank[d][:, :].rearrange("p (a c) -> p a c", c=C)[:, 1:4:2, :],
                                       ACT.Copy).then_inc(w_copied, 1)
                    for d in range(DUO):
                        act.wait_ge(o_ready, h * R + (DUO * half + d + 1))
                        act.activation(flat(o_sq, d), g.bank[2 + d][:, :], ACT.Square).then_inc(sq_ready, 1)
                    for d in range(DUO):
                        n = DUO * half + d
                        act.wait_ge(var_ready, h * R + (n + 1))
                        act.activation(stat[:, d, 1, :], stat[:, d, 0, :], ACT.Ln, bias=eps_o[:, 0:1], scale=1.0 / P).then_inc(act_own, 1)
                        act.wait_ge(act_own, h * R + (n + 1))
                        act.activation(stat[:, d, 2, :], stat[:, d, 1, :], ACT.Exp, scale=-0.5).then_inc(rstd_ready, 1)
                    for d in range(DUO):
                        act.wait_ge(ot_ready, h * R + (DUO * half + d + 1))
                        act.activation(flat(o_t, d), g.bank[4 + d][:, :], ACT.Copy, scale=norm_w[:, 0:1]).then_inc(ot_copied, 1)

        @block.vector
        def _(dve):
            own = Chain(dve, dve_own)
            own.add(dve.memset(pad[:, :, :, 0:TAPS - 1], 0.0))
            own.add(dve.memset(alpha_in[:, :, 0:1], 0.0))
            own.add(dve.memset(alpha_first[:, :, :], 0.0))
            own.add(dve.memset(eps_o[:, :], 1e-6))
            own.settle()
            for free in (pads_zero, dve_head, pe_head):
                dve.sem_inc(free, 1)
            dve.sem_inc(masked_used, DUO)
            SETUP, PER_HEAD = own.count, 42
            with dve.Fori(0, HEADS) as h:
                own = Chain(dve, dve_own, h * PER_HEAD + SETUP)
                dve.wait_ge(staged_in, h + 1)

                def convolve(half, m, k):
                    b = slice(BATCH // HALVES * half, BATCH // HALVES * (half + 1))
                    conv = qkv[:, m, :].rearrange("p (b t) -> p b t", t=T)[:, b, :]
                    if k == 0:
                        dve.wait_ge(proj_used, h * (3 * GROUPS) + (3 * GROUPS // HALVES * half + 2 * m + 2))
                        own.step(dve.tensor_scalar(conv, pad[:, m, b, 0:T], taps_h[:, m, 0:1], None, ALU.mult))
                    else:
                        own.step(dve.scalar_tensor_tensor(out=conv, in0=pad[:, m, b, k:k + T], scalar=taps_h[:, m, k:k + 1],
                                                          in1=conv, op0=ALU.mult, op1=ALU.add))
                    if (m, k) == (2, TAPS - 1):
                        dve.sem_inc(conv_ready, 1)

                def grow_and_scale(half):
                    t = slice(TILES // HALVES * half, TILES // HALVES * (half + 1))
                    b = slice(BATCH // HALVES * half, BATCH // HALVES * (half + 1))
                    own.step(dve.tensor_tensor_scan(grow[:, t, :].rearrange("p n c -> p (n c)"),
                                                    alpha_in[:, t, :].rearrange("p n c -> p (n c)"),
                                                    alpha_first[:, t, :].rearrange("p n c -> p (n c)"), 0.0, ALU.mult, ALU.add))
                    for m in range(2):
                        own.add(dve.tensor_tensor(kq_g[:, m, b, :], qkv[:, m, :].rearrange("p (b n c) -> p b n c", n=2, c=C)[:, b, 1, :],
                                                  grow[:, t, :][:, 1::2, :], ALU.mult))
                    own.settle()
                    dve.sem_inc(kq_ready, 1)
                steps = [(m, k) for m in range(3) for k in range(TAPS)]
                for m, k in steps:
                    convolve(0, m, k)
                dve.wait_ge(a_copied, h * GROUPS + GROUPS)
                dve.wait_ge(staged, h + 1)
                for half in range(HALVES):
                    for d in range(DUO):
                        n = DUO * half + d
                        t = slice(QUAD * n, QUAD * (n + 1))
                        own.step(dve.tensor_tensor(diag[:, d, :, :], g.ident[:, :].unsqueeze(1).to_broadcast([P, QUAD, C]),
                                                   spread(beta_h[:, t], C), ALU.mult))
                        own.step(dve.tensor_tensor_scan(flat(db, d), alpha_in[:, t, :].rearrange("p n c -> p (n c)"),
                                                        flat(diag, d), 0.0, ALU.mult, ALU.add))
                        dve.wait_ge(scores_ready, h * (2 * R) + (2 * n + 2))
                        dve.tensor_tensor(flat(lt, d), flat(db, d), g.bank[d][:, :], ALU.mult).then_inc(lt_ready, 1)
                        dve.tensor_tensor(flat(at, d), flat(db, d), g.bank[2 + d][:, :], ALU.mult).then_inc(at_ready, 1)
                    for lv in range(LEVELS):
                        for d in range(DUO):
                            it = half * DUO * LEVELS + lv * DUO + d
                            xit = half * DUO * (LEVELS - 1) + lv * DUO + d
                            if lv == 0:
                                ident4 = g.ident[:, :].unsqueeze(1).to_broadcast([P, QUAD, C])
                                dve.wait_ge(p_copied, h * (R * LEVELS) + (it + 1))
                                dve.tensor_tensor(xi[:, d, :, :], ident4, px[:, d, :, :], ALU.subtract).then_inc(x_ready, 1)
                                dve.tensor_tensor(xt[:, d, :, :], ident4, lt_n[:, d, :, :], ALU.subtract).then_inc(xt_ready, 1)
                            else:
                                if lv < LEVELS - 1:
                                    dve.wait_ge(xp_ready, h * (R * (LEVELS - 2)) + (half * DUO * (LEVELS - 2) + (lv - 1) * DUO + d + 1))
                                    dve.wait_ge(x_ready, h * (R * (LEVELS - 1)) + (xit - DUO + 1))
                                    dve.tensor_tensor(flat(xi, d), flat(xi, d), g.bank[2 + d][:, :], ALU.subtract).then_inc(x_ready, 1)
                                dve.wait_ge(xpt_ready, h * (R * (LEVELS - 1)) + (half * DUO * (LEVELS - 1) + (lv - 1) * DUO + d + 1))
                                dve.wait_ge(xt_ready, h * (R * LEVELS) + (it - DUO + 1))
                                dve.tensor_tensor(flat(xt, d), flat(xt, d), g.bank[4 + d][:, :], ALU.subtract).then_inc(xt_ready, 1)
                            dve.wait_ge(xt_ready, h * (R * LEVELS) + (it + 1))
                            dve.sem_inc(masked_used, 1)
                        if lv == 0:
                            grow_and_scale(half)
                        elif half + 1 < HALVES:
                            for m, k in steps[2 * (lv - 1):2 * lv]:
                                convolve(half + 1, m, k)
                    for d in range(DUO):
                        n = DUO * half + d
                        dve.wait_ge(ks_ready, h * R + (n + 1))
                        dve.tensor_tensor(v_tok[:, d, 1:4:2, :], v_tok[:, d, 1:4:2, :],
                                          g.bank[4 + d][:, 0:2 * C].rearrange("p (a c) -> p a c", c=C), ALU.subtract).then_inc(rhs_ready, 1)
                    for d in range(DUO):
                        n = DUO * half + d
                        dve.wait_ge(sq_ready, h * R + (n + 1))
                        dve.tensor_reduce(stat[:, d, 0, :], o_sq[:, d, :, :], AX.X, ALU.add).then_inc(var_ready, 1)
                    for d in range(DUO):
                        n = DUO * half + d
                        dve.wait_ge(rstd_ready, h * R + (n + 1))
                        own.step(dve.tensor_tensor(o_n[:, d, :, :], g.bank[2 + d][:, :].rearrange("p (a c) -> p a c", c=C),
                                                   spread(stat[:, d, 2, :], C), ALU.mult))
                        dve.wait_ge(sz_ready, h * R + (n + 1))
                        dve.tensor_tensor(flat(o_n, d), flat(o_n, d), flat(sz, d), ALU.mult).then_inc(on_ready, 1)
                    for d in range(DUO):
                        n = DUO * half + d
                        dve.wait_ge(out_ready, h * R + (n + 1))
                        x_q = g.x[:, QUAD * n:QUAD * (n + 1), :]
                        dve.tensor_tensor(x_q, x_q, g.bank[d][:, :].rearrange("p (n d) -> p n d", d=D), ALU.add).then_inc(out_added, 1)
                dve.wait_ge(out_added, h * R + R)
                dve.sem_inc(dve_head, 1)
                assert own.count == PER_HEAD, own.count


def rotary_tables():
    half = np.arange(0, 64, 2, dtype=np.float32)
    inv_freq = np.float32(1.0) / np.power(np.float32(10000.0), half / np.float32(64))
    t = np.arange(T, dtype=np.float32)
    freqs = t[:, None] * inv_freq[None, :]
    freqs = np.concatenate([freqs, freqs], -1).T
    base = (half + np.float32(0.4 * 64)) / np.float32(1.4 * 64)
    scale = base[None, :] ** ((t - T // 2) / np.float32(16))[:, None]
    scale = np.concatenate([scale, scale], -1).T
    sign = np.repeat(np.array([-1, 1], np.float32), 32)[:, None]
    cos, sin = np.cos(freqs), np.sin(freqs) * sign
    one = np.stack([8 * cos * scale, cos / scale, 8 * sin * scale, sin / scale], 1).astype(np.float32)
    return np.concatenate([one, one])


def local_stack(nc, g, d_in):
    LAYERS, PAIRS, W, E = 6, 8, 32, 64
    WINDOWS = T // W
    UNITS, CHUNKS = 341, 3
    LAST = UNITS - 2 * P
    SLOTS = PAIRS * GROUPS
    H = 2
    LN_SCALE = 2.0 ** 20
    with ExitStack() as ctx:
        sem = ctx.enter_context(Signals(nc, "local"))

        def sb(n, shape, dt=F32):
            return ctx.enter_context(nc.sbuf_tensor(f"local_{n}", shape, dt))
        base = sb("base", [P, 4, T])
        norm_and_turn(nc, g, "local_ln", [(base[:, :, :], d_in["base"])])
        w_layer = sb("w_layer", [P, PAIRS, 5 * P])
        w_pair = sb("w_pair", [P, 5, P])
        w_o, w_up, w_down = sb("w_o", [P, PAIRS, D]), sb("w_up", [P, 2 * UNITS]), sb("w_down", [P, CHUNKS, D])
        scales = sb("scales", [P, 4])
        vecs = sb("vecs", [P, 8])
        table = sb("table", [P, 4, T])
        xs = sb("xs", [P, BATCH, W + T])
        q_rot = sb("q_rot", [P, 2, 2 * GROUP])
        k_rot = sb("k_rot", [P, 2, SPG, W + T])
        v_at, v_moved = sb("v_at", [P, TILES, P]), sb("v_moved", [P, TILES, P])
        attn = sb("attn", [P, PAIRS, N])
        sq, lg, inv = sb("sq", [P, 2, GROUP]), sb("lg", [P, 2, GROUP]), sb("inv", [P, 2, GROUP])
        mask = sb("mask", [P, 4, 2 * W])
        z = sb("z", [P, 2, GROUP])
        term = sb("term", [P, 4, SPG, T])
        most, total = sb("most", [P, 2, 2 * TPG]), sb("total", [P, 2, 2, 2 * TPG])
        pt = sb("pt", [P, TPG, 2, 2, H * W])
        same_head, mean_of = sb("same_head", [P, P]), sb("mean_of", [P, P])
        guard, unscale = sb("guard", [P, 1]), sb("unscale", [P, 1])
        gelu, hid = sq, sb("hid", [P, 2, CHUNKS, GROUP])
        xc = attn[:, 1, :]
        rstd = v_at
        made, scales_loaded, vecs_loaded, pair_loaded, ffn_loaded = sem("made"), sem("scales_loaded"), sem("vecs_loaded"), sem("pair_loaded"), sem("ffn_loaded")
        vecs_free, pair_free, ffn_free = sem("vecs_free"), sem("pair_free"), sem("ffn_free")
        wo_loaded, staged, tabled = sem("wo_loaded"), sem("staged"), sem("tabled")
        assert SLOTS == 2 * 16
        xr_ready, turned, xs_ready = sem("xr_ready"), sem("turned"), sem("xs_ready")
        proj_ready, rotated, sq_ready, summed = sem("proj_ready"), sem("rotated"), sem("sq_ready"), sem("summed")
        v_ready, v_used, v_shifted = sem("v_ready"), sem("v_used"), sem("v_shifted")
        norm_ready, norm_used, inv_ready = sem("norm_ready"), sem("norm_used"), sem("inv_ready")
        qk_ready, s_ready, z_ready, e_ready = sem("qk_ready"), sem("s_ready"), sem("z_ready"), sem("e_ready")
        total_ready, p_ready = sem("total_ready"), sem("p_ready")
        pt_ready, pt_copied, o_ready, o_copied, wo_ready = (
            sem("pt_ready"), sem("pt_copied"), sem("o_ready"), sem("o_copied"), sem("wo_ready"))
        mean_ready, xc_ready, xsq_ready, var_ready, rstd_ready, h_ready = (
            sem("mean_ready"), sem("xc_ready"), sem("xsq_ready"), sem("var_ready"), sem("rstd_ready"), sem("h_ready"))
        up_ready, gelu_ready, hid_ready, down_ready = sem("up_ready"), sem("gelu_ready"), sem("hid_ready"), sem("down_ready")
        dve_own, act_own, pool_own, act_passed, sp_passed = sem("dve"), sem("act"), sem("pool"), sem("act_passed"), sem("sp_passed")
        pe_passed = sem("pe_passed")
        block = ctx.enter_context(nc.Block())
        FFN = GROUPS * CHUNKS
        normed = sem("normed")

        WO, ADD, TURN, MEAN, VAR, UP, DOWN, NEXT_TURN, STEPS_FFN = -1, -1, 0, 1, 2, 3, 4, 5, 9

        def at(step, stage):
            return step - stage if 0 <= step - stage < GROUPS else None

        def seqs(c):
            return slice(SPG * c, SPG * (c + 1))

        def slots(eng, l, project, slot, finish):
            first = l * SLOTS
            project(first, 0)
            slot(first, 0, True, None)
            with eng.Fori(0, PAIRS - 1) as hp:
                for j in range(1, GROUPS + 1):
                    slot(first + hp * GROUPS, j, True, hp)
            for j in range(1, GROUPS):
                slot(first + (PAIRS - 1) * GROUPS, j, j < GROUPS - 1, PAIRS - 1)
            finish(first + (PAIRS - 1) * GROUPS, GROUPS - 1)

        @block.sync
        def _(sp):
            sp.wait_ge(made, 1)

            def shift_values(s, c):
                sp.wait_ge(v_used, s + 1)
                t = slice(TPG * c, TPG * (c + 1))
                sp.dma_start(v_moved[W:P, t, :], v_at[0:P - W, t, :]).then_inc(v_shifted, 16)
                sp.dma_start(v_moved[0:W, TPG * c + 1:TPG * (c + 1):2, :], v_at[P - W:P, TPG * c:TPG * (c + 1):2, :]
                             ).then_inc(v_shifted, 16)
                wait_apart(sp, v_shifted, s * 32 + 32, sp_passed)
            with sp.Fori(0, LAYERS) as l:
                wait_apart(sp, tabled, l + 1, sp_passed)
                sp.dma_start(scales[:, :], d_in["scales"][bass.ts(l, 1), :, :].rearrange("a p n -> (a p) n")).then_inc(scales_loaded, 16)
                wait_apart(sp, pair_free, l + 1, sp_passed)
                sp.dma_start(w_layer[:, :, :], d_in["w_layer"][bass.ts(l, 1), :, :, :].rearrange("a p n m -> (a p) n m")
                             ).then_inc(pair_loaded, 16)
                wait_apart(sp, vecs_free, l + 1, sp_passed)
                sp.dma_start(vecs[:, :], d_in["vecs"][bass.ts(l, 1), :, :].rearrange("a p n -> (a p) n")).then_inc(vecs_loaded, 16)
                wait_apart(sp, ffn_free, l + 1, sp_passed)
                for part in (slice(0, PAIRS // 2), slice(PAIRS // 2, PAIRS)):
                    sp.dma_start(w_o[:, part, :], d_in["w_o"][bass.ts(l, 1), :, part, :].rearrange("a p n m -> (a p) n m")
                                 ).then_inc(wo_loaded, 16)
                sp.dma_start(w_up[:, :], d_in["w_up"][bass.ts(l, 1), :, :].rearrange("a p n -> (a p) n")).then_inc(ffn_loaded, 16)
                sp.dma_start(w_down[:, :, :], d_in["w_down"][bass.ts(l, 1), :, :, :].rearrange("a p n m -> (a p) n m")
                             ).then_inc(ffn_loaded, 16)
                with sp.Fori(0, PAIRS) as hp:
                    for c in range(GROUPS):
                        shift_values(l * SLOTS + hp * GROUPS + c, c)

        @block.gpsimd
        def _(pool):
            own = Chain(pool, pool_own)
            own.step(pool.memset(xs[:, :, 0:W + 1], 0.0))
            own.step(pool.memset(k_rot[:, :, :, 0:W], 0.0))
            own.step(pool.memset(q_rot[:, :, :], 0.0))
            own.step(pool.memset(pt[:, :, :, :, :], 0.0))
            own.step(pool.memset(v_moved[0:W, :, :], 0.0))
            own.step(pool.memset(same_head[:, :], 0.0))
            own.step(pool.memset(mean_of[:, :], 1.0 / D))
            own.step(pool.memset(guard[:, :], 1e-24 * LN_SCALE))
            own.step(pool.memset(unscale[:, :], 0.5 * float(np.log(LN_SCALE))))
            own.step(pool.memset(hid[64:P, :, CHUNKS - 1, :], 1.0))
            own.step(pool.memset(mask[:, :, :], 0.0))
            own.settle()
            for hh in range(2):
                own.step(pool.memset(same_head[E * hh:E * hh + E, E * hh:E * hh + E], 1.0))
            for quadrant in range(4):
                own.settle()
                m = mask[W * quadrant:W * (quadrant + 1), :, :]
                own.step(pool.affine_select(out=m, in_=m, compare_op=ALU.is_ge, fill=-1e30, base=0,
                                            pattern=[[0, 4], [1, 2 * W]], channel_multiplier=-1))
                own.step(pool.affine_select(out=m, in_=m, compare_op=ALU.is_ge, fill=-1e30, base=W,
                                            pattern=[[0, 4], [-1, 2 * W]], channel_multiplier=1))
            own.step(pool.memset(mask[0:H * W, 0, 0:W], -1e30))
            pool.sem_inc(made, 1)

            def stage(weights):
                pool.tensor_copy(w_pair[:, :, :].rearrange("p a c -> p (a c)"), weights.rearrange("p a c -> p (a c)")).then_inc(staged, GROUPS)

            def add_rotated(s):
                for m in range(2):
                    pool.wait_ge(rotated, s * 4 + (4 + 2 + 2 * m))
                    pool.tensor_tensor(term[:, m, :, :], term[:, m, :, :], term[:, 2 + m, :, :], ALU.add).then_inc(summed, 1)

            def slot(b, j, project_next, hp):
                s = b + j
                if j == GROUPS - 1 and project_next:
                    pool.wait_ge(v_ready, s + 1)
                    stage(w_layer[:, 1:, :][:, bass.ts(hp, 1), :])
                pool.wait_ge(total_ready, s + 1)
                rows = z[:, j % 2, :].rearrange("p (x k) -> p x k", k=2 * W)
                pool.tensor_tensor(rows, rows, spread(total[:, j % 2, 1, :], 2 * W), ALU.mult).then_inc(p_ready, 1)
                if project_next:
                    add_rotated(s + 1)

            def finish(b, j):
                pool.wait_ge(staged, b + GROUPS)
                pool.sem_inc(pair_free, 1)
            with pool.Fori(0, LAYERS) as l:
                pool.wait_ge(pair_loaded, l * 16 + 16)
                pool.wait_ge(xs_ready, l * 8 + 1)
                stage(w_layer[:, 0:1, :])
                slots(pool, l, lambda b, j: add_rotated(b), slot, finish)

        @block.tensor
        def _(pe):
            pe.wait_ge(made, 1)

            def turn(n, c):
                pe.wait_ge(xr_ready, n + 1)
                if not (isinstance(n, int) and n == 0):
                    pe.wait_ge(xs_ready, n)
                for i in range(TPG):
                    mm = pe.transpose(g.bank[6][:, i * P:(i + 1) * P], g.xn[:, TPG * c + i, :], g.ident[:, :])
                mm.then_inc(turned, 1)

            def project(b, j):
                s, c = b + j, j % GROUPS
                if c == 0:
                    pe.wait_ge(staged, s + GROUPS)
                pe.wait_ge(norm_used, s * 2 + 2)
                wait_apart(pe, rotated, s * 4 + 4, pe_passed)
                for m in range(4):
                    pe.matmul(g.bank[m][:, :].rearrange("p (b t) -> p b t", t=T), w_pair[:, m, :], xs[:, seqs(c), W:],
                              start=True, stop=True).then_inc(proj_ready, 1)
                for m in range(2):
                    pe.wait_ge(sq_ready, s * 2 + (m + 1))
                    if m == 0:
                        pe.wait_ge(rotated, s * 4 + 5)
                    else:
                        pe.wait_ge(pt_copied, s + (2 if j == 0 else 1))
                    pe.matmul(g.bank[4 * m][:, :], same_head[:, :], sq[:, m, :], start=True, stop=True).then_inc(norm_ready, 1)
                if j:
                    pe.wait_ge(z_ready, s)
                for i in range(TPG):
                    b_, n = divmod(i, 2)
                    mm = pe.matmul(g.bank[5][:, i * P:(i + 1) * P], xs[:, SPG * c + b_, W + n * P:W + (n + 1) * P],
                                   w_pair[:, 4, :], start=True, stop=True)
                mm.then_inc(v_ready, 1)

            def score(s, j):
                pe.wait_ge(qk_ready, s * 3 + 3)
                wait_apart(pe, v_used, s + 1, pe_passed)
                for b in range(SPG):
                    for w in range(WINDOWS):
                        n, half, r = w // 4, w // 2 % 2, w % 2
                        column = ((b * 2 + n) * 2 + half) * 2 * W
                        query = (b * WINDOWS + w) * H * W
                        mm = pe.matmul(g.bank[5][H * W * r:H * W * (r + 1), column:column + 2 * W],
                                       q_rot[:, j % 2, query:query + H * W], k_rot[:, j % 2, b, w * W:(w + 2) * W],
                                       start=True, stop=True)
                mm.then_inc(s_ready, 1)

            def turn_probs(s, j, project_next):
                pe.wait_ge(p_ready, s + 1)
                if project_next:
                    pe.wait_ge(norm_used, s * 2 + 6)
                for i in range(TPG):
                    mm = pe.transpose(g.bank[4][:, i * P:(i + 1) * P], z[:, j % 2, i * P:(i + 1) * P], g.ident[:, :])
                mm.then_inc(pt_ready, 1)

            def weigh_values(s, j):
                pe.wait_ge(pt_copied, s + 3)
                pe.wait_ge(v_shifted, s * 32 + 32)
                wait_apart(pe, o_copied, s + 1, pe_passed)
                for i in range(TPG):
                    for r in range(2):
                        mm = pe.matmul(g.bank[6 + i // 2][:, (2 * (i % 2) + r) * P:(2 * (i % 2) + r + 1) * P],
                                       (v_at if r else v_moved)[:, TPG * (j % GROUPS) + i, :],
                                       pt[:, i, r, :, :].rearrange("p s q -> p (s q)"), start=True, stop=True)
                mm.then_inc(o_ready, 1)

            def slot(b, j, project_next, hp):
                score(b + j, j)
                if project_next:
                    project(b, j + 1)
                else:
                    project_out(b + j, 0)
                if hp is not None:
                    weigh_values(b + (j - 1), j - 1)
                turn_probs(b + j, j, project_next)

            def project_out(last, c):
                if c == 0:
                    pe.wait_ge(wo_loaded, last + 1)
                pe.wait_ge(o_copied, last + (c - 1))
                for i in range(TPG):
                    for p in range(PAIRS):
                        t0 = c * GROUP + i * P
                        mm = pe.matmul(g.bank[c][:, i * P:(i + 1) * P], attn[:, p, t0:t0 + P], w_o[:, p, :],
                                       start=(p == 0), stop=(p == PAIRS - 1))
                mm.then_inc(wo_ready, 1)

            def mean(l, c):
                pe.wait_ge(xs_ready, l * 8 + (5 + c))
                if c:
                    pe.wait_ge(rstd_ready, l * GROUPS + c)
                pe.matmul(g.bank[7][:, :].rearrange("p (b t) -> p b t", t=T), mean_of[:, :], xs[:, seqs(c), W:],
                          start=True, stop=True).then_inc(mean_ready, 1)

            def variance(l, c):
                pe.wait_ge(xsq_ready, l * GROUPS + (c + 1))
                pe.matmul(g.bank[7][:, :], mean_of[:, :], attn[:, 0, tok(c)], start=True, stop=True).then_inc(var_ready, 1)

            def up(l, c):
                pe.wait_ge(ffn_loaded, l * 32 + 32)
                pe.wait_ge(h_ready, l * GROUPS + (c + 1))
                pe.wait_ge(xr_ready, l * 8 + 8)
                for m in range(CHUNKS):
                    i = CHUNKS * c + m
                    rows = P if m < CHUNKS - 1 else LAST
                    if i >= 2:
                        pe.wait_ge(hid_ready, l * FFN + (i - 1))
                    for k in range(2):
                        mm = pe.matmul(g.bank[2 * k + i % 2][0:rows, :], w_up[:, k * UNITS + m * P:k * UNITS + m * P + rows],
                                       g.xnT[:, tok(c)], start=True, stop=True)
                    mm.then_inc(up_ready, 1)

            def down(l, c):
                pe.wait_ge(hid_ready, l * FFN + CHUNKS * (c + 1))
                pe.wait_ge(xr_ready, l * 8 + (7 + c))
                for i in range(TPG):
                    for m in range(CHUNKS):
                        rows = P if m < CHUNKS - 1 else LAST + 1
                        mm = pe.matmul(g.bank[4 + c % 2][:, i * P:(i + 1) * P], hid[0:rows, c % 2, m, i * P:(i + 1) * P],
                                       w_down[0:rows, m, :], start=(m == 0), stop=(m == CHUNKS - 1))
                mm.then_inc(down_ready, 1)

            def finish(b, j):
                project_out(b + j, 1)
                weigh_values(b + j, j)

            for c in range(GROUPS):
                turn(c, c)
            with pe.Fori(0, LAYERS) as l:
                wait_apart(pe, xs_ready, l * 8 + 4, pe_passed)
                slots(pe, l, project, slot, finish)
                for k in range(STEPS_FFN):
                    if k and at(k, WO) is not None:
                        project_out(l * SLOTS + (SLOTS - 1), at(k, WO))
                    for stage, work in ((VAR, variance), (UP, up), (MEAN, mean)):
                        if at(k, stage) is not None:
                            work(l, at(k, stage))
                    if at(k, TURN) is not None:
                        pe.wait_ge(o_copied, l * SLOTS + (SLOTS + 1))
                        turn(l * 8 + (4 + at(k, TURN)), at(k, TURN))
                    if at(k, DOWN) is not None:
                        down(l, at(k, DOWN))
                    if at(k, NEXT_TURN) is not None:
                        turn(l * 8 + (8 + at(k, NEXT_TURN)), at(k, NEXT_TURN))
                pe.wait_ge(down_ready, l * GROUPS + GROUPS)
                pe.sem_inc(ffn_free, 1)

        @block.scalar
        def _(act):
            own = Chain(act, act_own)
            act.wait_ge(made, 1)
            for free, n in ((pair_free, 1), (ffn_free, 1), (norm_used, 2), (pt_copied, 2), (o_copied, 1)):
                act.sem_inc(free, n)

            def turn(n, c):
                act.wait_ge(turned, n + 1)
                bank = g.bank[6][:, :].rearrange("p (b t) -> p b t", t=T)
                act.activation(xs[0:64, seqs(c), W:], bank[0:64, :, :], ACT.Copy)
                act.activation(xs[64:P, seqs(c), W + 1:], bank[64:P, :, 0:T - 1], ACT.Copy).then_inc(xs_ready, 1)

            def copy_values(s, j):
                act.wait_ge(v_ready, s + 1)
                t = slice(TPG * (j % GROUPS), TPG * (j % GROUPS + 1))
                act.activation(v_at[:, t, :].rearrange("p n c -> p (n c)"), g.bank[5][:, :], ACT.Copy).then_inc(v_used, 1)

            def square(s, m):
                act.wait_ge(proj_ready, s * 4 + (m + 1))
                act.activation(sq[:, m, :], g.bank[m][:, :], ACT.Square).then_inc(sq_ready, 1)

            def invert_norms(s):
                for m in range(2):
                    act.wait_ge(norm_ready, s * 2 + (m + 1))
                    act.activation(lg[:, m, :], g.bank[4 * m][:, :], ACT.Ln, bias=guard[:, 0:1], scale=LN_SCALE).then_inc(norm_used, 1)
                    act.wait_ge(norm_used, s * 2 + (2 + m + 1))
                    act.activation(inv[:, m, :], lg[:, m, :], ACT.Exp, bias=unscale[:, 0:1], scale=-0.5).then_inc(inv_ready, 1)

            def project(b, j):
                square(b + j, 0)
                square(b + j, 1)
                invert_norms(b + j)
                copy_values(b + j, j)

            def copy_out(s, j, hp):
                wait_apart(act, o_ready, s + 1, act_passed)
                pair = attn[:, hp:hp + 1, tok(j)] if isinstance(hp, int) else attn[:, bass.ts(hp, 1), tok(j)]
                for x in range(SPG):
                    for hh in range(H):
                        ch = slice(E * hh, E * (hh + 1))
                        o = g.bank[6 + x][ch, :].rearrange("p (n r s h q) -> p n r s h q", n=2, r=2, s=2, h=H)
                        for n in range(2):
                            tokens = pair[ch, :, (2 * x + n) * P:(2 * x + n + 1) * P].rearrange("p a (s r q) -> p (a r) s q", s=2, r=2)
                            ins = act.activation(tokens, o[:, n, :, :, hh, :], ACT.Copy)
                ins.then_inc(o_copied, 1)

            def slot(b, j, project_next, hp):
                s = b + j
                if project_next:
                    square(s + 1, 0)
                act.wait_ge(z_ready, s + 1)
                act.activation(z[:, j % 2, :], z[:, j % 2, :], ACT.Exp).then_inc(e_ready, 1)
                if project_next:
                    square(s + 1, 1)
                    invert_norms(s + 1)
                    copy_values(s + 1, j + 1)
                act.wait_ge(pt_ready, s + 1)
                for half in range(2):
                    keys = slice(64 * half, 64 * half + 64)
                    ins = act.activation(pt[keys, :, :, half, :], g.bank[4][keys, :].rearrange("p (i r q) -> p i r q", i=TPG, r=2), ACT.Copy)
                ins.then_inc(pt_copied, 1)
                if hp is not None:
                    copy_out(b + (j - 1), j - 1, hp)

            def invert_deviation(l, c):
                own = Chain(act, act_own, (l * GROUPS + c) * 2)
                act.preload_act_table_set(LN_EXP)
                act.wait_ge(var_ready, l * GROUPS + (c + 1))
                own.step(act.activation(lg[:, c % 2, :], g.bank[7][:, :], ACT.Ln, bias=g.eps[:, 0:1]))
                own.step(act.activation(rstd[:, TPG * c:TPG * (c + 1), :].rearrange("p n c -> p (n c)"), lg[:, c % 2, :],
                                        ACT.Exp, scale=-0.5))
                act.sem_inc(rstd_ready, 1)

            def square_centred(l, c):
                act.wait_ge(xc_ready, l * GROUPS + (c + 1))
                act.activation(attn[:, 0, tok(c)], xc[:, tok(c)], ACT.Square).then_inc(xsq_ready, 1)

            def gelus(l, c):
                for m in range(CHUNKS):
                    i = CHUNKS * c + m
                    rows = P if m < CHUNKS - 1 else LAST
                    act.wait_ge(up_ready, l * FFN + (i + 1))
                    if i >= 2:
                        act.wait_ge(hid_ready, l * FFN + (i - 1))
                    act.activation(gelu[0:rows, i % 2, :], g.bank[2 + i % 2][0:rows, :], ACT.Gelu,
                                   bias=vecs[0:rows, 5 + m:6 + m]).then_inc(gelu_ready, 1)

            for c in range(GROUPS):
                turn(c, c)
            with act.Fori(0, LAYERS) as l:
                act.preload_act_table_set(LN_EXP)
                slots(act, l, project, slot, lambda b, j: copy_out(b + j, j, PAIRS - 1))
                act.wait_ge(vecs_loaded, l * 16 + 16)
                for k in range(STEPS_FFN):
                    for stage, work in ((VAR, invert_deviation), (UP, gelus), (MEAN, square_centred)):
                        if at(k, stage) is not None:
                            work(l, at(k, stage))
                    if at(k, TURN) is not None:
                        turn(l * 8 + (4 + at(k, TURN)), at(k, TURN))
                    if at(k, NEXT_TURN) is not None:
                        turn(l * 8 + (8 + at(k, NEXT_TURN)), at(k, NEXT_TURN))

        @block.vector
        def _(dve):
            dve.wait_ge(made, 1)
            for free, n in ((vecs_free, 1), (tabled, 1), (xr_ready, 4), (rotated, 4)):
                dve.sem_inc(free, n)
            STEPS = 3

            def times_table(s, k):
                dve.wait_ge(proj_ready, s * 4 + (k + 1))
                if k < 2:
                    dve.wait_ge(sq_ready, s * 2 + (k + 1))
                dve.tensor_tensor(term[:, k, :, :], g.bank[k][:, :].rearrange("p (b t) -> p b t", t=T),
                                  table[:, k, :].unsqueeze(1).to_broadcast([P, SPG, T]), ALU.mult).then_inc(rotated, 1)

            def over_norm(s, j):
                dve.wait_ge(inv_ready, s * 2 + 1)
                dve.wait_ge(summed, s * 2 + 1)
                for hh in range(H):
                    ch = slice(E * hh, E * (hh + 1))
                    dve.tensor_tensor(q_rot[ch, j % 2, :].rearrange("p (x h q) -> p x h q", h=H, q=W)[:, :, hh, :],
                                      term[ch, 0, :, :].rearrange("p b (w q) -> p (b w) q", q=W),
                                      inv[ch, 0, :].rearrange("p (x q) -> p x q", q=W), ALU.mult).then_inc(qk_ready, 1)
                dve.wait_ge(inv_ready, s * 2 + 2)
                dve.wait_ge(summed, s * 2 + 2)
                dve.tensor_tensor(k_rot[:, j % 2, :, W:], term[:, 1, :, :], inv[:, 1, :].rearrange("p (b t) -> p b t", t=T),
                                  ALU.mult).then_inc(qk_ready, 1)

            def project(b, j):
                for k in (0, 2, 1, 3):
                    times_table(b + j, k)
                over_norm(b + j, j)

            def slot(b, j, project_next, hp):
                s = b + j
                own = Chain(dve, dve_own, s * STEPS)
                rows = z[:, j % 2, :].rearrange("p (x k) -> p x k", k=2 * W)
                most_of, sums, over = most[:, j % 2, :], total[:, j % 2, 0, :], total[:, j % 2, 1, :]
                dve.wait_ge(s_ready, s + 1)
                own.step(dve.tensor_tensor(z[:, j % 2, :].rearrange("p (b k) -> p b k", b=SPG),
                                           g.bank[5][:, :].rearrange("p (b k) -> p b k", b=SPG),
                                           mask[:, :, :].rearrange("p x k -> p (x k)").unsqueeze(1).to_broadcast([P, SPG, GROUP // SPG]),
                                           ALU.add))
                own.step(dve.tensor_reduce(most_of, rows, AX.X, ALU.max))
                dve.tensor_tensor(rows, rows, spread(most_of, 2 * W), ALU.subtract).then_inc(z_ready, 1)
                if project_next:
                    times_table(s + 1, 0)
                dve.wait_ge(e_ready, s + 1)
                own.step(dve.tensor_reduce(sums, rows, AX.X, ALU.add))
                dve.reciprocal(over, sums).then_inc(total_ready, 1)
                if project_next:
                    for k in (2, 1, 3):
                        times_table(s + 1, k)
                    over_norm(s + 1, j + 1)
                assert own.count == STEPS, own.count

            def add_attention(l, c):
                dve.wait_ge(wo_ready, l * GROUPS + (c + 1))
                xr = g.xn[:, TPG * c:TPG * (c + 1), :]
                dve.tensor_tensor(xr, xr, g.bank[c][:, :].rearrange("p (n d) -> p n d", d=D), ALU.add).then_inc(xr_ready, 1)

            def centre(l, c):
                dve.wait_ge(mean_ready, l * GROUPS + (c + 1))
                dve.tensor_tensor(xc[:, tok(c)].rearrange("p (b t) -> p b t", t=T), xs[:, seqs(c), W:],
                                  g.bank[7][:, :].rearrange("p (b t) -> p b t", t=T), ALU.subtract).then_inc(xc_ready, 1)

            def layernorm(l, c):
                dve.wait_ge(rstd_ready, l * GROUPS + (c + 1))
                h = g.xnT[:, tok(c)]
                dve.tensor_tensor(h, xc[:, tok(c)], rstd[:, TPG * c:TPG * (c + 1), :].rearrange("p n c -> p (n c)"), ALU.mult).then_inc(normed, 1)
                dve.wait_ge(normed, l * GROUPS + (c + 1))
                dve.tensor_scalar(h, h, vecs[:, 0:1], vecs[:, 1:2], ALU.mult, ALU.add).then_inc(h_ready, 1)

            def gate(l, c):
                for m in range(CHUNKS):
                    i = CHUNKS * c + m
                    rows = P if m < CHUNKS - 1 else LAST
                    dve.wait_ge(gelu_ready, l * FFN + (i + 1))
                    if c >= 2 and m == 0:
                        dve.wait_ge(down_ready, l * GROUPS + (c - 1))
                    dve.scalar_tensor_tensor(out=hid[0:rows, c % 2, m, :], in0=g.bank[i % 2][0:rows, :],
                                             scalar=vecs[0:rows, 2 + m:3 + m], in1=gelu[0:rows, i % 2, :],
                                             op0=ALU.add, op1=ALU.mult).then_inc(hid_ready, 1)

            def add_down(l, c):
                dve.wait_ge(down_ready, l * GROUPS + (c + 1))
                xr = g.xn[:, TPG * c:TPG * (c + 1), :]
                dve.tensor_tensor(xr, xr, g.bank[4 + c % 2][:, :].rearrange("p (n d) -> p n d", d=D), ALU.add).then_inc(xr_ready, 1)

            with dve.Fori(0, LAYERS) as l:
                dve.wait_ge(scales_loaded, l * 16 + 16)
                for k in range(4):
                    ins = dve.tensor_scalar(table[:, k, :], base[:, k, :], scales[:, k:k + 1], None, ALU.mult)
                ins.then_inc(tabled, 1)
                dve.wait_ge(tabled, l + 2)
                slots(dve, l, project, slot, lambda b, j: None)
                add_attention(l, 0)
                dve.wait_ge(vecs_loaded, l * 16 + 16)
                for k in range(STEPS_FFN):
                    for stage, work in ((VAR, layernorm), (ADD, add_attention), (UP, gate), (MEAN, centre), (DOWN, add_down)):
                        if at(k, stage) is not None:
                            work(l, at(k, stage))
                dve.wait_ge(hid_ready, l * FFN + FFN)
                dve.sem_inc(vecs_free, 1)

    with ExitStack() as ctx:
        sem = ctx.enter_context(Signals(nc, "local_sum"))
        added = sem("added")
        block = ctx.enter_context(nc.Block())

        @block.vector
        def _(dve):
            dve.tensor_tensor(g.x[:, :, :], g.x[:, :, :], g.xn[:, :, :], ALU.add).then_inc(added, 1)
            dve.wait_ge(added, 1)


def store(nc, g, out_dram):
    with ExitStack() as ctx:
        stored = ctx.enter_context(nc.semaphore("stored"))
        block = ctx.enter_context(nc.Block())

        @block.sync
        def _(sp):
            sp.dma_start(out_dram.rearrange("(n p) d -> p n d", p=P), g.x[:, :, :]).then_inc(stored, 16)
            sp.wait_ge(stored, 16)


STAGES = (0, 1, 2, 3, 4, 5, 6, 7)


def build(nc, d_in, out_dram):
    g = Shared()
    with ExitStack() as ctx:
        def sb(n, shape):
            return ctx.enter_context(nc.sbuf_tensor(n, shape, F32))
        g.x, g.xn = sb("x", [P, TILES, D]), sb("xn", [P, TILES, D])
        g.xnT = sb("xnT", [P, N])
        g.ident, g.eps, g.one = sb("ident", [P, P]), sb("eps", [P, 1]), sb("one", [P, 1])
        g.bank = [ctx.enter_context(nc.psum_tensor(f"bank{i}", [P, 512], F32)) for i in range(8)]
        g.weights, g.weights_due = ctx.enter_context(nc.semaphore("weights")), 0
        g.gate_weights, g.gate_weights_due = ctx.enter_context(nc.semaphore("gate_weights")), 0
        set_up(nc, g, d_in["x"])
        if 0 in STAGES:
            mamba(nc, g, "mamba0", None, d_in["m0"])
        if 1 in STAGES:
            moe(nc, g, "moe0", d_in["f0"], 16, 9, lambda j: j if j < 8 else None, True, True, False)
        if 2 in STAGES:
            rotor_memory(nc, g, d_in["r1"])
        if 3 in STAGES:
            local_stack(nc, g, d_in["a1"])
        if 4 in STAGES:
            delta_rule(nc, g, d_in["g2"])
        if 5 in STAGES:
            moe(nc, g, "moe2", d_in["f2"], 8, 8, lambda j: j, True, False, False)
        if 6 in STAGES:
            mamba(nc, g, "mamba3", None, d_in["m3"])
        if 7 in STAGES:
            moe(nc, g, "moe3", d_in["f3"], 8, 32, lambda j: j // 4, False, False, True)
        store(nc, g, out_dram)


def lay_out(inputs):
    i = {k: np.asarray(v) for k, v in inputs.items()}

    def rows(a, n=P):
        return a.reshape(-1, n, *a.shape[1:]).swapaxes(0, 1)

    def everywhere(a):
        return np.broadcast_to(a[None], (P,) + a.shape)

    def mamba_side(p, names):
        w_x = i[p + names["w_x"]]
        out = {"w_in": i[p + "W_in"], "conv_w": rows(i[p + "conv_w"][:, 0, :]), "conv_b": rows(i[p + "conv_b"]),
               "w_bc": rows(w_x[:, -32:]), "b_dt": rows(i[p + "b_dt"]), "skip": rows(i[p + names["skip"]]),
               "w_out": rows(i[p + "W_out"])}
        a_log = i[p + "A_log"]
        out["a_log"] = rows(a_log) if a_log.ndim == 2 else np.broadcast_to(a_log, (P, 2, 16))
        if w_x.shape[1] == 33:
            out["w_dt"], out["w_dt_col"] = i[p + "W_dt"], rows(w_x[:, 0])
        else:
            out["w_dt"] = rows(i[p + "W_dt"])
        return out

    turned_half = np.concatenate([np.arange(32, 64), np.arange(32)])
    wq, wk, wv = (i["L1_ffn_Wqkv"][:, :, 1024 * n:1024 * (n + 1)].reshape(6, D, 8, 2, 64) for n in range(3))
    w_layer = np.stack([wq, wk, wq[..., turned_half], wk[..., turned_half], wv], 3).reshape(6, D, 8, 5 * P)
    scales = [np.concatenate([i[f"L1_ffn_{n}_scale"][:, order]] * 2, 1) for order in (np.arange(64), turned_half) for n in "qk"]
    b1 = np.zeros((6, 2, 3 * P), np.float32)
    b1[:, :, :341] = i["L1_ffn_b1"].reshape(6, 2, 341)
    w_down = np.zeros((6, 3 * P, D), np.float32)
    w_down[:, :341], w_down[:, 341] = i["L1_ffn_W2"], i["L1_ffn_b2"]
    return {
        "a1": {
            "base": rotary_tables(), "w_layer": w_layer,
            "scales": np.stack(scales, 2),
            "vecs": np.stack([i["L1_ffn_ln_g"], i["L1_ffn_ln_b"]] + [b1[:, k, P * m:P * (m + 1)] for k in range(2) for m in range(3)], 2),
            "w_o": i["L1_ffn_Wo"].reshape(6, 8, P, D).swapaxes(1, 2), "w_up": i["L1_ffn_W1"],
            "w_down": w_down.reshape(6, 3, P, D).swapaxes(1, 2),
        },
        "m0": mamba_side("L0_attn_", {"w_x": "W_xproj", "skip": "Dp"}),
        "m3": mamba_side("L3_attn_", {"w_x": "W_x", "skip": "D"}),
        "f0": {
            "gate_w": i["L0_ffn_gate_w"].T, "gate_b": everywhere(i["L0_ffn_expert_bias"]),
            "w1": np.concatenate([i["L0_ffn_w1"].reshape(-1, D), i["L0_ffn_sw1"]]).T.reshape(D, 9, P),
            "w3": np.concatenate([i["L0_ffn_w3"].reshape(-1, D), i["L0_ffn_sw3"]]).T.reshape(D, 9, P),
            "w2": rows(np.concatenate([i["L0_ffn_w2"].swapaxes(1, 2).reshape(-1, D), i["L0_ffn_sw2"].T])),
            "b1": rows(np.concatenate([i["L0_ffn_b1"].reshape(-1), i["L0_ffn_sb1"]])),
            "b3": rows(np.concatenate([i["L0_ffn_b3"].reshape(-1), i["L0_ffn_sb3"]])),
            "b2": np.concatenate([i["L0_ffn_b2"], i["L0_ffn_sb2"][None]]),
        },
        "f2": {
            "gate_w": i["L2_ffn_Wg"].T, "gate_b": everywhere(i["L2_ffn_bg"]),
            "w2": i["L2_ffn_We"].transpose(2, 0, 1), "b2": i["L2_ffn_be"],
        },
        "f3": {
            "gate_w": i["L3_ffn_gate_w"], "dom": i["L3_ffn_dom"].T,
            "w1": i["L3_ffn_W1"].transpose(1, 0, 2).reshape(D, 32, P),
            "w3": i["L3_ffn_W3"].transpose(1, 0, 2).reshape(D, 32, P),
            "w2": rows(i["L3_ffn_W2"].reshape(-1, D)),
        },
        "r1": {"w_v": i["L1_attn_Wv"].T, "w_o": i["L1_attn_Wo"].T, "freqs": i["L1_attn_freqs"][:, None]},
        "g2": {
            "w_ab": np.concatenate([i["L2_attn_a_w"], i["L2_attn_b_w"]]).T,
            "ab_bias": everywhere(np.concatenate([i["L2_attn_dt_bias"], np.zeros(8, np.float32)])),
            "a_log": everywhere(i["L2_attn_A_log"]), "norm_w": i["L2_attn_norm_w"][:, None],
            "w_qkv": i["L2_attn_qkv_w"].reshape(3, 8, P, D).transpose(3, 1, 0, 2),
            "taps": i["L2_attn_conv_w"].reshape(3, 8, P, 4).transpose(2, 1, 0, 3),
            "w_z": i["L2_attn_z_w"].reshape(8, P, D).transpose(2, 0, 1),
            "w_o": i["L2_attn_out_w"].reshape(D, 8, P).transpose(2, 1, 0),
        },
    }


def kernel(**inputs):
    import concourse.bacc as bacc
    from concourse.bass_utils import run_bass_kernel_spmd

    nc = bacc.Bacc("TRN2", target_bir_lowering=False, num_devices=1)
    arrays = {"x": np.ascontiguousarray(np.asarray(inputs["L0_attn_x"]).reshape(N, D))}
    d_in = {"x": nc.dram_tensor("x_dram", [N, D], F32, kind="ExternalInput").ap()}
    arrays = {"x_dram": arrays["x"]}
    for side, tensors in lay_out(inputs).items():
        d_in[side] = {}
        for name, a in tensors.items():
            a = np.ascontiguousarray(a)
            arrays[f"{side}_{name}_dram"] = a
            d_in[side][name] = nc.dram_tensor(f"{side}_{name}_dram", a.shape, F32, kind="ExternalInput").ap()
    out = nc.dram_tensor("out_dram", [N, D], F32, kind="ExternalOutput").ap()
    build(nc, d_in, out)
    r = run_bass_kernel_spmd(nc, [arrays], core_ids=[0])
    return r.results[0]["out_dram"].reshape(BATCH, T, D)
```
